# Optimizing a Trainium2 kernel written in Bass

```python
import numpy as np
import jax
import jax.numpy as jnp

def _softmax(x, axis=-1):
    return jax.nn.softmax(x, axis=axis)

def _gelu(x):
    return jax.nn.gelu(x, approximate=True)

def _silu(x):
    return jax.nn.silu(x)

def _sigmoid(x):
    return jax.nn.sigmoid(x)

def _layernorm(x, axis=-1, eps=1e-05):
    m = jnp.mean(x, axis=axis, keepdims=True)
    v = jnp.var(x, axis=axis, keepdims=True)
    return (x - m) / jnp.sqrt(v + eps)

def _scatter_add(tgt, idx, src, axis=0):
    return tgt.at[idx].add(src)

def _segment_sum(src, seg, n):
    return jax.ops.segment_sum(src, seg, n)
kernel_name = 'mk_gnn_ffn_d2_gnn_r8_9b8248'

def setup_inputs(seed: int=0):
    np.random.seed(seed)
    _w = jnp.asarray

    def _rec_inputs():
        import jax
        import jax.numpy as jnp
        _gk = jax.random.key(seed)
        x = -0.0003713 + 1 * jax.random.normal(jax.random.fold_in(_gk, 1), (6250, 256), jnp.float32)
        src = jax.random.randint(jax.random.fold_in(_gk, 2), (100000,), 0, 6250, jnp.int32)
        dst = jnp.minimum((6250 * jax.random.uniform(jax.random.fold_in(_gk, 3), (100000,)) ** 2.0).astype(jnp.int32), 49999)
        _o = jnp.argsort(dst, stable=True)
        src = src[_o]
        dst = dst[_o]
        edge_attr_128 = -5.16925e-05 + 1.00005 * jax.random.normal(jax.random.fold_in(_gk, 11), (100000, 128), jnp.float32)
        return (x, src, dst, edge_attr_128)
    x, src, dst, edge_attr_128 = _rec_inputs()

    def _L0_gnn_setup():
        import jax, jax.numpy as jnp
        import numpy as np
        N_NODES = 6250
        N_EDGES = 200000
        H_SIZE = 256
        HEADS = 8
        HEAD_DIM = H_SIZE // HEADS
        NEG_SLOPE = 0.2
        key = jax.random.key(seed)
        k_x, k_e, k_w, k_as, k_ad, k_b = jax.random.split(key, 6)
        x = jax.random.normal(k_x, (N_NODES, H_SIZE), dtype=jnp.float32)
        edge_index = jax.random.randint(k_e, (2, N_EDGES), 0, N_NODES, dtype=jnp.int64)
        scale = 1.0 / np.sqrt(H_SIZE)
        W = jax.random.normal(k_w, (H_SIZE, HEADS, HEAD_DIM), dtype=jnp.float32) * scale
        att_src = jax.random.normal(k_as, (HEADS, HEAD_DIM), dtype=jnp.float32) * scale
        att_dst = jax.random.normal(k_ad, (HEADS, HEAD_DIM), dtype=jnp.float32) * scale
        bias = jnp.zeros((H_SIZE,), dtype=jnp.float32)
        return {'x': x, 'edge_index': edge_index, 'W': W, 'att_src': att_src, 'att_dst': att_dst, 'bias': bias}
    _L0_gnn_all = _L0_gnn_setup()
    _L0_gnn_in = {k: v for k, v in _L0_gnn_all.items() if k in ('W', 'att_src', 'att_dst', 'bias')}
    del _L0_gnn_all

    def _L0_ffn_setup():
        import jax, jax.numpy as jnp
        import numpy as np
        E = 8
        K = 2
        D = 256
        H = 512
        DOUT = 256
        EPS = 1e-05
        key = jax.random.key(seed)
        ks = jax.random.split(key, 9)
        s = 0.02
        return {'x': jax.random.normal(ks[0], (4, 1024, D), jnp.float32), 'gamma': 1.0 + 0.05 * jax.random.normal(ks[1], (D,), jnp.float32), 'beta': 0.05 * jax.random.normal(ks[2], (D,), jnp.float32), 'Wr': 0.01 * jax.random.normal(ks[3], (D, E), jnp.float32), 'br': jnp.zeros((E,), jnp.float32), 'W1': s * jax.random.normal(ks[4], (E, D, H), jnp.float32), 'b1': s * jax.random.normal(ks[5], (E, H), jnp.float32), 'W2': s * jax.random.normal(ks[6], (E, H, DOUT), jnp.float32), 'b2': s * jax.random.normal(ks[7], (E, DOUT), jnp.float32)}
    _L0_ffn_all = _L0_ffn_setup()
    _L0_ffn_in = {k: v for k, v in _L0_ffn_all.items() if k in ('gamma', 'beta', 'Wr', 'br', 'W1', 'b1', 'W2', 'b2')}
    del _L0_ffn_all

    def _L1_gnn_setup():
        import jax, jax.numpy as jnp
        import numpy as np
        N_NODES = 6250
        N_EDGES = 100000
        IN_DIM = 256
        OUT_DIM = 256
        EDGE_DIM = 128
        BN_EPS = 1e-05
        key = jax.random.key(seed)
        ks = jax.random.split(key, 10)
        s = lambda d: 1.0 / np.sqrt(d)
        return {'x': jax.random.normal(ks[0], (N_NODES, IN_DIM), dtype=jnp.float32), 'edge_index': jax.random.randint(ks[1], (2, N_EDGES), 0, N_NODES, dtype=jnp.int64), 'edge_attr': jax.random.normal(ks[2], (N_EDGES, EDGE_DIM), dtype=jnp.float32), 'W_edge': jax.random.uniform(ks[3], (EDGE_DIM, IN_DIM), jnp.float32, -s(EDGE_DIM), s(EDGE_DIM)), 'b_edge': jnp.zeros((IN_DIM,), jnp.float32), 'W1': jax.random.uniform(ks[4], (IN_DIM, OUT_DIM), jnp.float32, -s(IN_DIM), s(IN_DIM)), 'b1': jnp.zeros((OUT_DIM,), jnp.float32), 'W2': jax.random.uniform(ks[5], (OUT_DIM, OUT_DIM), jnp.float32, -s(OUT_DIM), s(OUT_DIM)), 'b2': jnp.zeros((OUT_DIM,), jnp.float32), 'eps': jnp.float32(0.0), 'gamma': jnp.ones((OUT_DIM,), jnp.float32), 'beta': jnp.zeros((OUT_DIM,), jnp.float32)}
    _L1_gnn_all = _L1_gnn_setup()
    _L1_gnn_in = {k: v for k, v in _L1_gnn_all.items() if k in ('W_edge', 'b_edge', 'W1', 'b1', 'W2', 'b2', 'eps', 'gamma', 'beta')}
    del _L1_gnn_all

    def _L1_ffn_setup():
        import jax, jax.numpy as jnp
        import numpy as np
        E, D, H, TOP_K = (6, 256, 256, 2)
        ROUTER_H = D // 2
        key = jax.random.key(seed)
        ks = jax.random.split(key, 12)
        s = 1.0 / np.sqrt(D)
        sh = 1.0 / np.sqrt(H)
        sr = 1.0 / np.sqrt(ROUTER_H)
        return {'features': jax.random.normal(ks[0], (8, 512, D), dtype=jnp.float32), 'router_w1': jax.random.uniform(ks[1], (D, ROUTER_H), jnp.float32, -s, s), 'router_b1': jnp.zeros((ROUTER_H,), jnp.float32), 'router_w2': jax.random.uniform(ks[2], (ROUTER_H, E), jnp.float32, -sr, sr), 'router_b2': jnp.zeros((E,), jnp.float32), 'expert_w1': jax.random.uniform(ks[3], (E, D, H), jnp.float32, -s, s), 'expert_b1': jnp.zeros((E, H), jnp.float32), 'expert_w2': jax.random.uniform(ks[4], (E, H, H), jnp.float32, -sh, sh), 'expert_b2': jnp.zeros((E, H), jnp.float32), 'expert_w3': jax.random.uniform(ks[5], (E, H, D), jnp.float32, -sh, sh), 'expert_b3': jnp.zeros((E, D), jnp.float32)}
    _L1_ffn_all = _L1_ffn_setup()
    _L1_ffn_in = {k: v for k, v in _L1_ffn_all.items() if k in ('router_w1', 'router_b1', 'router_w2', 'router_b2', 'expert_w1', 'expert_b1', 'expert_w2', 'expert_b2', 'expert_w3', 'expert_b3')}
    del _L1_ffn_all
    return {'x': x, 'src': src, 'dst': dst, 'edge_attr_128': edge_attr_128, 'L0_gnn_W': _L0_gnn_in['W'], 'L0_gnn_att_src': _L0_gnn_in['att_src'], 'L0_gnn_att_dst': _L0_gnn_in['att_dst'], 'L0_gnn_bias': _L0_gnn_in['bias'], 'L0_ffn_gamma': _L0_ffn_in['gamma'], 'L0_ffn_beta': _L0_ffn_in['beta'], 'L0_ffn_Wr': _L0_ffn_in['Wr'], 'L0_ffn_br': _L0_ffn_in['br'], 'L0_ffn_W1': _L0_ffn_in['W1'], 'L0_ffn_b1': _L0_ffn_in['b1'], 'L0_ffn_W2': _L0_ffn_in['W2'], 'L0_ffn_b2': _L0_ffn_in['b2'], 'L1_gnn_W_edge': _L1_gnn_in['W_edge'], 'L1_gnn_b_edge': _L1_gnn_in['b_edge'], 'L1_gnn_W1': _L1_gnn_in['W1'], 'L1_gnn_b1': _L1_gnn_in['b1'], 'L1_gnn_W2': _L1_gnn_in['W2'], 'L1_gnn_b2': _L1_gnn_in['b2'], 'L1_gnn_eps': _L1_gnn_in['eps'], 'L1_gnn_gamma': _L1_gnn_in['gamma'], 'L1_gnn_beta': _L1_gnn_in['beta'], 'L1_ffn_router_w1': _L1_ffn_in['router_w1'], 'L1_ffn_router_b1': _L1_ffn_in['router_b1'], 'L1_ffn_router_w2': _L1_ffn_in['router_w2'], 'L1_ffn_router_b2': _L1_ffn_in['router_b2'], 'L1_ffn_expert_w1': _L1_ffn_in['expert_w1'], 'L1_ffn_expert_b1': _L1_ffn_in['expert_b1'], 'L1_ffn_expert_w2': _L1_ffn_in['expert_w2'], 'L1_ffn_expert_b2': _L1_ffn_in['expert_b2'], 'L1_ffn_expert_w3': _L1_ffn_in['expert_w3'], 'L1_ffn_expert_b3': _L1_ffn_in['expert_b3']}

def reference(x, src, dst, edge_attr_128, L0_gnn_W, L0_gnn_att_src, L0_gnn_att_dst, L0_gnn_bias, L0_ffn_gamma, L0_ffn_beta, L0_ffn_Wr, L0_ffn_br, L0_ffn_W1, L0_ffn_b1, L0_ffn_W2, L0_ffn_b2, L1_gnn_W_edge, L1_gnn_b_edge, L1_gnn_W1, L1_gnn_b1, L1_gnn_W2, L1_gnn_b2, L1_gnn_eps, L1_gnn_gamma, L1_gnn_beta, L1_ffn_router_w1, L1_ffn_router_b1, L1_ffn_router_w2, L1_ffn_router_b2, L1_ffn_expert_w1, L1_ffn_expert_b1, L1_ffn_expert_w2, L1_ffn_expert_b2, L1_ffn_expert_w3, L1_ffn_expert_b3):
    import jax
    import jax.numpy as jnp

    def _L0_gnn_ref(x, edge_index, W, att_src, att_dst, bias):
        import jax, jax.numpy as jnp
        import numpy as np
        N_NODES = 6250
        N_EDGES = 200000
        H_SIZE = 256
        HEADS = 8
        HEAD_DIM = H_SIZE // HEADS
        NEG_SLOPE = 0.2
        'GATConv (concat heads) -> relu -> dropout(eval=identity).\n\n            x: [N, F]; edge_index: [2, E] with (src=row0, dst=row1) meaning message j->i.\n            '
        N = x.shape[0]
        h = jnp.einsum('nf,fhd->nhd', x, W)
        a_src = jnp.sum(h * att_src, axis=-1)
        a_dst = jnp.sum(h * att_dst, axis=-1)
        src = edge_index[0]
        dst = edge_index[1]
        e = jax.nn.leaky_relu(a_src[src] + a_dst[dst], NEG_SLOPE)
        e_max = jax.ops.segment_max(e, dst, num_segments=N)
        e_exp = jnp.exp(e - e_max[dst])
        denom = jax.ops.segment_sum(e_exp, dst, num_segments=N)
        alpha = e_exp / (denom[dst] + 1e-16)
        msg = h[src] * alpha[:, :, None]
        out = jax.ops.segment_sum(msg, dst, num_segments=N)
        out = out.reshape(N, -1) + bias
        return jax.nn.relu(out)

    def _L0_ffn_ref(x, gamma, beta, Wr, br, W1, b1, W2, b2):
        import jax, jax.numpy as jnp
        import numpy as np
        E = 8
        K = 2
        D = 256
        H = 512
        DOUT = 256
        EPS = 1e-05
        mu = jnp.mean(x, axis=-1, keepdims=True)
        var = jnp.mean(jnp.square(x - mu), axis=-1, keepdims=True)
        xn = (x - mu) * jax.lax.rsqrt(var + EPS) * gamma + beta
        logits = jnp.einsum('bsd,de->bse', xn, Wr) + br
        top_vals, top_idx = jax.lax.top_k(logits, K)
        w = jax.nn.softmax(top_vals, axis=-1)
        w_full = jnp.einsum('bsk,bske->bse', w, jax.nn.one_hot(top_idx, E, dtype=w.dtype))
        y = jnp.zeros(x.shape[:-1] + (DOUT,), x.dtype)
        for e in range(E):
            h = jax.nn.gelu(jnp.einsum('bsd,dh->bsh', xn, W1[e]) + b1[e], approximate=False)
            y_e = jnp.einsum('bsh,hd->bsd', h, W2[e]) + b2[e]
            y = y + y_e * w_full[..., e, None]
        return y

    def _L1_gnn_ref(x, edge_index, edge_attr, W_edge, b_edge, W1, b1, W2, b2, eps, gamma, beta):
        import jax, jax.numpy as jnp
        import numpy as np
        N_NODES = 6250
        N_EDGES = 100000
        IN_DIM = 256
        OUT_DIM = 256
        EDGE_DIM = 128
        BN_EPS = 1e-05
        src, dst = (edge_index[0], edge_index[1])
        e = edge_attr @ W_edge + b_edge
        msg = jax.nn.relu(x[src] + e)
        agg = jax.ops.segment_sum(msg, dst, num_segments=x.shape[0])
        h = (1.0 + eps) * x + agg
        h = jax.nn.relu(h @ W1 + b1) @ W2 + b2
        mean = jnp.mean(h, axis=0)
        var = jnp.var(h, axis=0)
        h = (h - mean) * jax.lax.rsqrt(var + BN_EPS) * gamma + beta
        return jax.nn.relu(h)

    def _L1_ffn_ref(features, router_w1, router_b1, router_w2, router_b2, expert_w1, expert_b1, expert_w2, expert_b2, expert_w3, expert_b3):
        import jax, jax.numpy as jnp
        import numpy as np
        E, D, H, TOP_K = (6, 256, 256, 2)
        ROUTER_H = D // 2
        rh = jax.nn.relu(features @ router_w1 + router_b1)
        expert_logits = jax.nn.softmax(rh @ router_w2 + router_b2, axis=-1)
        top_w, top_i = jax.lax.top_k(expert_logits, TOP_K)
        routing_weights = jax.nn.softmax(top_w, axis=-1)
        h1 = jax.nn.relu(jnp.einsum('bsd,edh->bseh', features, expert_w1) + expert_b1)
        h2 = jax.nn.relu(jnp.einsum('bseh,ehf->bsef', h1, expert_w2) + expert_b2)
        expert_out = jnp.einsum('bsef,efo->bseo', h2, expert_w3) + expert_b3
        sel = jnp.take_along_axis(expert_out, top_i[:, :, :, None], axis=2)
        combined = jnp.sum(sel * routing_weights[..., None], axis=2)
        return combined
    edge_index = jnp.stack([src, dst])
    x = x + _L0_gnn_ref(_layernorm(x, axis=-1), edge_index, L0_gnn_W, L0_gnn_att_src, L0_gnn_att_dst, L0_gnn_bias)
    x = x + _L0_ffn_ref(_layernorm(x, axis=-1)[None], L0_ffn_gamma, L0_ffn_beta, L0_ffn_Wr, L0_ffn_br, L0_ffn_W1, L0_ffn_b1, L0_ffn_W2, L0_ffn_b2)[0]
    x = x + _L1_gnn_ref(_layernorm(x, axis=-1), edge_index, edge_attr_128, L1_gnn_W_edge, L1_gnn_b_edge, L1_gnn_W1, L1_gnn_b1, L1_gnn_W2, L1_gnn_b2, L1_gnn_eps, L1_gnn_gamma, L1_gnn_beta)
    x = x + _L1_ffn_ref(_layernorm(x, axis=-1)[None], L1_ffn_router_w1, L1_ffn_router_b1, L1_ffn_router_w2, L1_ffn_router_b2, L1_ffn_expert_w1, L1_ffn_expert_b1, L1_ffn_expert_w2, L1_ffn_expert_b2, L1_ffn_expert_w3, L1_ffn_expert_b3)[0]
    return x

_drawn_inputs = setup_inputs


def setup_inputs(seed=0):
    import zlib

    import numpy as np

    out = dict(_drawn_inputs(seed))
    spreads = {'L0_gnn_bias': (0.0, 0.1),
     'L0_ffn_br': (0.0, 0.1),
     'L1_gnn_b_edge': (0.0, 0.1),
     'L1_gnn_b1': (0.0, 0.691),
     'L1_gnn_b2': (0.0, 0.8),
     'L1_gnn_gamma': (1.0, 0.2),
     'L1_gnn_beta': (0.0, 0.1),
     'L1_ffn_router_b1': (0.0, 0.1),
     'L1_ffn_router_b2': (0.0, 0.1),
     'L1_ffn_expert_b1': (0.0, 0.8),
     'L1_ffn_expert_b2': (0.0, 0.377),
     'L1_ffn_expert_b3': (0.0, 0.1)}
    factors = {'L0_gnn_att_dst': 2.929,
     'L0_ffn_gamma': 5.658,
     'L0_ffn_beta': 4.869,
     'L0_ffn_b1': 8.0,
     'L0_ffn_b2': 3.366}
    for name, (base, spread) in spreads.items():
        noise = np.random.default_rng([zlib.crc32(name.encode()), seed]).standard_normal(out[name].shape)
        drawn = base * np.exp(spread * noise) if base else spread * noise
        out[name] = jnp.asarray(drawn.astype(out[name].dtype))
    for name, factor in factors.items():
        out[name] = (out[name] * factor).astype(out[name].dtype)
    return out
```

```python
import concourse.bass as bass
from concourse import mybir
from contextlib import ExitStack

fp32 = mybir.dt.float32
i32 = mybir.dt.int32
u32 = mybir.dt.uint32
ALU = mybir.AluOpType
ACT = mybir.ActivationFunctionType
AX = mybir.AxisListType

P = 128
N = 6250
D = 256
KD = D // P
E = 100000
HEADS = 8
HD = D // HEADS
NEG_SLOPE = 0.2
ED = 128
EPS = 1e-5
BIG = 1e30

NT = -(-N // P)
FULL_T = N // P
TAIL = N - FULL_T * P

CB = 4
EB = CB * P
NB = -(-E // EB)
NCH = NB * CB
LAST_E = E - (NB - 1) * EB
CQ = -(-NCH // P)
LAST_ROWS = NCH - (CQ - 1) * P
COUNT_AT, BEFORE_AT = 6, 12
FIELD, BEFORE_FIELD = 63, (1 << 14) - 1
SB = 16
SG = NCH // SB
BQ = P // CB

GT = 4
NG = NT // GT
GN = GT * P

MSG = D + HEADS


class Mem:
    pass


def bcast_free(ap, shape):
    return ap.to_broadcast(shape)


def pairs_loop(eng, mem, body):
    at = slice(body, body + 1) if isinstance(body, int) else bass.ds(body, 1)
    word = eng.value_load(mem.ranges[0:1, at])
    first = eng.snap((word & FIELD).with_bounds(min_val=0, max_val=NT - 1))
    count = eng.snap(((word >> COUNT_AT) & FIELD).with_bounds(min_val=1, max_val=NT))
    before = eng.snap(((word >> BEFORE_AT) & BEFORE_FIELD).with_bounds(min_val=0, max_val=NB * NT))
    return first, count, before


def phase_load(nc, mem, a):
    with ExitStack() as ctx:
        sem = lambda n: ctx.enter_context(nc.semaphore(n))
        zeroed, made, loaded = sem("ld_zeroed"), sem("ld_made"), sem("ld_loaded")
        block = ctx.enter_context(nc.Block())

        @block.gpsimd
        def _(pool):
            pool.memset(mem.ident[:, :], 1.0).then_inc(made, 1)
            pool.wait_ge(made, 1)
            pool.affine_select(out=mem.ident[:, :], in_=mem.ident[:, :], compare_op=ALU.is_equal, fill=0.0,
                               base=0, pattern=[[-1, P]], channel_multiplier=1).then_inc(made, 1)
            pool.iota(mem.iota_row[:, :], pattern=[[1, P]], base=0, channel_multiplier=0,
                      allow_small_or_imprecise_dtypes=True).then_inc(made, 1)
            pool.iota(mem.node_id[:, :], pattern=[[P, NT]], base=0, channel_multiplier=1,
                      allow_small_or_imprecise_dtypes=True).then_inc(made, 1)
            pool.iota(mem.neg_base[:, :], pattern=[[-P, NT]], base=0, channel_multiplier=0,
                      allow_small_or_imprecise_dtypes=True).then_inc(made, 1)
            pool.wait_ge(made, 5)

        @block.vector
        def _(dve):
            nc.vector.memset(mem.ones[:, :], 1.0).then_inc(zeroed, 1)
            nc.vector.memset(mem.zeros[:, :], 0.0).then_inc(zeroed, 1)
            nc.vector.memset(mem.X[:, FULL_T, :], 0.0).then_inc(zeroed, 1)
            dve.wait_ge(zeroed, 3)

        @block.sync
        def _(sp):
            sp.dma_start(mem.X[:, 0:FULL_T, :],
                         a["x"][0:FULL_T * P, :].rearrange("(t p) f -> p t f", p=P)).then_inc(loaded, 16)
            sp.wait_ge(zeroed, 3)
            sp.dma_start(mem.X[0:TAIL, FULL_T, :], a["x"][FULL_T * P:N, :]).then_inc(loaded, 16)
            sp.wait_ge(loaded, 32)


def phase_edges(nc, mem, a):
    with ExitStack() as ctx:
        sb = lambda n, s, d=fp32: ctx.enter_context(nc.sbuf_tensor(n, s, d))
        sem = lambda n: ctx.enter_context(nc.semaphore(n))
        raw_src = sb("raw_src", [P, CQ, P], i32)
        raw_dst = sb("raw_dst", [P, CQ, P], i32)
        srcf = sb("srcf", [P, CQ, P])
        dstf = sb("dstf", [P, CQ, P])
        differs = sb("differs", [P, CQ, P + 1])
        real_min = sb("real_min", [P, CQ, P])
        last = sb("last", [P, CQ, P])
        reset = sb("reset", [P, CQ, P])
        row_min = sb("row_min", [P, CQ])
        row_max = sb("row_max", [P, CQ])
        mm = sb("mm", [CQ, 2, BQ])
        mm_i = sb("mm_i", [CQ, 2, BQ], i32)
        mm_t = sb("mm_t", [CQ, 2, BQ], i32)
        flat = sb("flat", [1, 2, mem.NBP], i32)
        flat_f = sb("flat_f", [1, 2, mem.NBP])
        counts = sb("counts", [1, mem.NBP])
        so_far = sb("so_far", [1, mem.NBP])
        packs = sb("packs", [1, 3, mem.NBP], i32)
        ps = ctx.enter_context(nc.psum_tensor("e_ps", [P, 2, 512], fp32))
        ps_m = ctx.enter_context(nc.psum_tensor("e_psm", [P, 2, P], fp32))
        filled, loaded, masked = sem("ed_filled"), sem("ed_loaded"), sem("ed_masked")
        step, tr, ev = sem("ed_step"), sem("ed_tr"), sem("ed_ev")
        stored, back = sem("ed_stored"), sem("ed_back")
        block = ctx.enter_context(nc.Block())

        @block.sync
        def _(sp):
            sp.wait_ge(filled, 2)
            whole = (CQ - 1) * P * P
            rows = (E - whole) // P
            for raw, e in ((raw_src, a["src"]), (raw_dst, a["dst"])):
                sp.dma_start(raw[:, 0:CQ - 1, :],
                             e[0:whole].rearrange("(q p e) -> p q e", p=P, e=P)).then_inc(loaded, 16)
                sp.dma_start(raw[0:rows, CQ - 1, :],
                             e[whole:whole + rows * P].rearrange("(p e) -> p e", e=P)).then_inc(loaded, 16)
                sp.dma_start(raw[rows:rows + 1, CQ - 1, 0:E % P],
                             e[whole + rows * P:E].unsqueeze(0)).then_inc(loaded, 16)
            sp.wait_ge(step, 8)
            for sbt, dr in ((dstf, mem.dst_flat), (reset, mem.reset_flat)):
                sp.dma_start(dr[0:whole].rearrange("(q p e) -> p q e", p=P, e=P),
                             sbt[:, 0:CQ - 1, :]).then_inc(stored, 16)
                sp.dma_start(dr[whole:NCH * P].rearrange("(p e) -> p e", e=P),
                             sbt[0:LAST_ROWS, CQ - 1, :]).then_inc(stored, 16)
            sp.wait_ge(step, 11)
            for w in range(2):
                sp.dma_start(mem.range_flat[w, :].rearrange("(q b) -> q b", b=BQ), mm_t[:, w, :]).then_inc(back, 16)
            sp.wait_ge(back, 32)
            sp.dma_start(flat[:, :, :], mem.range_flat[:, :].unsqueeze(0)).then_inc(back, 16)
            sp.wait_ge(stored, 64)

        @block.vector
        def _(dve):
            nc.vector.memset(raw_src[:, :, :], 0).then_inc(filled, 1)
            nc.vector.memset(raw_dst[:, :, :], -1).then_inc(filled, 1)
            nc.vector.memset(differs[:, :, 0:1], 1.0)
            nc.vector.memset(differs[:, :, P:P + 1], 1.0)
            dve.wait_ge(loaded, 96)
            nc.vector.tensor_copy(srcf[:, :, :], raw_src[:, :, :]).then_inc(step, 1)
            nc.vector.tensor_copy(dstf[:, :, :], raw_dst[:, :, :]).then_inc(step, 1)
            dve.wait_ge(step, 2)
            nc.vector.tensor_scalar(real_min[:, :, :], dstf[:, :, :], 0.0, float(NT * P), ALU.is_lt, ALU.mult).then_inc(step, 1)
            nc.vector.tensor_reduce(row_max[:, :], dstf[:, :, :], AX.X, ALU.max).then_inc(step, 1)
            dve.wait_ge(step, 4)
            nc.vector.tensor_tensor(real_min[:, :, :], real_min[:, :, :], dstf[:, :, :], ALU.add).then_inc(step, 1)
            dve.wait_ge(step, 5)
            nc.vector.tensor_reduce(row_min[:, :], real_min[:, :, :], AX.X, ALU.min).then_inc(masked, 1)
            nc.vector.tensor_tensor(differs[:, :, 1:P], dstf[:, :, 1:P], dstf[:, :, 0:P - 1],
                                    ALU.not_equal).then_inc(step, 1)
            dve.wait_ge(step, 6)
            nc.vector.scalar_tensor_tensor(last[:, :, :], dstf[:, :, :], 1.0, differs[:, :, 1:P + 1],
                                           op0=ALU.add, op1=ALU.mult).then_inc(step, 1)
            nc.vector.tensor_scalar(reset[:, :, :], differs[:, :, 0:P], -BIG, None, ALU.mult).then_inc(step, 1)
            dve.wait_ge(step, 8)
            nc.vector.tensor_scalar(last[:, :, :], last[:, :, :], -1.0, None, ALU.add).then_inc(step, 1)
            dve.wait_ge(tr, 1)
            for w, op in ((0, ALU.min), (1, ALU.max)):
                ins = nc.vector.tensor_reduce(mm[:, w, :], ps_m[0:CQ, w, :].rearrange("q (b c) -> q b c", c=CB), AX.X, op)
            ins.then_inc(ev, 1)
            dve.wait_ge(ev, 1)
            nc.vector.tensor_copy(mm_i[:, :, :], mm[:, :, :]).then_inc(step, 1)
            dve.wait_ge(step, 10)
            nc.vector.tensor_scalar(mm_t[:, :, :], mm_i[:, :, :], 7, None, ALU.arith_shift_right).then_inc(step, 1)
            n_tr = 1
            for src, dst in ((srcf, mem.src_idx), (dstf, mem.dst_e), (last, mem.last_e)):
                for q in range(CQ):
                    w = P if q < CQ - 1 else LAST_ROWS
                    n_tr += 1
                    dve.wait_ge(tr, n_tr)
                    nc.vector.tensor_copy(dst[:, q * P:q * P + w], ps[:, n_tr % 2, 0:w]).then_inc(ev, 1)
            dve.wait_ge(back, 48)
            nc.vector.tensor_copy(flat_f[:, :, :], flat[:, :, :]).then_inc(step, 1)
            dve.wait_ge(step, 12)
            nc.vector.tensor_tensor(counts[:, :], flat_f[:, 1, :], flat_f[:, 0, :], ALU.subtract).then_inc(step, 1)
            dve.wait_ge(step, 13)
            nc.vector.tensor_scalar(counts[:, :], counts[:, :], 1.0, None, ALU.add).then_inc(step, 1)
            dve.wait_ge(step, 14)
            nc.vector.tensor_tensor_scan(so_far[:, :], counts[:, :], counts[:, :], 0.0, ALU.add, ALU.bypass).then_inc(step, 1)
            dve.wait_ge(step, 15)
            nc.vector.tensor_copy(packs[:, 1, :], counts[:, :]).then_inc(step, 1)
            nc.vector.tensor_tensor(packs[:, 2, :], so_far[:, :], counts[:, :], ALU.subtract).then_inc(step, 1)
            dve.wait_ge(step, 17)
            nc.vector.tensor_scalar(packs[:, 1, :], packs[:, 1, :], COUNT_AT, None, ALU.arith_shift_left).then_inc(step, 1)
            nc.vector.tensor_scalar(packs[:, 2, :], packs[:, 2, :], BEFORE_AT, None, ALU.arith_shift_left).then_inc(step, 1)
            dve.wait_ge(step, 19)
            nc.vector.tensor_tensor(packs[:, 0, :], packs[:, 1, :], packs[:, 2, :], ALU.bitwise_or).then_inc(step, 1)
            dve.wait_ge(step, 20)
            nc.vector.tensor_tensor(mem.ranges[:, :], packs[:, 0, :], flat[:, 0, :], ALU.bitwise_or).then_inc(step, 1)
            dve.wait_ge(step, 21)

        @block.tensor
        def _(pe):
            pe.wait_ge(masked, 1)
            nc.tensor.transpose(ps_m[0:CQ, 0, :], row_min[:, :], mem.ident[:, :])
            nc.tensor.transpose(ps_m[0:CQ, 1, :], row_max[:, :], mem.ident[:, :]).then_inc(tr, 1)
            pe.wait_ge(step, 9)
            n_tr = 1
            for src in (srcf, dstf, last):
                for q in range(CQ):
                    n_tr += 1
                    if n_tr >= 4:
                        pe.wait_ge(ev, n_tr - 2)
                    nc.tensor.transpose(ps[:, n_tr % 2, 0:P], src[:, q, :], mem.ident[:, :]).then_inc(tr, 1)


def layernorm_stats(nc, mem, name, src, first=None):
    with ExitStack() as ctx:
        sb = lambda n, s: ctx.enter_context(nc.sbuf_tensor(f"{name}_{n}", s, fp32))
        sem = lambda n: ctx.enter_context(nc.semaphore(f"{name}_{n}"))
        stats = sb("stats", [P, NT, 6])
        total, diff, m2, var = sb("total", [P, NT]), sb("diff", [P, NT]), sb("m2", [P, NT]), sb("var", [P, NT])
        std = sb("std", [P, NT])
        seen, step, rooted = sem("seen"), sem("step"), sem("rooted")
        block = ctx.enter_context(nc.Block())
        UN = 7

        @block.vector
        def _(dve):
            with dve.Fori(0, NT // UN) as i:
                for j in range(UN):
                    nc.vector.bn_stats(stats[:, bass.ds(i * UN + j, 1), :].rearrange("p a s -> p (a s)"),
                                       src[:, bass.ds(i * UN + j, 1), 0:D].rearrange("p a f -> p (a f)")).then_inc(seen, 1)
            dve.wait_ge(seen, NT)
            nc.vector.tensor_tensor(total[:, :], stats[:, :, 1], stats[:, :, 4], ALU.add).then_inc(step, 1)
            nc.vector.tensor_tensor(diff[:, :], stats[:, :, 1], stats[:, :, 4], ALU.subtract).then_inc(step, 1)
            nc.vector.tensor_tensor(m2[:, :], stats[:, :, 2], stats[:, :, 5], ALU.add).then_inc(step, 1)
            dve.wait_ge(step, 3)
            nc.vector.tensor_scalar(mem.mean[:, :], total[:, :], 0.5, None, ALU.mult).then_inc(step, 1)
            nc.vector.scalar_tensor_tensor(diff[:, :], diff[:, :], 0.25, diff[:, :],
                                           op0=ALU.mult, op1=ALU.mult).then_inc(step, 1)
            dve.wait_ge(step, 5)
            nc.vector.scalar_tensor_tensor(var[:, :], m2[:, :], 1.0 / D, diff[:, :],
                                           op0=ALU.mult, op1=ALU.add).then_inc(step, 1)
            dve.wait_ge(step, 6)
            nc.vector.tensor_scalar(var[:, :], var[:, :], EPS, None, ALU.add).then_inc(step, 1)
            dve.wait_ge(rooted, 1)
            nc.vector.reciprocal(mem.rstd[:, :], std[:, :]).then_inc(step, 1)
            dve.wait_ge(step, 8)

        @block.scalar
        def _(act):
            act.wait_ge(step, 7)
            nc.scalar.activation(std[:, :], var[:, :], ACT.Sqrt).then_inc(rooted, 1)


def phase_project(nc, mem, a):
    WN = D + 2 * HEADS
    with ExitStack() as ctx:
        sb = lambda n, s: ctx.enter_context(nc.sbuf_tensor(f"pj_{n}", s, fp32))
        sem = lambda n: ctx.enter_context(nc.semaphore(f"pj_{n}"))
        W = sb("W", [P, KD, WN])
        att = sb("att", [P, 2, D])
        prod = sb("prod", [P, KD, 2, D])
        xs = sb("xs", [P, 2, GT, D])
        xT = sb("xT", [P, KD, GN])
        hs = sb("hs", [P, 2, GT, WN])
        ps_t = ctx.enter_context(nc.psum_tensor("pj_pst", [P, KD, GN], fp32))
        ps_h = ctx.enter_context(nc.psum_tensor("pj_psh", [P, 2, 512], fp32))
        w_in, prods, w_ready = sem("w_in"), sem("prods"), sem("w_ready")
        xs_ready, tr_done, xt_ready = sem("xs_ready"), sem("tr_done"), sem("xt_ready")
        h_done, h_taken, a_taken, go = sem("h_done"), sem("h_taken"), sem("a_taken"), sem("go")
        h_stored = [sem(f"h_stored{s}") for s in range(2)]
        a_stored, hs_free = sem("a_stored"), sem("hs_free")
        block = ctx.enter_context(nc.Block())

        def groups(eng, do):
            with eng.Fori(0, NG // 2) as i:
                do(2 * i, 0, i, GT)
                do(2 * i + 1, 1, i, GT)
            do(NG, 0, NG // 2, NT - NG * GT)

        @block.sync
        def _(sp):
            sp.dma_start(W[:, :, 0:D], a["L0_gnn_W"].rearrange("(k p) h d -> p k (h d)", p=P)).then_inc(w_in, 16)
            for w, n in enumerate(("L0_gnn_att_src", "L0_gnn_att_dst")):
                sp.dma_start(att[:, w, :], a[n].rearrange("h d -> (h d)").partition_broadcast(P)).then_inc(w_in, 16)

            def store(g, s, i, nt):
                sp.wait_ge(a_taken, g * GT + nt)
                rows = mem.h_table[bass.ds(g * GN, nt * P), :] if not isinstance(g, int) else \
                    mem.h_table[g * GN:g * GN + nt * P, :]
                sp.dma_start(rows.rearrange("(t p) f -> p t f", p=P), hs[:, s, 0:nt, 0:D]).then_inc(h_stored[s], 16)
                sp.wait_ge(h_stored[s], 16 * (i + 1))
                sp.sem_inc(hs_free, 1)
            groups(sp, store)
            sp.wait_ge(a_taken, NT)
            sp.dma_start(mem.as_table[:, :].rearrange("(t p) h -> p t h", p=P),
                         mem.a_node[:, :, 0:HEADS]).then_inc(a_stored, 16)
            sp.wait_ge(a_stored, 16)
            sp.wait_ge(h_stored[0], 16 * (NG // 2 + 1))
            sp.wait_ge(h_stored[1], 16 * (NG // 2))

        @block.vector
        def _(dve):
            dve.wait_ge(w_in, 48)
            for k in range(KD):
                for w in range(2):
                    nc.vector.tensor_tensor(prod[:, k, w, :], W[:, k, 0:D], att[:, w, :], ALU.mult).then_inc(prods, 1)
            dve.wait_ge(prods, 2 * KD)
            for k in range(KD):
                nc.vector.tensor_reduce(W[:, k, D:WN].rearrange("p (w h) -> p w h", w=2),
                                        prod[:, k, :, :].rearrange("p w (h d) -> p w h d", d=HD),
                                        AX.X, ALU.add).then_inc(w_ready, 1)

            def apply(g, s, i, nt):
                dve.wait_ge(tr_done, g + 1)
                for j in range(nt):
                    t = g * GT + j
                    nc.vector.tensor_scalar(xs[:, s, j, :], tile_at(mem.X, t), col(mem.mean, t), col(mem.rstd, t),
                                            ALU.subtract, ALU.mult).then_inc(xs_ready, 1)

            def take(g, s, i, nt):
                for j in range(nt):
                    t = g * GT + j
                    dve.wait_ge(h_taken, t + 3)
                    nc.vector.tensor_copy(tile_at(mem.a_node, t), hs[:, s, j, D:WN]).then_inc(a_taken, 1)
            groups(dve, lambda *g: (apply(*g), take(*g)))

        @block.tensor
        def _(pe):
            pe.sem_inc(tr_done, 2)
            pe.wait_ge(w_ready, KD)

            def group(g, s, i, nt):
                pe.wait_ge(xs_ready, g * GT + nt)
                for k in range(KD):
                    for j in range(nt):
                        ins = nc.tensor.transpose(ps_t[:, k, j * P:(j + 1) * P], xs[:, s, j, k * P:(k + 1) * P],
                                                  mem.ident[:, :])
                ins.then_inc(tr_done, 1)
                pe.wait_ge(xt_ready, g + 1)
                for j in range(nt):
                    t = g * GT + j
                    pe.wait_ge(h_taken, t + 1)
                    for k in range(KD):
                        ins = nc.tensor.matmul(ps_h[:, j % 2, 0:WN], xT[:, k, j * P:(j + 1) * P], W[:, k, :],
                                               start=(k == 0), stop=(k == KD - 1))
                    ins.then_inc(h_done, 1)
            groups(pe, group)

        @block.scalar
        def _(act):
            act.sem_inc(h_taken, 2)
            act.sem_inc(hs_free, 2)
            act.sem_inc(go, 1)

            def group(g, s, i, nt):
                act.wait_ge(tr_done, g + 3)
                ins = nc.scalar.activation(xT[:, :, 0:nt * P], ps_t[:, :, 0:nt * P], ACT.Copy)
                ins.then_inc(xt_ready, 1)
                act.wait_ge(hs_free, g + 1)
                for j in range(nt):
                    t = g * GT + j
                    act.wait_ge(h_done, t + 1)
                    nc.scalar.activation(hs[:, s, j, :], ps_h[:, j % 2, 0:WN], ACT.Copy).then_inc(h_taken, 1)
            groups(act, group)


def tile_at(tensor, t, w=None):
    if isinstance(t, int):
        return tensor[:, t, :] if w is None else tensor[:, t, 0:w]
    ap = tensor[:, bass.ds(t, 1), :] if w is None else tensor[:, bass.ds(t, 1), 0:w]
    return ap.rearrange("p a f -> p (a f)")


def acc_as(acc, n):
    return acc[:, :, :].rearrange("p t f -> p (t f)")[:, 0:n]


def col(tensor, t):
    return tensor[:, t:t + 1] if isinstance(t, int) else tensor[:, bass.ds(t, 1)]


def phase_gather_scores(nc, mem, A):
    GC = 16
    with ExitStack() as ctx:
        sb = lambda n, s, d=fp32: ctx.enter_context(nc.sbuf_tensor(f"gs_{n}", s, d))
        sem = lambda n: ctx.enter_context(nc.semaphore(f"gs_{n}"))
        idx = sb("idx", [P, 2, GC], i32)
        rows = sb("rows", [P, 2, GC, HEADS])
        idx_ready, go = sem("idx_ready"), sem("go")
        taken = sem("taken")
        landed = [sem(f"landed{s}") for s in range(2)]
        block = ctx.enter_context(nc.Block())

        def steps(eng, do):
            with eng.Fori(0, SG // 2) as i:
                do(2 * i, 0, i)
                do(2 * i + 1, 1, i)
            do(SG - 1, 0, SG // 2)

        @block.gpsimd
        def _(pool):
            pool.sem_inc(go, 1)

            def gather(n, s, i):
                pool.wait_ge(idx_ready, n + 1)
                pool.sem_inc(go, 1)
                for j in range(GC):
                    pool.indirect_dma_start(rows[:, s, j, :], None, mem.as_table[:, :],
                                            bass.IndirectOffsetOnAxis(ap=idx[:, s, j:j + 1].bitcast(u32), axis=0))\
                        .then_inc(landed[s], 16)
            steps(pool, gather)

        @block.scalar
        def _(act):
            act.sem_inc(taken, 2)

            def take_index(n, s):
                act.wait_ge(taken, n + 1)
                nc.scalar.copy(idx[:, s, :], cols(mem.src_idx, n * GC, GC)).then_inc(idx_ready, 1)
            take_index(0, 0)
            take_index(1, 1)

            def step(n, s, i):
                act.wait_ge(landed[s], 16 * GC * (i + 1))
                nc.scalar.activation(chunks(A, n * GC, GC), rows[:, s, :, :], ACT.Copy).then_inc(taken, 1)
                if not isinstance(n, int) or n + 2 < SG:
                    take_index(n + 2, s)

            with act.Fori(0, SG // 2 - 1) as i:
                step(2 * i, 0, i)
                step(2 * i + 1, 1, i)
            for n in range(SG - 3, SG):
                step(n, n % 2, n // 2)


def phase_prefix_max(nc, mem, A, R):
    with ExitStack() as ctx:
        sb = lambda n, s: ctx.enter_context(nc.sbuf_tensor(f"pm_{n}", s, fp32))
        sem = lambda n: ctx.enter_context(nc.semaphore(f"pm_{n}"))
        S = sb("S", [P, SG, P])
        reset = sb("reset", [P, SG, P])
        slot = sb("slot", [P, 2, SB, HEADS])
        back = sb("back", [P, 2, P])
        ps = ctx.enter_context(nc.psum_tensor("pm_ps", [P, 2, 512], fp32))
        loaded, packed, tr, out = sem("loaded"), sem("packed"), sem("tr"), sem("out")
        scanned, go, packed2, tr2, out2 = sem("scanned"), sem("go"), sem("packed2"), sem("tr2"), sem("out2")
        Av = A[:, :, :].rearrange("e (k g) h -> e g k h", g=SG)
        Rv = R[:, :, :].rearrange("e (k g) h -> e g k h", g=SG)
        block = ctx.enter_context(nc.Block())

        def steps(eng, do):
            with eng.Fori(0, SG // 2) as i:
                do(2 * i, 0)
                do(2 * i + 1, 1)
            do(SG - 1, 0)

        def group(view, g, w=None):
            v = view[:, g:g + 1] if isinstance(g, int) else view[:, bass.ds(g, 1)]
            v = v.rearrange("e a k h -> e (a k) h")
            return v if w is None else v[:, :, 0:w]

        @block.sync
        def _(sp):
            flat = mem.reset_flat[:].rearrange("(k e) -> k e", k=SB)
            for k in range(SB):
                sp.dma_start(reset[k * HEADS:(k + 1) * HEADS, :, :].rearrange("h g e -> h (g e)"),
                             flat[k, :].partition_broadcast(HEADS)).then_inc(loaded, 16)

        @block.vector
        def _(dve):
            dve.sem_inc(tr, 2)
            dve.sem_inc(tr2, 2)
            dve.sem_inc(go, 1)

            def pack(g, s):
                dve.wait_ge(tr, g + 1)
                nc.vector.tensor_copy(slot[:, s, :, :], group(Av, g)).then_inc(packed, 1)
            steps(dve, pack)
            dve.wait_ge(out, SG + 2)
            dve.wait_ge(loaded, 16 * SB)
            flat = S[:, :, :].rearrange("p g e -> p (g e)")
            nc.vector.tensor_tensor_scan(flat, reset[:, :, :].rearrange("p g e -> p (g e)"), flat, -BIG,
                                         ALU.add, ALU.max).then_inc(scanned, 1)
            nc.vector.memset(R[:, :, HEADS:HEADS + 1], 1.0).then_inc(scanned, 1)
            dve.wait_ge(scanned, 1)

            def pack_back(g, s):
                dve.wait_ge(tr2, g + 1)
                nc.vector.tensor_copy(back[:, s, :], tile_at(S, g)).then_inc(packed2, 1)
            steps(dve, pack_back)

        @block.tensor
        def _(pe):
            def turn(src, ready, freed, done):
                def f(g, s):
                    pe.wait_ge(ready, g + 1)
                    pe.wait_ge(freed, g + 1)
                    nc.tensor.transpose(ps[:, s, 0:P], src(s), mem.ident[:, :]).then_inc(done, 1)
                return f
            steps(pe, turn(lambda s: slot[:, s, :, :].rearrange("p k h -> p (k h)"), packed, out, tr))
            steps(pe, turn(lambda s: back[:, s, :], packed2, out2, tr2))

        @block.scalar
        def _(act):
            act.sem_inc(out, 2)
            act.sem_inc(out2, 2)

            def copy_out(g, s):
                act.wait_ge(tr, g + 3)
                nc.scalar.activation(tile_at(S, g), ps[:, s, 0:P], ACT.Copy).then_inc(out, 1)
            steps(act, copy_out)

            def copy_back(g, s):
                act.wait_ge(tr2, g + 3)
                act.wait_ge(scanned, 2)
                nc.scalar.activation(group(Rv, g, HEADS), ps[:, s, 0:P].rearrange("p (k h) -> p k h", h=HEADS),
                                     ACT.Copy).then_inc(out2, 1)
            steps(act, copy_back)


def tile_of(first, r):
    return (first + r).with_bounds(min_val=0, max_val=NT - 1)


def bodies(eng, do):
    with eng.Fori(0, NB // 2 - 1) as i:
        do(2 * i, 0, i)
        do(2 * i + 1, 1, i)
    do(NB - 2, 0, NB // 2 - 1)
    do(NB - 1, 1, NB // 2 - 1)


def cols(tensor, at, n):
    return tensor[:, at:at + n] if isinstance(at, int) else tensor[:, bass.ds(at, n)]


def chunks(tensor, at, n):
    return tensor[:, at:at + n, :] if isinstance(at, int) else tensor[:, bass.ds(at, n), :]


def last_plus(n, b):
    return not isinstance(b, int) or b + n < NB


def phase_node_max(nc, mem, R, T):
    with ExitStack() as ctx:
        sb = lambda n, s, d=fp32: ctx.enter_context(nc.sbuf_tensor(f"nm_{n}", s, d))
        sem = lambda n: ctx.enter_context(nc.semaphore(f"nm_{n}"))
        pick = sb("pick", [P, CB, P])
        absent = sb("absent", [P, CB, 1])
        cand = sb("cand", [P, CB, HEADS])
        best = sb("best", [P, HEADS])
        lrelu = sb("lrelu", [P, NT, HEADS])
        ps = ctx.enter_context(nc.psum_tensor("nm_ps", [P, 512], fp32))
        picked, found, step, zero = sem("picked"), sem("found"), sem("step"), sem("zero")
        sel = ps[:, 0:CB * (HEADS + 1)].rearrange("p (c h) -> p c h", c=CB)
        block = ctx.enter_context(nc.Block())
        STEPS = 4

        @block.vector
        def _(dve):
            nc.vector.memset(T[:, :, :], -BIG).then_inc(zero, 1)
            dve.sem_inc(found, 1)

            def body(b, s, i):
                first, count, before = pairs_loop(dve, mem, b)
                with dve.Fori(0, count) as r:
                    q, t = before + r, tile_of(first, r)
                    dve.wait_ge(found, q + 1)
                    for j in range(CB):
                        ins = nc.vector.tensor_scalar(pick[:, j, :], mem.iota_row[:, :], cols(mem.last_e, b * CB + j, 1),
                                                      col(mem.neg_base, t), ALU.subtract, ALU.is_equal)
                    ins.then_inc(picked, 1)
                    dve.wait_ge(found, q + 2)
                    nc.vector.tensor_scalar(absent[:, :, :], sel[:, :, HEADS:HEADS + 1], BIG, -BIG,
                                            ALU.mult, ALU.add).then_inc(step, 1)
                    dve.wait_ge(step, q * STEPS + 1)
                    nc.vector.tensor_tensor(cand[:, :, :], sel[:, :, 0:HEADS],
                                            absent[:, :, :].to_broadcast([P, CB, HEADS]), ALU.add).then_inc(step, 1)
                    dve.wait_ge(step, q * STEPS + 2)
                    nc.vector.tensor_reduce(best[:, :], cand[:, :, :].rearrange("p c h -> p h c"), AX.X,
                                            ALU.max).then_inc(step, 1)
                    dve.wait_ge(step, q * STEPS + 3)
                    nc.vector.tensor_tensor(tile_at(T, t), tile_at(T, t), best[:, :], ALU.max).then_inc(step, 1)
            bodies(dve, body)
            _, last_count, last_before = pairs_loop(dve, mem, NB - 1)
            dve.wait_ge(step, (last_before + last_count) * STEPS)
            nc.vector.tensor_tensor(T[:, :, :], T[:, :, :], mem.a_node[:, :, HEADS:2 * HEADS], ALU.add).then_inc(zero, 1)
            nc.vector.tensor_copy(mem.node_terms[:, :, 0:HEADS], mem.a_node[:, :, HEADS:2 * HEADS])
            dve.wait_ge(zero, 2)
            nc.vector.tensor_scalar(lrelu[:, :, :], T[:, :, :], NEG_SLOPE, None, ALU.mult).then_inc(zero, 1)
            dve.wait_ge(zero, 3)
            nc.vector.tensor_tensor(mem.node_terms[:, :, HEADS:2 * HEADS], T[:, :, :], lrelu[:, :, :],
                                    ALU.max).then_inc(zero, 1)
            dve.wait_ge(zero, 4)

        @block.tensor
        def _(pe):
            def body(b, s, i):
                first, count, before = pairs_loop(pe, mem, b)
                with pe.Fori(0, count) as r:
                    q = before + r
                    pe.wait_ge(picked, q + 1)
                    for j in range(CB):
                        ins = nc.tensor.matmul(sel[:, j, :], pick[:, j, :], tile_at(R, b * CB + j), start=True, stop=True)
                    ins.then_inc(found, 1)
            bodies(pe, body)


def phase_attention(nc, mem, A, acc):
    with ExitStack() as ctx:
        sb = lambda n, s, d=fp32: ctx.enter_context(nc.sbuf_tensor(f"at_{n}", s, d))
        pb = lambda n, s: ctx.enter_context(nc.psum_tensor(f"at_{n}", s, fp32))
        sem = lambda n: ctx.enter_context(nc.semaphore(f"at_{n}"))
        idx = sb("idx", [P, 2, CB], i32)
        hrow = sb("hrow", [P, 2, CB, D])
        dst_row = sb("dst_row", [P, 2, EB])
        member_t = sb("member_t", [P, EB])
        member = sb("member", [P, CB, P])
        msg = sb("msg", [P, 2, CB, MSG])
        score = sb("score", [P, CB, HEADS])
        leaky = sb("leaky", [P, CB, HEADS])
        shifted = sb("shifted", [P, CB, HEADS])
        ps_u = pb("psu", [P, 2, 512])
        ps_a = pb("psa", [P, 512])
        go, cleared = sem("go"), sem("cleared")
        idx_ready, member_t_ready, u_read, terms_open = sem("idx_ready"), sem("member_t_ready"), sem("u_read"), sem("terms_open")
        shift_ready, score_step, exp_done, msg_done = sem("shift_ready"), sem("score_step"), sem("exp_done"), sem("msg_done")
        member_ready, summed, acc_done = sem("member_ready"), sem("summed"), sem("acc_done")
        landed = [sem(f"landed{s}") for s in range(2)]
        dst_in = [sem(f"dst_in{s}") for s in range(2)]
        terms = [ps_u[:, s, 0:CB * 2 * HEADS].rearrange("p (c h) -> p c h", c=CB) for s in range(2)]
        block = ctx.enter_context(nc.Block())

        @block.sync
        def _(sp):
            def load(b, s, i):
                sp.wait_ge(shift_ready, b + 1)
                row = mem.dst_flat[b * EB:(b + 1) * EB] if isinstance(b, int) else mem.dst_flat[bass.ds(b * EB, EB)]
                sp.dma_start(dst_row[:, s, :], row.partition_broadcast(P)).then_inc(dst_in[s], 16)
            bodies(sp, load)

        @block.gpsimd
        def _(pool):
            pool.sem_inc(go, 1)
            pool.memset(acc[:, :, :], 0.0).then_inc(cleared, 1)

            def gather(b, s, i):
                pool.wait_ge(idx_ready, b + 1)
                pool.sem_inc(go, 1)
                for j in range(CB):
                    pool.indirect_dma_start(hrow[:, s, j, :], None, mem.h_table[:, :],
                                            bass.IndirectOffsetOnAxis(ap=idx[:, s, j:j + 1].bitcast(u32), axis=0))\
                        .then_inc(landed[s], 16)
            bodies(pool, gather)

        @block.vector
        def _(dve):
            dve.sem_inc(shift_ready, 2)
            dve.sem_inc(msg_done, 2)

            def mark_t(b, s, i):
                dve.wait_ge(dst_in[s], 16 * (i + 1))
                first, count, before = pairs_loop(dve, mem, b)
                with dve.Fori(0, count) as r:
                    q, t = before + r, tile_of(first, r)
                    dve.wait_ge(u_read, q + 1)
                    nc.vector.tensor_scalar(member_t[:, :], dst_row[:, s, :], col(mem.node_id, t), None,
                                            ALU.is_equal).then_inc(member_t_ready, 1)

            mark_t(0, 0, 0)

            def body(b, s, i):
                if last_plus(1, b):
                    mark_t(b + 1, 1 - s, i + s)
                first, count, before = pairs_loop(dve, mem, b)
                dve.wait_ge(u_read, before + count + 1)
                nc.vector.tensor_tensor(score[:, :, :], chunks(A, b * CB, CB), terms[s][:, :, 0:HEADS],
                                        ALU.add).then_inc(score_step, 1)
                dve.wait_ge(score_step, 2 * b + 1)
                nc.vector.scalar_tensor_tensor(leaky[:, :, :], score[:, :, :], NEG_SLOPE, score[:, :, :],
                                               op0=ALU.mult, op1=ALU.max).then_inc(score_step, 1)
                dve.wait_ge(score_step, 2 * b + 2)
                nc.vector.tensor_tensor(shifted[:, :, :], leaky[:, :, :], terms[s][:, :, HEADS:2 * HEADS],
                                        ALU.subtract).then_inc(shift_ready, 1)
                dve.wait_ge(landed[s], 16 * CB * (i + 1))
                dve.wait_ge(exp_done, b + 1)
                nc.vector.tensor_tensor(msg[:, s, :, 0:D].rearrange("p c (h d) -> p c h d", d=HD),
                                        hrow[:, s, :, :].rearrange("p c (h d) -> p c h d", d=HD),
                                        msg[:, s, :, D:MSG].unsqueeze(3).to_broadcast([P, CB, HEADS, HD]),
                                        ALU.mult).then_inc(msg_done, 1)
                with dve.Fori(0, count) as r:
                    q, t = before + r, tile_of(first, r)
                    dve.wait_ge(summed, q + 1)
                    for j in range(CB):
                        ins = nc.vector.tensor_scalar(member[:, j, :], mem.iota_row[:, :], cols(mem.dst_e, b * CB + j, 1),
                                                      col(mem.neg_base, t), ALU.subtract, ALU.is_equal)
                    ins.then_inc(member_ready, 1)
            bodies(dve, body)

        @block.tensor
        def _(pe):
            pe.sem_inc(u_read, 1)
            pe.sem_inc(summed, 1)

            def open_terms(b, s):
                pe.wait_ge(shift_ready, b + 1)
                nc.tensor.matmul(ps_u[:, s, 0:CB * 2 * HEADS], mem.zeros[:, :], mem.zeros[:, 0:CB * 2 * HEADS],
                                 start=True, stop=False, skip_group_check=True).then_inc(terms_open, 1)

            def node_to_edge(b, s):
                open_terms(b, s)
                first, count, before = pairs_loop(pe, mem, b)
                with pe.Fori(0, count) as r:
                    q, t = before + r, tile_of(first, r)
                    pe.wait_ge(member_t_ready, q + 1)
                    for j in range(CB):
                        ins = nc.tensor.matmul(terms[s][:, j, :], member_t[:, j * P:(j + 1) * P],
                                               tile_at(mem.node_terms, t), start=False, stop=True, skip_group_check=True)
                    ins.then_inc(u_read, 1)

            node_to_edge(0, 0)

            def body(b, s, i):
                if last_plus(1, b):
                    node_to_edge(b + 1, 1 - s)
                first, count, before = pairs_loop(pe, mem, b)
                with pe.Fori(0, count) as r:
                    q, t = before + r, tile_of(first, r)
                    pe.wait_ge(msg_done, b + 3)
                    pe.wait_ge(member_ready, q + 1)
                    pe.wait_ge(acc_done, q + 1)
                    for j in range(CB):
                        nc.tensor.matmul(ps_a[:, 0:MSG], member[:, j, :], msg[:, s, j, :], start=(j == 0), stop=False)
                    nc.tensor.matmul(ps_a[:, 0:MSG], mem.ident[:, :], tile_at(acc, t), start=False,
                                     stop=True).then_inc(summed, 1)
            bodies(pe, body)

        @block.scalar
        def _(act):
            act.sem_inc(acc_done, 1)

            def take_index(b, s):
                act.wait_ge(msg_done, b + 1)
                nc.scalar.copy(idx[:, s, :], cols(mem.src_idx, b * CB, CB)).then_inc(idx_ready, 1)
            take_index(0, 0)
            take_index(1, 1)
            act.wait_ge(cleared, 1)

            def body(b, s, i):
                act.wait_ge(terms_open, b + 1)
                act.wait_ge(shift_ready, b + 3)
                nc.scalar.activation(msg[:, s, :, D:MSG], shifted[:, :, :], ACT.Exp).then_inc(exp_done, 1)
                if last_plus(2, b):
                    take_index(b + 2, s)
                first, count, before = pairs_loop(act, mem, b)
                with act.Fori(0, count) as r:
                    q, t = before + r, tile_of(first, r)
                    act.wait_ge(summed, q + 2)
                    nc.scalar.activation(tile_at(acc, t), ps_a[:, 0:MSG], ACT.Copy).then_inc(acc_done, 1)
            bodies(act, body)


def phase_attention_out(nc, mem, a, acc):
    UN = 7
    with ExitStack() as ctx:
        sb = lambda n, s: ctx.enter_context(nc.sbuf_tensor(f"ao_{n}", s, fp32))
        sem = lambda n: ctx.enter_context(nc.semaphore(f"ao_{n}"))
        den = sb("den", [P, NT, HEADS])
        bias = sb("bias", [P, D])
        msg = sb("msg", [P, 2, D])
        bias_in, step, scaled, biased, done = sem("bias_in"), sem("step"), sem("scaled"), sem("biased"), sem("done")
        block = ctx.enter_context(nc.Block())

        @block.sync
        def _(sp):
            sp.dma_start(bias[:, :], a["L0_gnn_bias"].partition_broadcast(P)).then_inc(bias_in, 16)

        @block.vector
        def _(dve):
            nc.vector.tensor_scalar(den[:, :, :], acc[:, :, D:MSG], 1e-16, None, ALU.add).then_inc(step, 1)
            dve.wait_ge(step, 1)
            nc.vector.reciprocal(den[:, :, :], den[:, :, :]).then_inc(step, 1)
            dve.wait_ge(step, 2)
            dve.wait_ge(bias_in, 16)
            for t in range(NT):
                s = t % 2
                nc.vector.tensor_tensor(msg[:, s, :].rearrange("p (h d) -> p h d", d=HD),
                                        tile_at(acc, t, D).rearrange("p (h d) -> p h d", d=HD),
                                        den[:, t, :].unsqueeze(2).to_broadcast([P, HEADS, HD]), ALU.mult).then_inc(scaled, 1)
                dve.wait_ge(scaled, t + 1)
                nc.vector.tensor_tensor(msg[:, s, :], msg[:, s, :], bias[:, :], ALU.add).then_inc(biased, 1)
                dve.wait_ge(biased, t + 1)
                nc.vector.scalar_tensor_tensor(tile_at(mem.X, t), msg[:, s, :], 0.0, tile_at(mem.X, t),
                                               op0=ALU.max, op1=ALU.add).then_inc(done, 1)
            dve.wait_ge(done, NT)


def phase_normalize(nc, mem, name, src, dst, bias_ap=None, table=None):
    UN = 7
    with ExitStack() as ctx:
        sb = lambda n, s: ctx.enter_context(nc.sbuf_tensor(f"{name}_{n}", s, fp32))
        sem = lambda n: ctx.enter_context(nc.semaphore(f"{name}_{n}"))
        done = sem("done")
        if table is not None:
            bias = sb("bias", [P, D])
            bias_in, stored = sem("bias_in"), sem("stored")
        block = ctx.enter_context(nc.Block())

        if table is not None:
            @block.sync
            def _(sp):
                sp.dma_start(bias[:, :], bias_ap.partition_broadcast(P)).then_inc(bias_in, 16)
                sp.wait_ge(done, 2 * NT)
                sp.dma_start(table[:, :].rearrange("(t p) f -> p t f", p=P), dst[:, :, 0:D]).then_inc(stored, 16)
                sp.wait_ge(stored, 16)

        @block.vector
        def _(dve):
            with dve.Fori(0, NT // UN) as i:
                for j in range(UN):
                    t = i * UN + j
                    nc.vector.tensor_scalar(tile_at(dst, t, D), tile_at(src, t), col(mem.mean, t), col(mem.rstd, t),
                                            ALU.subtract, ALU.mult).then_inc(done, 1)
            dve.wait_ge(done, NT)
            if table is not None:
                dve.wait_ge(bias_in, 16)
                with dve.Fori(0, NT // UN) as i:
                    for j in range(UN):
                        t = i * UN + j
                        nc.vector.tensor_tensor(tile_at(dst, t, D), tile_at(dst, t, D), bias[:, :], ALU.add).then_inc(done, 1)
                dve.wait_ge(done, 2 * NT)


class Moe:
    pass


def phase_moe(nc, mem, a, m, src, out=None):
    nm = m.name
    NE, L = m.experts, len(m.weights)
    HB = m.hidden // P
    with ExitStack() as ctx:
        sb = lambda n, s, d=fp32: ctx.enter_context(nc.sbuf_tensor(f"{nm}_{n}", s, d))
        pb = lambda n, s: ctx.enter_context(nc.psum_tensor(f"{nm}_{n}", s, fp32))
        sem = lambda n: ctx.enter_context(nc.semaphore(f"{nm}_{n}"))
        Ws, Bs = [], []
        for l in range(L):
            kb = KD if l == 0 else HB
            width = D if l == L - 1 else m.hidden
            Ws.append(sb(f"w{l}", [P, NE, kb, width]))
            Bs.append(sb(f"b{l}", [P, NE, HB]) if l < L - 1 else sb(f"b{l}", [NE, D]))
        rows_in = sb("brows", [NE * HB, (L - 1), P])
        xs = sb("xs", [P, GT, D])
        xT = sb("xT", [P, KD, GN])
        hT = [sb(f"hT{l}", [P, 2, HB, GN]) for l in range(L - 1)]
        wr = sb("wr", [P, m.router_blocks, NE])
        br = sb("br", [1, NE])
        logit = sb("logit", [P, GT, 8])
        top = sb("top", [P, GT, 8])
        idx = sb("idx", [P, GT, 8], u32)
        idxf = sb("idxf", [P, GT, 2])
        diff = sb("diff", [P, GT])
        ex = sb("ex", [P, GT])
        w12 = sb("w12", [P, GT, 2])
        hot = sb("hot", [P, GT, 2, NE])
        wf = sb("wf", [P, GT, NE])
        wT = sb("wT", [NE, GN])
        num = sb("num", [P, NE])
        if m.affine:
            gb = sb("gb", [P, 2, KD])
        if m.router_hidden:
            wr1, br1, rh = sb("wr1", [P, KD, P]), sb("br1", [P, 1]), sb("rh", [P, GN])
            peak, total = sb("peak", [P, GT]), sb("total", [P, GT])
        ps_t = pb("pst", [P, KD, GN])
        ps_h = pb("psh", [P, 2, GN])
        ps_y = pb("psy", [P, 2, GN])
        ps_r = pb("psr", [P, GN])
        ps_w = pb("psw", [P, GN])
        w_in, b_turned, ready = sem("w_in"), sem("b_turned"), sem("ready")
        xs_ready, tr_done, xt_ready = sem("xs_ready"), sem("tr_done"), sem("xt_ready")
        hid_done, act_done, y_done, y_taken = sem("hid_done"), sem("act_done"), sem("y_done"), sem("y_taken")
        r_done, rh_ready, r_step, exp_done = sem("r_done"), sem("rh_ready"), sem("r_step"), sem("exp_done")
        wt_done, wt_ready, b_done, stored = sem("wt_done"), sem("wt_ready"), sem("b_done"), sem("stored")
        r_bias, settled = sem("bias_added"), sem("settled")
        layers = L - 1
        HPG = NE * layers * HB
        block = ctx.enter_context(nc.Block())

        def groups(eng, do):
            with eng.Fori(0, NG) as g:
                do(g, GT)
            do(NG, NT - NG * GT)

        n_loads = [0]

        @block.sync
        def _(sp):
            def load(dst, src_ap, scattered=False):
                sp.dma_start(dst, src_ap, allow_slow_non_contiguous=scattered).then_inc(w_in, 16)
                n_loads[0] += 1
            load(br[:, :], a[m.router_bias].unsqueeze(0))
            if m.router_hidden:
                load(wr1[:, :, :], a["L1_ffn_router_w1"].rearrange("(k p) h -> p k h", p=P))
                load(br1[:, :], a["L1_ffn_router_b1"].unsqueeze(1), True)
                load(wr[:, 0, :], a[m.router])
            else:
                load(wr[:, :, :], a[m.router].rearrange("(k p) e -> p k e", p=P))
            if m.affine:
                load(gb[:, 0, :], a[m.affine[0]].rearrange("(k p) -> p k", p=P), True)
                load(gb[:, 1, :], a[m.affine[1]].rearrange("(k p) -> p k", p=P), True)
            for l in range(L):
                for e in range(NE):
                    load(Ws[l][:, e, :, :], a[m.weights[l]][e, :, :].rearrange("(k p) n -> p k n", p=P))
                if l < L - 1:
                    load(rows_in[:, l, :], a[m.biases[l]].rearrange("e (b p) -> (e b) p", p=P))
                else:
                    load(Bs[l][:, :], a[m.biases[l]])
            if out is not None:
                def store(g, nt):
                    if isinstance(g, int):
                        sp.wait_ge(y_taken, 2 + NG * NE * GT + NE * nt)
                        sp.dma_start(out[FULL_T * P:N, :], mem.X[0:TAIL, FULL_T, :]).then_inc(stored, 16)
                    else:
                        sp.wait_ge(y_taken, (g + 1) * (NE * GT) + 2)
                        sp.dma_start(out[bass.ds(g * GN, GN), :].rearrange("(t p) f -> p t f", p=P),
                                     mem.X[:, bass.ds(g * GT, GT), :]).then_inc(stored, 16)
                groups(sp, store)
                sp.wait_ge(stored, 16 * (NG + 1))

        @block.gpsimd
        def _(pool):
            pool.iota(num[:, :], pattern=[[1, NE]], base=0, channel_multiplier=0,
                      allow_small_or_imprecise_dtypes=True).then_inc(ready, 1)

        @block.vector
        def _(dve):
            dve.sem_inc(y_taken, 2)
            nc.vector.memset(logit[:, :, :], -BIG).then_inc(ready, 1)
            dve.wait_ge(ready, 3)
            STEPS = m.router_steps
            def group(g, nt):
                for j in range(nt):
                    t = g * GT + j
                    nc.vector.tensor_scalar(xs[:, j, :], tile_at(src, t, D), col(mem.mean, t), col(mem.rstd, t),
                                            ALU.subtract, ALU.mult).then_inc(xs_ready, 1)
                n = [0]

                def chain(ins):
                    ins.then_inc(r_step, 1)
                    n[0] += 1
                    dve.wait_ge(r_step, g * STEPS + n[0])

                dve.wait_ge(r_done, g + 1)
                chain(nc.vector.tensor_copy(logit[:, 0:nt, 0:NE], ps_r[:, 0:nt * 8].rearrange("p (t e) -> p t e", e=8)[:, :, 0:NE]))
                if m.router_hidden:
                    chain(nc.vector.tensor_reduce(peak[:, 0:nt], logit[:, 0:nt, 0:NE], AX.X, ALU.max))
                    chain(nc.vector.tensor_tensor(logit[:, 0:nt, 0:NE], logit[:, 0:nt, 0:NE],
                                                  peak[:, 0:nt].unsqueeze(2).to_broadcast([P, nt, NE]), ALU.subtract))
                    dve.wait_ge(exp_done, 2 * g + 1)
                    chain(nc.vector.tensor_reduce(total[:, 0:nt], logit[:, 0:nt, 0:NE], AX.X, ALU.add))
                    chain(nc.vector.reciprocal(total[:, 0:nt], total[:, 0:nt]))
                    chain(nc.vector.tensor_tensor(logit[:, 0:nt, 0:NE], logit[:, 0:nt, 0:NE],
                                                  total[:, 0:nt].unsqueeze(2).to_broadcast([P, nt, NE]), ALU.mult))
                dve.sem_inc(settled, 1)
                for j in range(nt):
                    ins = nc.vector.max(top[:, j, :], logit[:, j, :])
                chain(ins)
                dve.sem_inc(settled, 1)
                for j in range(nt):
                    ins = nc.vector.max_index(idx[:, j, :], top[:, j, :], logit[:, j, :])
                chain(ins)
                chain(nc.vector.tensor_copy(idxf[:, 0:nt, :], idx[:, 0:nt, 0:2]))
                chain(nc.vector.tensor_tensor(diff[:, 0:nt], top[:, 0:nt, 1], top[:, 0:nt, 0], ALU.subtract))
                dve.wait_ge(exp_done, (2 * g + 2) if m.router_hidden else (g + 1))
                chain(nc.vector.tensor_scalar(w12[:, 0:nt, 0], ex[:, 0:nt], 1.0, None, ALU.add))
                chain(nc.vector.reciprocal(w12[:, 0:nt, 0], w12[:, 0:nt, 0]))
                chain(nc.vector.tensor_tensor(w12[:, 0:nt, 1], w12[:, 0:nt, 0], ex[:, 0:nt], ALU.mult))
                for j in range(nt):
                    for w in range(2):
                        ins = nc.vector.tensor_scalar(hot[:, j, w, :], num[:, :], idxf[:, j, w:w + 1], w12[:, j, w:w + 1],
                                                      ALU.is_equal, ALU.mult)
                chain(ins)
                chain(nc.vector.tensor_tensor(wf[:, 0:nt, :], hot[:, 0:nt, 0, :], hot[:, 0:nt, 1, :], ALU.add))
                assert n[0] == STEPS, n[0]
                dve.wait_ge(wt_done, g + 1)
                nc.vector.tensor_copy(wT[:, 0:nt * P], ps_w[0:NE, 0:nt * P]).then_inc(wt_ready, 1)
                for h in range(-(-nt // 2)):
                    w = min(2, nt - 2 * h)
                    dve.wait_ge(b_done, 2 * g + h + 1)
                    t = g * GT + 2 * h
                    nc.vector.tensor_tensor(tiles_at(mem.X, t, w), tiles_at(mem.X, t, w), ps_y[:, h, 0:w * D], ALU.add)\
                        .then_inc(r_bias, 1)
                dve.wait_ge(r_bias, 2 * g + -(-nt // 2))
                for e in range(NE):
                    for j in range(nt):
                        t = g * GT + j
                        at = g * (NE * GT) + e * nt + j
                        dve.wait_ge(y_done, at + 1)
                        if e > 0:
                            dve.wait_ge(y_taken, at - nt + 3)
                        nc.vector.scalar_tensor_tensor(tile_at(mem.X, t), ps_y[:, at_slot(e * nt + j), 0:D], wf[:, j, e:e + 1],
                                                       tile_at(mem.X, t), op0=ALU.mult, op1=ALU.add).then_inc(y_taken, 1)
            groups(dve, group)
            dve.wait_ge(y_taken, 2 + NE * NT)

        @block.tensor
        def _(pe):
            pe.wait_ge(w_in, 16 * n_loads[0])
            for l in range(layers):
                nc.tensor.transpose(ps_r[:, l * NE * HB:(l + 1) * NE * HB], rows_in[:, l, :], mem.ident[0:NE * HB, 0:NE * HB])
            pe.wait_ge(ready, 2)
            nc.tensor.matmul(ps_w[:, 0:1], mem.zeros[:, :], mem.zeros[:, 0:1], start=True, stop=True).then_inc(b_turned, 1)
            pe.wait_ge(ready, 3)

            def group(g, nt):
                w = nt * P
                pe.wait_ge(xs_ready, g * GT + nt)
                for k in range(KD):
                    for j in range(nt):
                        ins = nc.tensor.transpose(ps_t[:, k, j * P:(j + 1) * P], xs[:, j, k * P:(k + 1) * P], mem.ident[:, :])
                ins.then_inc(tr_done, 1)
                pe.wait_ge(xt_ready, g + 1)
                if m.router_hidden:
                    for k in range(KD):
                        ins = nc.tensor.matmul(ps_r[:, 0:w], wr1[:, k, :], xT[:, k, 0:w], start=(k == 0), stop=(k == KD - 1))
                    ins.then_inc(rh_ready, 1)
                    pe.wait_ge(rh_ready, 2 * g + 2)
                for j in range(nt):
                    o = ps_r[:, j * 8:j * 8 + NE]
                    nc.tensor.matmul(o, mem.ones[0:1, :], br[:, :], start=True, stop=False)
                    for k in range(m.router_blocks):
                        lhs = rh[:, j * P:(j + 1) * P] if m.router_hidden else xT[:, k, j * P:(j + 1) * P]
                        ins = nc.tensor.matmul(o, lhs, wr[:, k, :], start=False, stop=(k == m.router_blocks - 1))
                ins.then_inc(r_done, 1)

                def hidden(e, l):
                    src_t = xT if l == 0 else hT[l - 1][:, e % 2, :, :]
                    kb = KD if l == 0 else HB
                    base = g * HPG + (e * layers + l) * HB
                    if l > 0:
                        pe.wait_ge(act_done, base + 2)
                    for b in range(HB):
                        pe.wait_ge(act_done, base + b + 1)
                        for k in range(kb):
                            ins = nc.tensor.matmul(ps_h[:, (e * layers * HB + l * HB + b) % 2, 0:w], Ws[l][:, e, k, b * P:(b + 1) * P],
                                                   src_t[:, k, 0:w], start=(k == 0), stop=(k == kb - 1))
                        ins.then_inc(hid_done, 1)

                def last(e):
                    base = g * HPG + (e + 1) * layers * HB
                    pe.wait_ge(act_done, base + 2)
                    for j in range(nt):
                        at = g * (NE * GT) + e * nt + j
                        pe.wait_ge(y_taken, at + 1)
                        for k in range(HB):
                            ins = nc.tensor.matmul(ps_y[:, at_slot(e * nt + j), 0:D], hT[layers - 1][:, e % 2, k, j * P:(j + 1) * P],
                                                   Ws[L - 1][:, e, k, :], start=(k == 0), stop=(k == HB - 1))
                        ins.then_inc(y_done, 1)

                hidden(0, 0)
                pe.wait_ge(r_step, (g + 1) * m.router_steps)
                for j in range(nt):
                    ins = nc.tensor.transpose(ps_w[0:NE, j * P:(j + 1) * P], wf[:, j, :], mem.ident[:, :])
                ins.then_inc(wt_done, 1)
                pe.wait_ge(wt_ready, g + 1)
                for h in range(-(-nt // 2)):
                    n = min(2, nt - 2 * h)
                    for j in range(n):
                        at = 2 * h + j
                        ins = nc.tensor.matmul(ps_y[:, h, j * D:(j + 1) * D], wT[:, at * P:(at + 1) * P], Bs[L - 1][:, :],
                                               start=True, stop=True)
                    ins.then_inc(b_done, 1)
                pe.wait_ge(r_bias, 2 * g + -(-nt // 2))
                for e in range(NE):
                    for l in range(layers):
                        if (e, l) != (0, 0) and not (l == 0):
                            hidden(e, l)
                    if e + 1 < NE:
                        hidden(e + 1, 0)
                    last(e)
            groups(pe, group)

        @block.scalar
        def _(act):
            act.sem_inc(act_done, 2)
            act.wait_ge(b_turned, 1)
            for l in range(layers):
                nc.scalar.activation(Bs[l][:, :, :].rearrange("p e b -> p (e b)"), ps_r[:, l * NE * HB:(l + 1) * NE * HB],
                                     ACT.Copy).then_inc(ready, 1) if l == layers - 1 else \
                    nc.scalar.activation(Bs[l][:, :, :].rearrange("p e b -> p (e b)"), ps_r[:, l * NE * HB:(l + 1) * NE * HB], ACT.Copy)
            act.wait_ge(ready, 3)

            def group(g, nt):
                w = nt * P
                act.wait_ge(tr_done, g + 1)
                if m.affine:
                    for k in range(KD):
                        ins = nc.scalar.activation(xT[:, k, 0:w], ps_t[:, k, 0:w], ACT.Identity,
                                                   bias=gb[:, 1, k:k + 1], scale=gb[:, 0, k:k + 1])
                else:
                    ins = nc.scalar.activation(xT[:, :, 0:w], ps_t[:, :, 0:w], ACT.Copy)
                ins.then_inc(xt_ready, 1)
                if m.router_hidden:
                    act.wait_ge(rh_ready, 2 * g + 1)
                    nc.scalar.activation(rh[:, 0:w], ps_r[:, 0:w], ACT.Relu, bias=br1[:, 0:1]).then_inc(rh_ready, 1)
                    act.wait_ge(r_step, g * m.router_steps + 3)
                    nc.scalar.activation(logit[:, 0:nt, 0:NE], logit[:, 0:nt, 0:NE], ACT.Exp).then_inc(exp_done, 1)

                def hidden(e, l):
                    base = g * HPG + (e * layers + l) * HB
                    for b in range(HB):
                        act.wait_ge(hid_done, base + b + 1)
                        nc.scalar.activation(hT[l][:, e % 2, b, 0:w], ps_h[:, (e * layers * HB + l * HB + b) % 2, 0:w], m.act,
                                             bias=Bs[l][:, e, b:b + 1]).then_inc(act_done, 1)
                hidden(0, 0)
                act.wait_ge(r_step, g * m.router_steps + m.diff_step)
                nc.scalar.activation(ex[:, 0:nt], diff[:, 0:nt], ACT.Exp).then_inc(exp_done, 1)
                for e in range(NE):
                    for l in range(1, layers):
                        hidden(e, l)
                    if e + 1 < NE:
                        hidden(e + 1, 0)
            groups(act, group)


def at_slot(n):
    return n % 2


def tiles_at(tensor, t, n):
    ap = tensor[:, t:t + n, :] if isinstance(t, int) else tensor[:, bass.ds(t, n), :]
    return ap.rearrange("p t f -> p (t f)")


def phase_edge_messages(nc, mem, a, acc):
    with ExitStack() as ctx:
        sb = lambda n, s, d=fp32: ctx.enter_context(nc.sbuf_tensor(f"em_{n}", s, d))
        pb = lambda n, s: ctx.enter_context(nc.psum_tensor(f"em_{n}", s, fp32))
        sem = lambda n: ctx.enter_context(nc.semaphore(f"em_{n}"))
        We = sb("We", [P, D])
        idx = sb("idx", [P, 2, CB], i32)
        xrow = sb("xrow", [P, 2, CB, D])
        attr = sb("attr", [P, 2, CB, ED])
        attr_t = sb("attr_t", [P, 2, EB])
        member = sb("member", [P, CB, P])
        msg = sb("msg", [P, 2, CB, D])
        ps_t = pb("pst", [P, EB])
        ps_e = [pb(f"pse{s}", [P, CB, D]) for s in range(2)]
        ps_a = pb("psa", [P, 512])
        go, cleared, w_in, part_in = sem("go"), sem("cleared"), sem("w_in"), sem("part_in")
        idx_ready, tr_done, at_ready, e_done = sem("idx_ready"), sem("tr_done"), sem("at_ready"), sem("e_done")
        add_done, relu_done, member_ready = sem("add_done"), sem("relu_done"), sem("member_ready")
        summed, acc_done = sem("summed"), sem("acc_done")
        landed = [sem(f"landed{s}") for s in range(2)]
        attr_in = [sem(f"attr_in{s}") for s in range(2)]
        block = ctx.enter_context(nc.Block())

        @block.sync
        def _(sp):
            sp.dma_start(We[:, :], a["L1_gnn_W_edge"]).then_inc(w_in, 16)

            def load(b, s, i):
                sp.wait_ge(tr_done, b + 1)
                if isinstance(b, int) and b == NB - 1:
                    full = LAST_E // P
                    at = b * EB
                    sp.dma_start(attr[0:LAST_E % P, s, full, :], a["edge_attr_128"][at + full * P:E, :]).then_inc(part_in, 16)
                    sp.wait_ge(part_in, 16)
                    sp.dma_start(attr[:, s, 0:full, :], a["edge_attr_128"][at:at + full * P, :]
                                 .rearrange("(c p) f -> p c f", p=P)).then_inc(attr_in[s], 16)
                else:
                    rows = a["edge_attr_128"][b * EB:(b + 1) * EB, :] if isinstance(b, int) else \
                        a["edge_attr_128"][bass.ds(b * EB, EB), :]
                    sp.dma_start(attr[:, s, :, :], rows.rearrange("(c p) f -> p c f", p=P)).then_inc(attr_in[s], 16)
            bodies(sp, load)

        @block.gpsimd
        def _(pool):
            pool.memset(acc[:, :, 0:D], 0.0).then_inc(cleared, 1)

            def gather(b, s, i):
                pool.wait_ge(idx_ready, b + 1)
                pool.sem_inc(go, 1)
                for j in range(CB):
                    pool.indirect_dma_start(xrow[:, s, j, :], None, mem.xn_table[:, :],
                                            bass.IndirectOffsetOnAxis(ap=idx[:, s, j:j + 1].bitcast(u32), axis=0))\
                        .then_inc(landed[s], 16)
            bodies(pool, gather)

        @block.vector
        def _(dve):
            dve.sem_inc(add_done, 2)

            def body(b, s, i):
                dve.wait_ge(landed[s], 16 * CB * (i + 1))
                dve.wait_ge(e_done, b + 3)
                nc.vector.tensor_tensor(msg[:, s, :, :], ps_e[s][:, :, :], xrow[:, s, :, :], ALU.add).then_inc(add_done, 1)
                first, count, before = pairs_loop(dve, mem, b)
                with dve.Fori(0, count) as r:
                    q, t = before + r, tile_of(first, r)
                    dve.wait_ge(summed, q + 1)
                    for j in range(CB):
                        ins = nc.vector.tensor_scalar(member[:, j, :], mem.iota_row[:, :], cols(mem.dst_e, b * CB + j, 1),
                                                      col(mem.neg_base, t), ALU.subtract, ALU.is_equal)
                    ins.then_inc(member_ready, 1)
            bodies(dve, body)

        @block.tensor
        def _(pe):
            pe.sem_inc(summed, 1)
            pe.sem_inc(tr_done, 2)
            pe.sem_inc(e_done, 2)
            pe.wait_ge(w_in, 16)

            def turn(b, s, i):
                pe.wait_ge(attr_in[s], 16 * (i + 1))
                pe.wait_ge(at_ready, b + 1)
                for j in range(CB):
                    ins = nc.tensor.transpose(ps_t[:, j * P:(j + 1) * P], attr[:, s, j, :], mem.ident[:, :])
                ins.then_inc(tr_done, 1)

            def edge_linear(b, s):
                pe.wait_ge(at_ready, b + 2)
                pe.wait_ge(add_done, b + 1)
                for j in range(CB):
                    ins = nc.tensor.matmul(ps_e[s][:, j, :], attr_t[:, s, j * P:(j + 1) * P], We[:, :], start=True, stop=True)
                ins.then_inc(e_done, 1)

            turn(0, 0, 0)
            turn(1, 1, 0)
            edge_linear(0, 0)

            def body(b, s, i):
                if last_plus(2, b):
                    turn(b + 2, s, i + 1)
                if last_plus(1, b):
                    edge_linear(b + 1, 1 - s)
                first, count, before = pairs_loop(pe, mem, b)
                with pe.Fori(0, count) as r:
                    q, t = before + r, tile_of(first, r)
                    pe.wait_ge(relu_done, b + 1)
                    pe.wait_ge(member_ready, q + 1)
                    pe.wait_ge(acc_done, q + 1)
                    for j in range(CB):
                        nc.tensor.matmul(ps_a[:, 0:D], member[:, j, :], msg[:, s, j, :], start=(j == 0), stop=False)
                    nc.tensor.matmul(ps_a[:, 0:D], mem.ident[:, :], tile_at(acc, t, D), start=False, stop=True).then_inc(summed, 1)
            bodies(pe, body)

        @block.scalar
        def _(act):
            act.sem_inc(acc_done, 1)
            act.sem_inc(at_ready, 1)

            def take_index(b, s):
                act.wait_ge(add_done, b + 1)
                nc.scalar.copy(idx[:, s, :], cols(mem.src_idx, b * CB, CB)).then_inc(idx_ready, 1)

            def take_attr(b, s):
                act.wait_ge(tr_done, b + 3)
                act.wait_ge(e_done, b + 1)
                nc.scalar.activation(attr_t[:, s, :], ps_t[:, :], ACT.Copy).then_inc(at_ready, 1)
            take_index(0, 0)
            take_index(1, 1)
            take_attr(0, 0)
            take_attr(1, 1)
            act.wait_ge(cleared, 1)

            def body(b, s, i):
                act.wait_ge(add_done, b + 3)
                nc.scalar.activation(msg[:, s, :, :], msg[:, s, :, :], ACT.Relu).then_inc(relu_done, 1)
                if last_plus(2, b):
                    take_index(b + 2, s)
                    take_attr(b + 2, s)
                first, count, before = pairs_loop(act, mem, b)
                with act.Fori(0, count) as r:
                    q, t = before + r, tile_of(first, r)
                    act.wait_ge(summed, q + 2)
                    nc.scalar.activation(tile_at(acc, t, D), ps_a[:, 0:D], ACT.Copy).then_inc(acc_done, 1)
            bodies(act, body)


def phase_node_mlp(nc, mem, a, acc):
    LN_ = (N - NG * GN)
    with ExitStack() as ctx:
        sb = lambda n, s, d=fp32: ctx.enter_context(nc.sbuf_tensor(f"ml_{n}", s, d))
        pb = lambda n, s: ctx.enter_context(nc.psum_tensor(f"ml_{n}", s, fp32))
        sem = lambda n: ctx.enter_context(nc.semaphore(f"ml_{n}"))
        W1, W2 = sb("W1", [P, KD, D]), sb("W2", [P, KD, D])
        vecs = sb("vecs", [P, 4, KD])
        eps1 = sb("eps1", [P, 1])
        xn = sb("xn", [P, 2, D])
        hs = sb("hs", [P, GT, D])
        hT = sb("hT", [P, KD, GN])
        h1 = sb("h1", [P, KD, GN])
        H = sb("H", [P, KD, NT * P])
        stats = sb("stats", [P, KD, NG + 1, 6])
        mv = sb("mv", [P, KD, 2])
        scale, shift, std = sb("scale", [P, KD]), sb("shift", [P, KD]), sb("std", [P, KD])
        yT = sb("yT", [P, 2, KD, GN])
        ps_t = pb("pst", [P, KD, GN])
        ps_h = pb("psh", [P, KD, GN])
        ps_y = pb("psy", [P, 2, 2, 512])
        w_in, xn_done, hs_ready, tr_done = sem("w_in"), sem("xn_done"), sem("hs_ready"), sem("tr_done")
        ht_ready, m_done, h1_ready, h2_ready = sem("ht_ready"), sem("m_done"), sem("h1_ready"), sem("h2_ready")
        seen, step, rooted, scaled = sem("seen"), sem("step"), sem("rooted"), sem("scaled")
        y_ready, y_turned, y_added = sem("y_ready"), sem("y_turned"), sem("y_added")
        block = ctx.enter_context(nc.Block())
        names = ("L1_gnn_b1", "L1_gnn_b2", "L1_gnn_gamma", "L1_gnn_beta")

        @block.sync
        def _(sp):
            sp.dma_start(W1[:, :, :], a["L1_gnn_W1"].rearrange("(k p) n -> p k n", p=P)).then_inc(w_in, 16)
            sp.dma_start(W2[:, :, :], a["L1_gnn_W2"].rearrange("(k p) n -> p k n", p=P)).then_inc(w_in, 16)
            sp.dma_start(eps1[:, :], a["L1_gnn_eps"].partition_broadcast(P)).then_inc(w_in, 16)
            for n, name in enumerate(names):
                sp.dma_start(vecs[:, n, :], a[name].rearrange("(k p) -> p k", p=P), allow_slow_non_contiguous=True).then_inc(w_in, 16)

        @block.vector
        def _(dve):
            dve.sem_inc(hs_ready, 1)
            dve.wait_ge(w_in, 16 * 7)
            nc.vector.tensor_scalar(eps1[:, :], eps1[:, :], 1.0, None, ALU.add).then_inc(step, 1)
            dve.wait_ge(step, 1)

            def group(g, nt):
                dve.wait_ge(tr_done, g + 1)
                for j in range(nt):
                    t = g * GT + j
                    s = j % 2
                    nc.vector.tensor_scalar(xn[:, s, :], tile_at(mem.X, t), col(mem.mean, t), col(mem.rstd, t),
                                            ALU.subtract, ALU.mult).then_inc(xn_done, 1)
                    dve.wait_ge(xn_done, t + 1)
                    nc.vector.scalar_tensor_tensor(hs[:, j, :], xn[:, s, :], eps1[:, 0:1], tile_at(acc, t, D),
                                                   op0=ALU.mult, op1=ALU.add).then_inc(hs_ready, 1)

            def groups_(do):
                with dve.Fori(0, NG) as g:
                    do(g, GT)
                do(NG, NT - NG * GT)
            groups_(group)
            dve.wait_ge(h2_ready, NG + 1)
            for g in range(NG + 1):
                w = GN if g < NG else LN_
                for k in range(KD):
                    nc.vector.bn_stats(stats[:, k, g, :], H[:, k, g * GN:g * GN + w]).then_inc(seen, 1)
            dve.wait_ge(seen, KD * (NG + 1))
            for k in range(KD):
                nc.vector.bn_aggr(mv[:, k, :], stats[:, k, :, :].rearrange("p g s -> p (g s)")).then_inc(step, 1)
            dve.wait_ge(step, 3)
            nc.vector.tensor_scalar(shift[:, :], mv[:, :, 1], EPS, None, ALU.add).then_inc(step, 1)
            dve.wait_ge(rooted, 1)
            nc.vector.reciprocal(scale[:, :], std[:, :]).then_inc(step, 1)
            dve.wait_ge(step, 5)
            nc.vector.tensor_tensor(scale[:, :], scale[:, :], vecs[:, 2, :], ALU.mult).then_inc(step, 1)
            dve.wait_ge(step, 6)
            nc.vector.tensor_tensor(shift[:, :], mv[:, :, 0], scale[:, :], ALU.mult).then_inc(step, 1)
            dve.wait_ge(step, 7)
            nc.vector.tensor_tensor(shift[:, :], vecs[:, 3, :], shift[:, :], ALU.subtract).then_inc(scaled, 1)
            for g in range(NG + 1):
                nt = GT if g < NG else NT - NG * GT
                dve.wait_ge(y_turned, g + 1)
                x4 = mem.X[:, g * GT:g * GT + nt, :].rearrange("p t f -> p (t f)")
                y4 = ps_y[:, g % 2, :, :].rearrange("p b f -> p (b f)")[:, 0:nt * D]
                nc.vector.tensor_tensor(x4, x4, y4, ALU.add).then_inc(y_added, 1)
            dve.wait_ge(y_added, NG + 1)

        @block.tensor
        def _(pe):
            pe.sem_inc(tr_done, 1)
            pe.wait_ge(w_in, 16 * 7)

            def group(g, nt):
                w = nt * P
                pe.wait_ge(hs_ready, g * GT + nt + 1)
                for k in range(KD):
                    for j in range(nt):
                        ins = nc.tensor.transpose(ps_t[:, k, j * P:(j + 1) * P], hs[:, j, k * P:(k + 1) * P], mem.ident[:, :])
                ins.then_inc(tr_done, 1)
                for n, (W, x, ready) in enumerate(((W1, hT, ht_ready), (W2, h1, h1_ready))):
                    pe.wait_ge(ready, g + 1)
                    for b in range(KD):
                        for k in range(KD):
                            ins = nc.tensor.matmul(ps_h[:, b, 0:w], W[:, k, b * P:(b + 1) * P], x[:, k, 0:w],
                                                   start=(k == 0), stop=(k == KD - 1))
                    ins.then_inc(m_done, 1)
            with pe.Fori(0, NG) as g:
                group(g, GT)
            pe_last = group(NG, NT - NG * GT)
            for g in range(NG + 1):
                nt = GT if g < NG else NT - NG * GT
                pe.wait_ge(y_ready, g + 1)
                if g >= 2:
                    pe.wait_ge(y_added, g - 1)
                for j in range(nt):
                    for k in range(KD):
                        ins = nc.tensor.transpose(ps_y[:, g % 2, j // 2, (j % 2) * D + k * P:(j % 2) * D + (k + 1) * P],
                                                  yT[:, g % 2, k, j * P:(j + 1) * P], mem.ident[:, :])
                ins.then_inc(y_turned, 1)

        @block.scalar
        def _(act):
            act.wait_ge(w_in, 16 * 7)

            def group(g, nt):
                w = nt * P
                act.wait_ge(tr_done, g + 2)
                nc.scalar.activation(hT[:, :, 0:w], ps_t[:, :, 0:w], ACT.Copy).then_inc(ht_ready, 1)
                act.wait_ge(m_done, 2 * g + 1)
                for k in range(KD):
                    ins = nc.scalar.activation(h1[:, k, 0:w], ps_h[:, k, 0:w], ACT.Relu, bias=vecs[:, 0, k:k + 1])
                ins.then_inc(h1_ready, 1)
                act.wait_ge(m_done, 2 * g + 2)
                for k in range(KD):
                    o = H[:, k, g * GN:g * GN + w] if isinstance(g, int) else H[:, k, bass.ds(g * GN, w)]
                    ins = nc.scalar.activation(o, ps_h[:, k, 0:w], ACT.Identity, bias=vecs[:, 1, k:k + 1])
                ins.then_inc(h2_ready, 1)
            with act.Fori(0, NG) as g:
                group(g, GT)
            group(NG, NT - NG * GT)
            act.wait_ge(step, 4)
            nc.scalar.activation(std[:, :], shift[:, :], ACT.Sqrt).then_inc(rooted, 1)
            act.wait_ge(scaled, 1)
            for g in range(NG + 1):
                w = GN if g < NG else (NT - NG * GT) * P
                if g >= 2:
                    act.wait_ge(y_turned, g - 1)
                for k in range(KD):
                    ins = nc.scalar.activation(yT[:, g % 2, k, 0:w], H[:, k, g * GN:g * GN + w], ACT.Relu,
                                               bias=shift[:, k:k + 1], scale=scale[:, k:k + 1])
                ins.then_inc(y_ready, 1)


def build(nc, a, out):
    mem = Mem()
    mem.NBP = CQ * BQ
    top = ExitStack()
    with top:
        sb = lambda n, s, d=fp32: top.enter_context(nc.sbuf_tensor(n, s, d))
        dr = lambda n, s, d=fp32: nc.dram_tensor(n, s, d, kind="Internal").ap()
        mem.dst_flat, mem.reset_flat = dr("dst_flat", [NCH * P]), dr("reset_flat", [NCH * P])
        mem.range_flat = dr("range_flat", [2, mem.NBP], i32)
        mem.h_table, mem.as_table, mem.xn_table = dr("h_table", [NT * P, D]), dr("as_table", [NT * P, HEADS]), dr("xn_table", [NT * P, D])
        mem.ident = sb("ident", [P, P])
        mem.iota_row = sb("iota_row", [P, P])
        mem.node_id = sb("node_id", [P, NT])
        mem.neg_base = sb("neg_base", [P, NT])
        mem.ones = sb("ones", [P, P])
        mem.zeros = sb("zeros", [P, P])
        mem.src_idx = sb("src_idx", [P, NCH], i32)
        mem.dst_e = sb("dst_e", [P, NCH])
        mem.ranges = sb("ranges", [1, mem.NBP], i32)
        mem.mean, mem.rstd = sb("mean", [P, NT]), sb("rstd", [P, NT])
        mem.X = sb("X", [P, NT, D])
        acc = sb("acc", [P, NT, MSG])
        with ExitStack() as inner:
            mem.last_e = inner.enter_context(nc.sbuf_tensor("last_e", [P, NCH], fp32))
            mem.a_node = inner.enter_context(nc.sbuf_tensor("a_node", [P, NT, 2 * HEADS], fp32))
            phase_load(nc, mem, a)
            phase_edges(nc, mem, a)
            layernorm_stats(nc, mem, "ln0", mem.X)
            phase_project(nc, mem, a)
            A = inner.enter_context(nc.sbuf_tensor("A", [P, NCH, HEADS], fp32))
            mem.node_terms = inner.enter_context(nc.sbuf_tensor("node_terms", [P, NT, 2 * HEADS], fp32))
            R = acc_as(acc, NCH * (HEADS + 1)).rearrange("p (c h) -> p c h", h=HEADS + 1)
            phase_gather_scores(nc, mem, A)
            phase_prefix_max(nc, mem, A, R)
            T = inner.enter_context(nc.sbuf_tensor("T", [P, NT, HEADS], fp32))
            phase_node_max(nc, mem, R, T)
            phase_attention(nc, mem, A, acc)
        phase_attention_out(nc, mem, a, acc)
        layernorm_stats(nc, mem, "ln1", mem.X)
        phase_normalize(nc, mem, "no1", mem.X, acc)
        layernorm_stats(nc, mem, "ln2", acc)
        m = Moe()
        m.name, m.experts, m.hidden, m.act = "m0", 8, 512, ACT.Gelu
        m.weights, m.biases = ("L0_ffn_W1", "L0_ffn_W2"), ("L0_ffn_b1", "L0_ffn_b2")
        m.affine, m.router, m.router_bias, m.router_hidden, m.router_blocks = \
            ("L0_ffn_gamma", "L0_ffn_beta"), "L0_ffn_Wr", "L0_ffn_br", False, KD
        m.router_steps, m.diff_step = 10, 5
        phase_moe(nc, mem, a, m, acc)
        layernorm_stats(nc, mem, "ln3", mem.X)
        phase_normalize(nc, mem, "no3", mem.X, acc, a["L1_gnn_b_edge"], mem.xn_table)
        phase_edge_messages(nc, mem, a, acc)
        phase_node_mlp(nc, mem, a, acc)
        layernorm_stats(nc, mem, "ln4", mem.X)
        m = Moe()
        m.name, m.experts, m.hidden, m.act = "m1", 6, 256, ACT.Relu
        m.weights = ("L1_ffn_expert_w1", "L1_ffn_expert_w2", "L1_ffn_expert_w3")
        m.biases = ("L1_ffn_expert_b1", "L1_ffn_expert_b2", "L1_ffn_expert_b3")
        m.affine, m.router, m.router_bias, m.router_hidden, m.router_blocks = \
            None, "L1_ffn_router_w2", "L1_ffn_router_b2", True, 1
        m.router_steps, m.diff_step = 15, 10
        phase_moe(nc, mem, a, m, mem.X, out)


_OUTS = [((N, D), "float32")]


def kernel(**inputs):
    import numpy as _np
    import concourse.bacc as _bacc
    from concourse import mybir as _mybir
    from concourse.bass_utils import run_bass_kernel_spmd as _run

    nc = _bacc.Bacc("TRN2", target_bir_lowering=False, num_devices=1)
    arrays, args = {}, {}
    for name, value in inputs.items():
        a = _np.ascontiguousarray(value)
        if a.ndim == 0:
            a = a.reshape(1)
        arrays[f"in_{name}_dram"] = a
        args[name] = nc.dram_tensor(f"in_{name}_dram", a.shape, _mybir.dt.from_np(a.dtype), kind="ExternalInput").ap()
    outs = [nc.dram_tensor(f"out_{i}_dram", shape, _mybir.dt.from_np(_np.dtype(dtype)), kind="ExternalOutput").ap()
            for i, (shape, dtype) in enumerate(_OUTS)]
    build(nc, args, outs[0])
    r = _run(nc, [arrays], core_ids=[0])
    return r.results[0]["out_0_dram"]
```

```python
import concourse.bass as bass
from concourse import mybir
from contextlib import ExitStack

fp32 = mybir.dt.float32
bf16 = mybir.dt.bfloat16
i32 = mybir.dt.int32
u32 = mybir.dt.uint32
ALU = mybir.AluOpType
ACT = mybir.ActivationFunctionType
AX = mybir.AxisListType

P = 128
N = 6250
D = 256
KD = D // P
E = 100000
HEADS = 8
HD = D // HEADS
NEG_SLOPE = 0.2
ED = 128
EPS = 1e-5
BIG = 1e30

NT = -(-N // P)
FULL_T = N // P
TAIL = N - FULL_T * P

CB = 8
EB = CB * P
NB = -(-E // EB)
NCH = NB * CB
LAST_E = E - (NB - 1) * EB
CQ = -(-NCH // P)
LAST_ROWS = NCH - (CQ - 1) * P
COUNT_AT, FURTHER_AT = 6, 12
BODIES_FIELD = 255
FIELD, FURTHER_FIELD = 63, (1 << 14) - 1
SB = 16
SG = NCH // SB
HC = CB // 2
BQ = P // CB

GT = 4
NG = NT // GT
GN = GT * P

PARTS = 3
MSG = D + HEADS


class Mem:
    pass


def bcast_free(ap, shape):
    return ap.to_broadcast(shape)


def body_pairs(eng, mem, body):
    at = slice(body, body + 1) if isinstance(body, int) else bass.ds(body, 1)
    word = eng.value_load(mem.ranges[0:1, at])
    first = eng.snap((word & FIELD).with_bounds(min_val=0, max_val=NT - 1))
    count = eng.snap(((word >> COUNT_AT) & FIELD).with_bounds(min_val=1, max_val=NT))
    further = eng.snap(((word >> FURTHER_AT) & FURTHER_FIELD).with_bounds(min_val=0, max_val=NB * (NT - 1)))
    before = eng.snap(further + body)
    return first, count, before, further


def pairs_loop(eng, mem, body):
    return body_pairs(eng, mem, body)[0:3]


def phase_load(nc, mem, a):
    with ExitStack() as ctx:
        sem = lambda n: ctx.enter_context(nc.semaphore(n))
        zeroed, made, loaded = sem("ld_zeroed"), sem("ld_made"), sem("ld_loaded")
        block = ctx.enter_context(nc.Block())

        @block.gpsimd
        def _(pool):
            pool.memset(mem.ident[:, :], 1.0).then_inc(made, 1)
            pool.wait_ge(made, 1)
            pool.affine_select(out=mem.ident[:, :], in_=mem.ident[:, :], compare_op=ALU.is_equal, fill=0.0,
                               base=0, pattern=[[-1, P]], channel_multiplier=1).then_inc(made, 1)
            pool.memset(mem.flip[:, :], 1.0).then_inc(made, 1)
            pool.wait_ge(made, 3)
            pool.affine_select(out=mem.flip[:, :], in_=mem.flip[:, :], compare_op=ALU.is_equal, fill=0.0,
                               base=-(P - 1), pattern=[[1, P]], channel_multiplier=1).then_inc(made, 1)
            pool.iota(mem.iota_row[:, :], pattern=[[1, P]], base=0, channel_multiplier=0,
                      allow_small_or_imprecise_dtypes=True).then_inc(made, 1)
            pool.iota(mem.node_id[:, :], pattern=[[P, NT]], base=0, channel_multiplier=1,
                      allow_small_or_imprecise_dtypes=True).then_inc(made, 1)
            pool.iota(mem.neg_base[:, :], pattern=[[-P, NT]], base=0, channel_multiplier=0,
                      allow_small_or_imprecise_dtypes=True).then_inc(made, 1)
            pool.wait_ge(made, 7)

        @block.vector
        def _(dve):
            nc.vector.memset(mem.ones[:, :], 1.0).then_inc(zeroed, 1)
            nc.vector.memset(mem.zeros[:, :], 0.0).then_inc(zeroed, 1)
            nc.vector.memset(mem.X[:, FULL_T, :], 0.0).then_inc(zeroed, 1)
            dve.wait_ge(zeroed, 3)

        @block.sync
        def _(sp):
            sp.dma_start(mem.X[:, 0:FULL_T, :],
                         a["x"][0:FULL_T * P, :].rearrange("(t p) f -> p t f", p=P)).then_inc(loaded, 16)
            sp.wait_ge(zeroed, 3)
            sp.dma_start(mem.X[0:TAIL, FULL_T, :], a["x"][FULL_T * P:N, :]).then_inc(loaded, 16)
            sp.wait_ge(loaded, 32)


def phase_edges(nc, mem, a):
    with ExitStack() as ctx:
        sb = lambda n, s, d=fp32: ctx.enter_context(nc.sbuf_tensor(n, s, d))
        sem = lambda n: ctx.enter_context(nc.semaphore(n))
        raw_src = sb("raw_src", [P, CQ, P], i32)
        raw_dst = sb("raw_dst", [P, CQ, P], i32)
        srcf = sb("srcf", [P, CQ, P])
        raw_next = sb("raw_next", [P, CQ, P], i32)
        dstf = sb("dstf", [P, CQ, P])
        nextf = sb("nextf", [P, CQ, P])
        falls = sb("falls", [P, CQ, P])
        real_next = sb("real_next", [P, CQ, P])
        any_falls = sb("any_falls", [P, 1])
        unsorted = sb("unsorted", [1, 1])
        first_reset = sb("first_reset", [1, 1])
        real_min = sb("real_min", [P, CQ, P])
        reset = sb("reset", [P, CQ, P])
        row_min = sb("row_min", [P, CQ])
        row_max = sb("row_max", [P, CQ])
        mm = sb("mm", [CQ, 2, BQ])
        mm_i = sb("mm_i", [CQ, 2, BQ], i32)
        mm_t = sb("mm_t", [CQ, 2, BQ], i32)
        flat = sb("flat", [1, 2, mem.NBP], i32)
        flat_f = sb("flat_f", [1, 2, mem.NBP])
        counts = sb("counts", [1, mem.NBP])
        plus_one = sb("plus_one", [1, mem.NBP])
        so_far = sb("so_far", [1, mem.NBP])
        packs = sb("packs", [1, 3, mem.NBP], i32)
        ps = ctx.enter_context(nc.psum_tensor("e_ps", [P, 2, 512], fp32))
        ps_m = ctx.enter_context(nc.psum_tensor("e_psm", [P, 2, P], fp32))
        filled, loaded = sem("ed_filled"), sem("ed_loaded")
        step, tr, ev = sem("ed_step"), sem("ed_tr"), sem("ed_ev")
        stored, back, next_step, tr_falls = sem("ed_stored"), sem("ed_back"), sem("ed_next_step"), sem("ed_tr_falls")
        block = ctx.enter_context(nc.Block())

        @block.sync
        def _(sp):
            sp.wait_ge(filled, 3)
            whole = (CQ - 1) * P * P
            rows = (E - whole) // P
            for raw, e in ((raw_src, a["src"]), (raw_dst, a["dst"])):
                sp.dma_start(raw[:, 0:CQ - 1, :],
                             e[0:whole].rearrange("(q p e) -> p q e", p=P, e=P)).then_inc(loaded, 16)
                sp.dma_start(raw[0:rows, CQ - 1, :],
                             e[whole:whole + rows * P].rearrange("(p e) -> p e", e=P)).then_inc(loaded, 16)
                sp.dma_start(raw[rows:rows + 1, CQ - 1, 0:E % P],
                             e[whole + rows * P:E].unsqueeze(0)).then_inc(loaded, 16)
            sp.dma_start(raw_next[:, 0:CQ - 1, :],
                         a["dst"][1:whole + 1].rearrange("(q p e) -> p q e", p=P, e=P)).then_inc(loaded, 16)
            sp.dma_start(raw_next[0:rows, CQ - 1, :],
                         a["dst"][whole + 1:whole + 1 + rows * P].rearrange("(p e) -> p e", e=P)).then_inc(loaded, 16)
            sp.dma_start(raw_next[rows:rows + 1, CQ - 1, 0:E % P - 1],
                         a["dst"][whole + 1 + rows * P:E].unsqueeze(0)).then_inc(loaded, 16)
            sp.wait_ge(step, 6)
            sp.dma_start(mem.reset_flat[0:1].unsqueeze(0), first_reset[:, :]).then_inc(stored, 16)
            for sbt, dr in ((dstf, mem.dst_flat), (reset, mem.reset_flat[1:1 + NCH * P])):
                sp.dma_start(dr[0:whole].rearrange("(q p e) -> p q e", p=P, e=P),
                             sbt[:, 0:CQ - 1, :]).then_inc(stored, 16)
                sp.dma_start(dr[whole:NCH * P].rearrange("(p e) -> p e", e=P),
                             sbt[0:LAST_ROWS, CQ - 1, :]).then_inc(stored, 16)
            sp.wait_ge(step, 8)
            for w in range(2):
                sp.dma_start(mem.range_flat[w, :].rearrange("(q b) -> q b", b=BQ), mm_t[:, w, :]).then_inc(back, 16)
            sp.wait_ge(back, 32)
            sp.dma_start(flat[:, :, :], mem.range_flat[:, :].unsqueeze(0)).then_inc(back, 16)
            sp.wait_ge(stored, 80)

        @block.vector
        def _(dve):
            nc.vector.memset(raw_src[:, :, :], 0).then_inc(filled, 1)
            nc.vector.memset(raw_dst[:, :, :], -1).then_inc(filled, 1)
            nc.vector.memset(raw_next[:, :, :], -1).then_inc(filled, 1)
            nc.vector.memset(first_reset[:, :], -BIG).then_inc(filled, 1)
            dve.wait_ge(loaded, 144)
            nc.vector.tensor_copy(nextf[:, :, :], raw_next[:, :, :]).then_inc(next_step, 1)
            nc.vector.tensor_copy(srcf[:, :, :], raw_src[:, :, :]).then_inc(step, 1)
            nc.vector.tensor_copy(dstf[:, :, :], raw_dst[:, :, :]).then_inc(step, 1)
            dve.wait_ge(step, 2)
            nc.vector.tensor_scalar(real_min[:, :, :], dstf[:, :, :], 0.0, float(NT * P), ALU.is_lt, ALU.mult).then_inc(step, 1)
            nc.vector.tensor_reduce(row_max[:, :], dstf[:, :, :], AX.X, ALU.max).then_inc(step, 1)
            dve.wait_ge(step, 4)
            nc.vector.tensor_tensor(real_min[:, :, :], real_min[:, :, :], dstf[:, :, :], ALU.add).then_inc(step, 1)
            dve.wait_ge(step, 5)
            nc.vector.tensor_reduce(row_min[:, :], real_min[:, :, :], AX.X, ALU.min).then_inc(next_step, 1)
            dve.wait_ge(next_step, 1)
            nc.vector.tensor_tensor(falls[:, :, :], nextf[:, :, :], dstf[:, :, :], ALU.is_lt).then_inc(next_step, 1)
            nc.vector.tensor_scalar(real_next[:, :, :], nextf[:, :, :], 0.0, None, ALU.is_ge).then_inc(next_step, 1)
            nc.vector.tensor_tensor(reset[:, :, :], nextf[:, :, :], dstf[:, :, :], ALU.not_equal).then_inc(next_step, 1)
            dve.wait_ge(next_step, 5)
            nc.vector.tensor_tensor(falls[:, :, :], falls[:, :, :], real_next[:, :, :], ALU.mult).then_inc(next_step, 1)
            nc.vector.tensor_scalar(reset[:, :, :], reset[:, :, :], -BIG, None, ALU.mult).then_inc(step, 1)
            dve.wait_ge(next_step, 6)
            nc.vector.tensor_reduce(any_falls[:, :], falls[:, :, :].rearrange("p q e -> p (q e)"), AX.X, ALU.max).then_inc(next_step, 1)
            dve.wait_ge(tr_falls, 1)
            nc.vector.tensor_reduce(unsorted[:, :], ps_m[0:1, 0, :], AX.X, ALU.max).then_inc(next_step, 1)
            dve.wait_ge(next_step, 8)
            nc.vector.tensor_scalar(mem.general_steps[:, :], unsorted[:, :], float(NB), None, ALU.mult).then_inc(next_step, 1)
            dve.wait_ge(tr, 1)
            for w, op in ((0, ALU.min), (1, ALU.max)):
                ins = nc.vector.tensor_reduce(mm[:, w, :], ps_m[0:CQ, w, :].rearrange("q (b c) -> q b c", c=CB), AX.X, op)
            ins.then_inc(ev, 1)
            dve.wait_ge(ev, 1)
            nc.vector.tensor_copy(mm_i[:, :, :], mm[:, :, :]).then_inc(step, 1)
            dve.wait_ge(step, 7)
            nc.vector.tensor_scalar(mm_t[:, :, :], mm_i[:, :, :], 7, None, ALU.arith_shift_right).then_inc(step, 1)
            n_tr = 1
            for src, dst in ((srcf, mem.src_idx), (dstf, mem.dst_e), (reset, mem.reset_e)):
                for q in range(CQ):
                    w = P if q < CQ - 1 else LAST_ROWS
                    n_tr += 1
                    dve.wait_ge(tr, n_tr)
                    nc.vector.tensor_copy(dst[:, q * P:q * P + w], ps[:, n_tr % 2, 0:w]).then_inc(ev, 1)
            dve.wait_ge(back, 48)
            nc.vector.tensor_copy(flat_f[:, :, :], flat[:, :, :]).then_inc(step, 1)
            dve.wait_ge(step, 9)
            nc.vector.tensor_tensor(counts[:, :], flat_f[:, 1, :], flat_f[:, 0, :], ALU.subtract).then_inc(step, 1)
            dve.wait_ge(step, 10)
            nc.vector.tensor_scalar(plus_one[:, :], counts[:, :], 1.0, None, ALU.add).then_inc(step, 1)
            dve.wait_ge(step, 11)
            nc.vector.tensor_tensor_scan(so_far[:, :], counts[:, :], counts[:, :], 0.0, ALU.add, ALU.bypass).then_inc(step, 1)
            dve.wait_ge(step, 12)
            nc.vector.tensor_copy(packs[:, 1, :], plus_one[:, :]).then_inc(step, 1)
            nc.vector.tensor_tensor(packs[:, 2, :], so_far[:, :], counts[:, :], ALU.subtract).then_inc(step, 1)
            dve.wait_ge(step, 14)
            nc.vector.tensor_scalar(packs[:, 1, :], packs[:, 1, :], COUNT_AT, None, ALU.arith_shift_left).then_inc(step, 1)
            nc.vector.tensor_scalar(packs[:, 2, :], packs[:, 2, :], FURTHER_AT, None, ALU.arith_shift_left).then_inc(step, 1)
            dve.wait_ge(step, 16)
            nc.vector.tensor_tensor(packs[:, 0, :], packs[:, 1, :], packs[:, 2, :], ALU.bitwise_or).then_inc(step, 1)
            dve.wait_ge(step, 17)
            nc.vector.tensor_tensor(mem.ranges[:, :], packs[:, 0, :], flat[:, 0, :], ALU.bitwise_or).then_inc(step, 1)
            dve.wait_ge(step, 18)

        @block.tensor
        def _(pe):
            pe.wait_ge(next_step, 7)
            nc.tensor.transpose(ps_m[0:1, 0, :], any_falls[:, :], mem.ident[:, :]).then_inc(tr_falls, 1)
            pe.wait_ge(next_step, 8)
            nc.tensor.transpose(ps_m[0:CQ, 0, :], row_min[:, :], mem.ident[:, :])
            nc.tensor.transpose(ps_m[0:CQ, 1, :], row_max[:, :], mem.ident[:, :]).then_inc(tr, 1)
            pe.wait_ge(step, 6)
            n_tr = 1
            for src in (srcf, dstf, reset):
                for q in range(CQ):
                    n_tr += 1
                    if n_tr >= 4:
                        pe.wait_ge(ev, n_tr - 2)
                    nc.tensor.transpose(ps[:, n_tr % 2, 0:P], src[:, q, :], mem.ident[:, :]).then_inc(tr, 1)


def layernorm_stats(nc, mem, name, src, first=None):
    with ExitStack() as ctx:
        sb = lambda n, s: ctx.enter_context(nc.sbuf_tensor(f"{name}_{n}", s, fp32))
        sem = lambda n: ctx.enter_context(nc.semaphore(f"{name}_{n}"))
        stats = sb("stats", [P, NT, 6])
        total, diff, m2, var = sb("total", [P, NT]), sb("diff", [P, NT]), sb("m2", [P, NT]), sb("var", [P, NT])
        std = sb("std", [P, NT])
        step = sem("step")
        mem.roots += 1
        block = ctx.enter_context(nc.Block())
        UN = 7

        @block.vector
        def _(dve):
            with dve.Fori(0, NT // UN) as i:
                for j in range(UN):
                    nc.vector.bn_stats(stats[:, bass.ds(i * UN + j, 1), :].rearrange("p a s -> p (a s)"),
                                       src[:, bass.ds(i * UN + j, 1), 0:D].rearrange("p a f -> p (a f)")).then_inc(step, 1)
            dve.wait_ge(step, NT)
            nc.vector.tensor_tensor(total[:, :], stats[:, :, 1], stats[:, :, 4], ALU.add).then_inc(step, 1)
            nc.vector.tensor_tensor(diff[:, :], stats[:, :, 1], stats[:, :, 4], ALU.subtract).then_inc(step, 1)
            nc.vector.tensor_tensor(m2[:, :], stats[:, :, 2], stats[:, :, 5], ALU.add).then_inc(step, 1)
            dve.wait_ge(step, NT + 3)
            nc.vector.tensor_scalar(mem.mean[:, :], total[:, :], 0.5, None, ALU.mult).then_inc(step, 1)
            nc.vector.scalar_tensor_tensor(diff[:, :], diff[:, :], 0.25, diff[:, :],
                                           op0=ALU.mult, op1=ALU.mult).then_inc(step, 1)
            dve.wait_ge(step, NT + 5)
            nc.vector.scalar_tensor_tensor(var[:, :], m2[:, :], 1.0 / D, diff[:, :],
                                           op0=ALU.mult, op1=ALU.add).then_inc(step, 1)
            dve.wait_ge(step, NT + 6)
            nc.vector.tensor_scalar(var[:, :], var[:, :], EPS, None, ALU.add).then_inc(step, 1)
            dve.wait_ge(mem.rooted, mem.roots)
            nc.vector.reciprocal(mem.rstd[:, :], std[:, :]).then_inc(step, 1)
            dve.wait_ge(step, NT + 8)

        @block.scalar
        def _(act):
            act.wait_ge(step, NT + 7)
            nc.scalar.activation(std[:, :], var[:, :], ACT.Sqrt).then_inc(mem.rooted, 1)


def phase_project(nc, mem, a):
    WN = D + 2 * HEADS
    with ExitStack() as ctx:
        sb = lambda n, s: ctx.enter_context(nc.sbuf_tensor(f"pj_{n}", s, fp32))
        sem = lambda n: ctx.enter_context(nc.semaphore(f"pj_{n}"))
        W = sb("W", [P, KD, WN])
        att = sb("att", [P, 2, D])
        prod = sb("prod", [P, KD, 2, D])
        xs = sb("xs", [P, 2, GT, D])
        xT = sb("xT", [P, KD, GN])
        hs = sb("hs", [P, 2, GT, WN])
        ps_t = ctx.enter_context(nc.psum_tensor("pj_pst", [P, KD, GN], fp32))
        ps_h = ctx.enter_context(nc.psum_tensor("pj_psh", [P, 2, 512], fp32))
        w_in, prods, w_ready = sem("w_in"), sem("prods"), sem("w_ready")
        xs_ready, tr_done, xt_ready = sem("xs_ready"), sem("tr_done"), sem("xt_ready")
        h_done, h_taken, a_taken = sem("h_done"), sem("h_taken"), sem("a_taken")
        h_stored = [sem(f"h_stored{s}") for s in range(2)]
        a_stored, hs_free = sem("a_stored"), sem("hs_free")
        block = ctx.enter_context(nc.Block())

        def groups(eng, do):
            with eng.Fori(0, NG // 2) as i:
                do(2 * i, 0, i, GT)
                do(2 * i + 1, 1, i, GT)
            do(NG, 0, NG // 2, NT - NG * GT)

        @block.sync
        def _(sp):
            sp.dma_start(W[:, :, 0:D], a["L0_gnn_W"].rearrange("(k p) h d -> p k (h d)", p=P)).then_inc(w_in, 16)
            for w, n in enumerate(("L0_gnn_att_src", "L0_gnn_att_dst")):
                sp.dma_start(att[:, w, :], a[n].rearrange("h d -> (h d)").partition_broadcast(P)).then_inc(w_in, 16)

            def store(g, s, i, nt):
                sp.wait_ge(a_taken, g * GT + nt)
                rows = mem.h_table[bass.ds(g * GN, nt * P), :] if not isinstance(g, int) else \
                    mem.h_table[g * GN:g * GN + nt * P, :]
                sp.dma_start(rows.rearrange("(t p) f -> p t f", p=P), hs[:, s, 0:nt, 0:D]).then_inc(h_stored[s], 16)
                sp.wait_ge(h_stored[s], 16 * (i + 1))
                sp.sem_inc(hs_free, 1)
            groups(sp, store)
            sp.wait_ge(a_taken, NT)
            sp.dma_start(mem.as_table[:, :].rearrange("(t p) h -> p t h", p=P),
                         mem.a_node[:, :, 0:HEADS]).then_inc(a_stored, 16)
            sp.wait_ge(a_stored, 16)
            sp.wait_ge(h_stored[0], 16 * (NG // 2 + 1))
            sp.wait_ge(h_stored[1], 16 * (NG // 2))

        @block.vector
        def _(dve):
            dve.wait_ge(w_in, 48)
            for k in range(KD):
                for w in range(2):
                    nc.vector.tensor_tensor(prod[:, k, w, :], W[:, k, 0:D], att[:, w, :], ALU.mult).then_inc(prods, 1)
            dve.wait_ge(prods, 2 * KD)
            for k in range(KD):
                nc.vector.tensor_reduce(W[:, k, D:WN].rearrange("p (w h) -> p w h", w=2),
                                        prod[:, k, :, :].rearrange("p w (h d) -> p w h d", d=HD),
                                        AX.X, ALU.add).then_inc(w_ready, 1)

            def apply(g, s, i, nt):
                dve.wait_ge(tr_done, g + 1)
                for j in range(nt):
                    t = g * GT + j
                    nc.vector.tensor_scalar(xs[:, s, j, :], tile_at(mem.X, t), col(mem.mean, t), col(mem.rstd, t),
                                            ALU.subtract, ALU.mult).then_inc(xs_ready, 1)

            def take(g, s, i, nt):
                for j in range(nt):
                    t = g * GT + j
                    dve.wait_ge(h_taken, t + 3)
                    nc.vector.tensor_copy(tile_at(mem.a_node, t), hs[:, s, j, D:WN]).then_inc(a_taken, 1)
            groups(dve, lambda *g: (apply(*g), take(*g)))

        @block.tensor
        def _(pe):
            pe.sem_inc(tr_done, 2)
            pe.wait_ge(w_ready, KD)

            def group(g, s, i, nt):
                pe.wait_ge(xs_ready, g * GT + nt)
                for k in range(KD):
                    for j in range(nt):
                        ins = nc.tensor.transpose(ps_t[:, k, j * P:(j + 1) * P], xs[:, s, j, k * P:(k + 1) * P],
                                                  mem.ident[:, :])
                ins.then_inc(tr_done, 1)
                pe.wait_ge(xt_ready, g + 1)
                for j in range(nt):
                    t = g * GT + j
                    pe.wait_ge(h_taken, t + 1)
                    for k in range(KD):
                        ins = nc.tensor.matmul(ps_h[:, j % 2, 0:WN], xT[:, k, j * P:(j + 1) * P], W[:, k, :],
                                               start=(k == 0), stop=(k == KD - 1))
                    ins.then_inc(h_done, 1)
            groups(pe, group)

        @block.scalar
        def _(act):
            act.sem_inc(h_taken, 2)
            act.sem_inc(hs_free, 2)


            def group(g, s, i, nt):
                act.wait_ge(tr_done, g + 3)
                ins = nc.scalar.activation(xT[:, :, 0:nt * P], ps_t[:, :, 0:nt * P], ACT.Copy)
                ins.then_inc(xt_ready, 1)
                act.wait_ge(hs_free, g + 1)
                for j in range(nt):
                    t = g * GT + j
                    act.wait_ge(h_done, t + 1)
                    nc.scalar.activation(hs[:, s, j, :], ps_h[:, j % 2, 0:WN], ACT.Copy).then_inc(h_taken, 1)
            groups(act, group)


def tile_at(tensor, t, w=None):
    if isinstance(t, int):
        return tensor[:, t, :] if w is None else tensor[:, t, 0:w]
    ap = tensor[:, bass.ds(t, 1), :] if w is None else tensor[:, bass.ds(t, 1), 0:w]
    return ap.rearrange("p a f -> p (a f)")


def acc_as(acc, n):
    return acc[:, :, :].rearrange("p t f -> p (t f)")[:, 0:n]


def col(tensor, t):
    return tensor[:, t:t + 1] if isinstance(t, int) else tensor[:, bass.ds(t, 1)]


def phase_scores(nc, mem, AR):
    GC = 16
    PT = PARTS * HEADS
    with ExitStack() as ctx:
        sb = lambda n, s, d=fp32: ctx.enter_context(nc.sbuf_tensor(f"gs_{n}", s, d))
        sem = lambda n: ctx.enter_context(nc.semaphore(f"gs_{n}"))
        idx = sb("idx", [P, 2, GC], i32)
        rows = sb("rows", [P, 2, GC, HEADS])
        parts = sb("parts", [P, NT, PT], bf16)
        rest = sb("rest", [P, 2, NT, HEADS])
        dst_row = sb("dst_row", [P, 2, EB])
        member_t = sb("member_t", [P, 2 * EB], bf16)
        zeros = sb("zeros", [P, CB * PT], bf16)
        ps = ctx.enter_context(nc.psum_tensor("gs_ps", [P, 2, 512], fp32))
        idx_ready, taken, dve_step, marked = sem("idx_ready"), sem("taken"), sem("dve_step"), sem("marked")
        spread, a_dst_taken = sem("spread"), sem("a_dst_taken")
        landed = [sem(f"landed{s}") for s in range(2)]
        dst_in = [sem(f"dst_in{s}") for s in range(2)]
        terms = [ps[:, s, 0:CB * PT].rearrange("p (c h) -> p c h", c=CB) for s in range(2)]
        block = ctx.enter_context(nc.Block())

        def steps(eng, do):
            with eng.Fori(0, SG // 2) as i:
                do(2 * i, 0, i)
                do(2 * i + 1, 1, i)
            do(SG - 1, 0, SG // 2)

        def pair_slot(q):
            return (q & 1) * EB

        @block.sync
        def _(sp):
            def load(b, s, i):
                sp.wait_ge(a_dst_taken, b + 1)
                row = mem.dst_flat[b * EB:(b + 1) * EB] if isinstance(b, int) else mem.dst_flat[bass.ds(b * EB, EB)]
                sp.dma_start(dst_row[:, s, :], row.partition_broadcast(P)).then_inc(dst_in[s], 16)
            bodies(sp, load)

        @block.gpsimd
        def _(pool):
            def gather(n, s, i):
                pool.wait_ge(idx_ready, n + 1)
                pool.sem_inc(mem.tick, 1)
                for j in range(GC):
                    pool.indirect_dma_start(rows[:, s, j, :], None, mem.as_table[:, :],
                                            bass.IndirectOffsetOnAxis(ap=idx[:, s, j:j + 1].bitcast(u32), axis=0))\
                        .then_inc(landed[s], 16)
            steps(pool, gather)

        @block.scalar
        def _(act):
            act.sem_inc(taken, 2)

            def take_index(n, s):
                act.wait_ge(taken, n + 1)
                nc.scalar.copy(idx[:, s, :], cols(mem.src_idx, n * GC, GC)).then_inc(idx_ready, 1)
            take_index(0, 0)
            take_index(1, 1)

            def step(n, s, i):
                act.wait_ge(landed[s], 16 * GC * (i + 1))
                nc.scalar.activation(AR[:, n * GC:(n + 1) * GC, 0, :] if isinstance(n, int) else AR[:, bass.ds(n * GC, GC), 0, :],
                                     rows[:, s, :, :], ACT.Copy).then_inc(taken, 1)
                if not isinstance(n, int) or n + 2 < SG:
                    take_index(n + 2, s)

            with act.Fori(0, SG // 2 - 1) as i:
                step(2 * i, 0, i)
                step(2 * i + 1, 1, i)
            for n in range(SG - 3, SG):
                step(n, n % 2, n // 2)

        @block.vector
        def _(dve):
            dve.sem_inc(a_dst_taken, 2)
            left = mem.a_node[:, :, HEADS:2 * HEADS]
            for k in range(PARTS):
                part = parts[:, :, k * HEADS:(k + 1) * HEADS]
                nc.vector.tensor_copy(part, left).then_inc(dve_step, 1)
                dve.wait_ge(dve_step, 2 * k + 1)
                if k < PARTS - 1:
                    nc.vector.tensor_tensor(rest[:, k, :, :], left, part, ALU.subtract).then_inc(dve_step, 1)
                    dve.wait_ge(dve_step, 2 * k + 2)
                    left = rest[:, k, :, :]
            nc.vector.memset(zeros[:, :], 0.0).then_inc(dve_step, 1)

            def mark(b, s, i):
                first, count, before = pairs_loop(dve, mem, b)
                with dve.Fori(0, count) as r:
                    q, t = before + r, tile_of(first, r)
                    dve.wait_ge(dst_in[s], 16 * (i + 1))
                    dve.wait_ge(spread, q + 1)
                    nc.vector.tensor_scalar(member_t[:, bass.ds(pair_slot(q), EB)], dst_row[:, s, :],
                                            col(mem.node_id, t), None, ALU.is_equal).then_inc(marked, 1)

            mark(0, 0, 0)

            def body(b, s, i):
                if last_plus(1, b):
                    mark(b + 1, 1 - s, i + s)
                _, count, before = pairs_loop(dve, mem, b)
                dve.wait_ge(spread, before + count + 2)
                nc.vector.tensor_reduce(AR[:, b * CB:(b + 1) * CB, 1, :] if isinstance(b, int) else AR[:, bass.ds(b * CB, CB), 1, :],
                                        terms[s].rearrange("p c (k h) -> p c h k", k=PARTS), AX.X, ALU.add)\
                    .then_inc(a_dst_taken, 1)
            bodies(dve, body)
            dve.wait_ge(a_dst_taken, NB + 2)
            dve.wait_ge(taken, SG + 2)
            nc.vector.tensor_tensor(AR[:, :, 0, :], AR[:, :, 0, :], AR[:, :, 1, :], ALU.add).then_inc(dve_step, 1)
            dve.wait_ge(dve_step, 2 * PARTS + 1)
            nc.vector.scalar_tensor_tensor(AR[:, :, 0, :], AR[:, :, 0, :], NEG_SLOPE, AR[:, :, 0, :],
                                           op0=ALU.mult, op1=ALU.max).then_inc(dve_step, 1)
            dve.wait_ge(dve_step, 2 * PARTS + 2)

        @block.tensor
        def _(pe):
            pe.sem_inc(spread, 2)
            pe.wait_ge(dve_step, 2 * PARTS)

            def body(b, s, i):
                pe.wait_ge(a_dst_taken, b + 1)
                nc.tensor.matmul(ps[:, s, 0:CB * PT], zeros[:, 0:P], zeros[:, :],
                                 start=True, stop=False, skip_group_check=True)
                first, count, before = pairs_loop(pe, mem, b)
                with pe.Fori(0, count) as r:
                    q, t = before + r, tile_of(first, r)
                    pe.wait_ge(marked, q + 1)
                    for j in range(CB):
                        ins = nc.tensor.matmul(terms[s][:, j, :], member_t[:, bass.ds(pair_slot(q) + j * P, P)],
                                               tile_at(parts, t), start=False, stop=True, skip_group_check=True)
                    ins.then_inc(spread, 1)
            bodies(pe, body)


def phase_run_max(nc, mem, AR, S):
    with ExitStack() as ctx:
        sb = lambda n, s: ctx.enter_context(nc.sbuf_tensor(f"pm_{n}", s, fp32))
        sem = lambda n: ctx.enter_context(nc.semaphore(f"pm_{n}"))
        reset = sb("reset", [P, SG, P])
        slot = sb("slot", [P, 2, 2, SB, HEADS])
        ends = sb("ends", [P, 2])
        chain = sb("chain", [1, 2, HEADS, SB])
        carry_chain = sb("carry_chain", [1, HEADS, SB])
        carry_row = sb("carry_row", [1, P + HEADS])
        carry_part = sb("carry_part", [P, 1])
        carry = sb("carry", [P, 1])
        ps = ctx.enter_context(nc.psum_tensor("pm_ps", [P, 2, 512], fp32))
        ps_c = ctx.enter_context(nc.psum_tensor("pm_psc", [P, 512], fp32))
        loaded = sem("loaded")
        Av = AR[:, :, 0, :].rearrange("e (k g) h -> e g k h", g=SG)
        Rv = AR[:, :, 1, :].rearrange("e (k g) h -> e g k h", g=SG)
        Ev = mem.reset_e[:, :].rearrange("e (k g) -> e g k", g=SG)
        flat = S[:, :, :].rearrange("p g e -> p (g e)")
        flat_reset = reset[:, :, :].rearrange("p g e -> p (g e)")
        packed, turned, out, scanned = sem("packed"), sem("turned"), sem("out"), sem("scanned")
        chained, crossed = sem("chained"), sem("crossed")
        packed_back, turned_back, out_back = sem("packed_back"), sem("turned_back"), sem("out_back")
        SCANNED, CHAINED, CROSSED = 4, 8, 3
        flipped, flip_read = sem("flipped"), sem("flip_read")
        WC = 512 // HEADS
        WIDE = -(-NCH // WC)
        block = ctx.enter_context(nc.Block())

        def steps(eng, do):
            with eng.Fori(0, SG // 2) as i:
                do(2 * i, 0)
                do(2 * i + 1, 1)
            do(SG - 1, 0)

        def group(view, g):
            v = view[:, g:g + 1] if isinstance(g, int) else view[:, bass.ds(g, 1)]
            return v.rearrange("e a k h -> e (a k) h") if len(v.shape) == 4 else v.rearrange("e a k -> e (a k)")


        passes = ((0, True, mem.ident), (1, False, mem.flip))

        @block.sync
        def _(sp):
            resets = mem.reset_flat[0:NCH * P].rearrange("(k e) -> k e", k=SB)
            for k in range(SB):
                sp.dma_start(reset[k * HEADS:(k + 1) * HEADS, :, :].rearrange("h g e -> h (g e)"),
                             resets[k, :].partition_broadcast(HEADS)).then_inc(loaded, 16)

        def at(forward, g):
            return g if forward else ((SG - 1) - g if isinstance(g, int) else (g * -1 + (SG - 1)))

        @block.vector
        def _(dve):
            dve.sem_inc(turned, 2)
            dve.sem_inc(turned_back, 2)
            for n, forward, matrix in passes:
                if n == 1:
                    dve.wait_ge(out_back, SG + 2)

                def pack(g, s):
                    dve.wait_ge(turned, n * SG + g + 1)
                    ins = nc.vector.tensor_copy(slot[:, s, 0, :, :], group(Av if forward else Rv, g))
                    if not forward:
                        ins = nc.vector.tensor_copy(slot[:, s, 1, :, :],
                                                    group(Ev, g).unsqueeze(2).to_broadcast([P, SB, HEADS]))
                    ins.then_inc(packed, 1)
                steps(dve, pack)
                dve.wait_ge(out, (n + 1) * SG + 2)
                if forward:
                    dve.wait_ge(loaded, 16 * SB)
                nc.vector.tensor_tensor_scan(mem.scratch, flat_reset, flat, -BIG, ALU.add, ALU.max).then_inc(scanned, 1)
                nc.vector.tensor_reduce(ends[:, 1:2], flat_reset, AX.X, ALU.min).then_inc(scanned, 1)
                dve.wait_ge(scanned, n * SCANNED + 2)
                nc.vector.tensor_copy(ends[:, 0:1], mem.scratch[:, SG * P - 1:SG * P]).then_inc(scanned, 1)
                dve.wait_ge(crossed, n * CROSSED + 1)
                nc.vector.tensor_copy(chain[:, 0, :, :], ps_c[0:1, 0:P].rearrange("p (k h) -> p h k", h=HEADS)).then_inc(chained, 1)
                nc.vector.tensor_copy(chain[:, 1, :, :], ps_c[0:1, P:2 * P].rearrange("p (k h) -> p h k", h=HEADS)).then_inc(chained, 1)
                dve.wait_ge(chained, n * CHAINED + 2)
                nc.vector.memset(chain[:, 1, :, 0:1], -BIG).then_inc(chained, 1)
                nc.vector.memset(carry_row[:, 0:HEADS], -BIG).then_inc(chained, 1)
                dve.wait_ge(chained, n * CHAINED + 4)
                nc.vector.tensor_tensor_scan(carry_chain[:, :, :].rearrange("p h k -> p (h k)"),
                                             chain[:, 1, :, :].rearrange("p h k -> p (h k)"),
                                             chain[:, 0, :, :].rearrange("p h k -> p (h k)"), -BIG,
                                             ALU.add, ALU.max).then_inc(chained, 1)
                dve.wait_ge(chained, n * CHAINED + 5)
                nc.vector.tensor_copy(carry_row[:, HEADS:HEADS + P].rearrange("p (k h) -> p h k", h=HEADS),
                                      carry_chain[:, :, :]).then_inc(chained, 1)
                dve.wait_ge(crossed, n * CROSSED + 2)
                nc.vector.tensor_copy(carry_part[:, :], ps_c[:, 0:1]).then_inc(chained, 1)
                dve.wait_ge(crossed, n * CROSSED + 3)
                nc.vector.tensor_copy(carry[:, :], ps_c[:, 0:1]).then_inc(chained, 1)
                dve.wait_ge(chained, n * CHAINED + 8)
                nc.vector.tensor_tensor_scan(flat, flat_reset, flat, carry[:, 0:1], ALU.add, ALU.max).then_inc(scanned, 1)
                dve.wait_ge(scanned, n * SCANNED + 4)

                def pack_back(g, s):
                    dve.wait_ge(turned_back, n * SG + g + 1)
                    nc.vector.tensor_copy(slot[:, s, 0, :, :].rearrange("p k h -> p (k h)"),
                                          tile_at(S, at(forward, g))).then_inc(packed_back, 1)
                steps(dve, pack_back)
            for w in range(WIDE):
                dve.wait_ge(flipped, w + 1)
                c0, c1 = w * WC, min((w + 1) * WC, NCH)
                nc.vector.tensor_copy(AR[:, c0:c1, 1, :], ps[:, w % 2, 0:(c1 - c0) * HEADS].rearrange("p (c h) -> p c h", h=HEADS))\
                    .then_inc(flip_read, 1)
            dve.wait_ge(flip_read, WIDE)

        @block.tensor
        def _(pe):
            for n, forward, matrix in passes:
                width = 1 if forward else 2

                def turn(g, s):
                    pe.wait_ge(packed, n * SG + g + 1)
                    pe.wait_ge(out, n * SG + g + 1)
                    for w in range(width):
                        ins = nc.tensor.matmul(ps[:, s, w * P:(w + 1) * P], slot[:, s, w, :, :].rearrange("p k h -> p (k h)"),
                                               matrix[:, :], start=True, stop=True)
                    ins.then_inc(turned, 1)
                steps(pe, turn)
                pe.wait_ge(scanned, n * SCANNED + 3)
                nc.tensor.matmul(ps_c[0:1, 0:P], ends[:, 0:1], matrix[:, :], start=True, stop=True)
                nc.tensor.matmul(ps_c[0:1, P:2 * P], ends[:, 1:2], matrix[:, :], start=True, stop=True).then_inc(crossed, 1)
                pe.wait_ge(chained, n * CHAINED + 6)
                nc.tensor.matmul(ps_c[:, 0:1], carry_row[:, 0:P], mem.ones[0:1, 0:1], start=True, stop=True).then_inc(crossed, 1)
                pe.wait_ge(chained, n * CHAINED + 7)
                nc.tensor.matmul(ps_c[:, 0:1], matrix[:, :], carry_part[:, :], start=True, stop=True).then_inc(crossed, 1)

                def turn_back(g, s):
                    pe.wait_ge(packed_back, n * SG + g + 1)
                    pe.wait_ge(out_back, n * SG + g + 1)
                    nc.tensor.matmul(ps[:, s, 0:P], slot[:, s, 0, :, :].rearrange("p k h -> p (k h)"), mem.ident[:, :],
                                     start=True, stop=True).then_inc(turned_back, 1)
                steps(pe, turn_back)
            for w in range(WIDE):
                if w == 0:
                    pe.wait_ge(out_back, 2 * SG + 2)
                if w >= 2:
                    pe.wait_ge(flip_read, w - 1)
                c0, c1 = w * WC, min((w + 1) * WC, NCH)
                nc.tensor.matmul(ps[:, w % 2, 0:(c1 - c0) * HEADS], mem.flip[:, :], mem.scratch[:, c0 * HEADS:c1 * HEADS],
                                 start=True, stop=True).then_inc(flipped, 1)

        @block.scalar
        def _(act):
            act.sem_inc(out, 2)
            act.sem_inc(out_back, 2)
            for n, forward, matrix in passes:

                def copy_out(g, s):
                    act.wait_ge(turned, n * SG + g + 3)
                    ins = nc.scalar.activation(tile_at(S, at(forward, g)), ps[:, s, 0:P], ACT.Copy)
                    if not forward:
                        ins = nc.scalar.activation(tile_at(reset, at(forward, g)), ps[:, s, P:2 * P], ACT.Copy)
                    ins.then_inc(out, 1)
                steps(act, copy_out)

                def copy_back(g, s):
                    act.wait_ge(turned_back, n * SG + g + 3)
                    view = Rv if forward else mem.scratch[:, :].rearrange("e (k g h) -> e g k h", g=SG, h=HEADS)
                    nc.scalar.activation(group(view, g), ps[:, s, 0:P].rearrange("p (k h) -> p k h", h=HEADS),
                                         ACT.Copy).then_inc(out_back, 1)
                steps(act, copy_back)


def tile_of(first, r):
    return (first + r).with_bounds(min_val=0, max_val=NT - 1)


def bodies(eng, do):
    with eng.Fori(0, NB // 2 - 1) as i:
        do(2 * i, 0, i)
        do(2 * i + 1, 1, i)
    do(NB - 2, 0, NB // 2 - 1)
    do(NB - 1, 1, NB // 2 - 1)


def cols(tensor, at, n):
    return tensor[:, at:at + n] if isinstance(at, int) else tensor[:, bass.ds(at, n)]


def chunks(tensor, at, n):
    return tensor[:, at:at + n, :] if isinstance(at, int) else tensor[:, bass.ds(at, n), :]


def last_plus(n, b):
    return not isinstance(b, int) or b + n < NB


def phase_weights(nc, mem, AR):
    with ExitStack() as ctx:
        sb = lambda n, s, d=fp32: ctx.enter_context(nc.sbuf_tensor(f"nm_{n}", s, d))
        sem = lambda n: ctx.enter_context(nc.semaphore(f"nm_{n}"))
        ROWS = HEADS + 1
        T = sb("T", [P, NT, HEADS])
        spread = sb("spread", [P, ROWS, P])
        rows = sb("rows", [P, ROWS, P])
        inside = sb("inside", [P, P])
        outside = sb("outside", [P, P])
        cand = sb("cand", [P, HEADS, P])
        best = sb("best", [P, HEADS])
        ps = ctx.enter_context(nc.psum_tensor("nm_ps", [P, 3 * 512], fp32))
        ps_n = ctx.enter_context(nc.psum_tensor("nm_psn", [P, 512], fp32))
        spread_ready, turned, step, start = sem("spread_ready"), sem("turned"), sem("step"), sem("start")
        inside_ready, found, added = sem("inside_ready"), sem("found"), sem("added")
        merged, shifted = sem("merged"), sem("shifted")
        block = ctx.enter_context(nc.Block())
        STEPS = 5

        def general(eng, do):
            steps = eng.value_load(mem.general_steps[0:1, 0:1])
            steps = eng.snap((steps & BODIES_FIELD).with_bounds(min_val=0, max_val=NB))
            with eng.If(steps > 0):
                for again in range(2):
                    with eng.Fori(0, steps) as b:
                        do(b, again)

        @block.vector
        def _(dve):
            nc.vector.memset(T[:, :, :], -BIG).then_inc(start, 1)
            dve.wait_ge(start, 1)

            def body(b, again):
                first, count, before = pairs_loop(dve, mem, b)
                for j in range(CB):
                    c = b * CB + j
                    n = c + again * NCH
                    nc.vector.tensor_copy(spread[:, 0:HEADS, :], AR[:, bass.ds(c, 1), 0, :].rearrange("p a h -> p (a h)")
                                          .unsqueeze(2).to_broadcast([P, HEADS, P])).then_inc(spread_ready, 1)
                    nc.vector.tensor_copy(spread[:, HEADS, :], cols(mem.dst_e, c, 1).to_broadcast([P, P]))\
                        .then_inc(spread_ready, 1)
                    dve.wait_ge(turned, n + 1)
                    nc.vector.tensor_copy(rows[:, :, :].rearrange("p r e -> p (r e)"), ps[:, 0:ROWS * P])\
                        .then_inc(start, 1)
                    if again:
                        nc.vector.memset(best[:, :], 0.0).then_inc(start, 1)
                    with dve.Fori(0, count) as r:
                        q, t = before * CB + count * j + r, tile_of(first, r)
                        if not again:
                            dve.wait_ge(start, c + 2)
                            nc.vector.tensor_scalar(inside[:, :], rows[:, HEADS, :], col(mem.node_id, t), None,
                                                    ALU.is_equal).then_inc(step, 1)
                            dve.wait_ge(step, q * STEPS + 1)
                            nc.vector.tensor_scalar(outside[:, :], inside[:, :], BIG, -BIG, ALU.mult, ALU.add).then_inc(step, 1)
                            dve.wait_ge(step, q * STEPS + 2)
                            nc.vector.tensor_tensor(cand[:, :, :], rows[:, 0:HEADS, :],
                                                    outside[:, :].unsqueeze(1).to_broadcast([P, HEADS, P]), ALU.add).then_inc(step, 1)
                            dve.wait_ge(step, q * STEPS + 3)
                            nc.vector.tensor_reduce(best[:, :], cand[:, :, :], AX.X, ALU.max).then_inc(step, 1)
                            dve.wait_ge(step, q * STEPS + 4)
                            nc.vector.tensor_tensor(tile_at(T, t), tile_at(T, t), best[:, :], ALU.max).then_inc(step, 1)
                            dve.wait_ge(step, q * STEPS + 5)
                        else:
                            dve.wait_ge(start, 2 * c + (NCH + 3))
                            nc.vector.tensor_scalar(inside[:, :], rows[:, HEADS, :], col(mem.node_id, t), None,
                                                    ALU.is_equal).then_inc(inside_ready, 1)
                            dve.wait_ge(found, q + 1)
                            nc.vector.tensor_tensor(best[:, :], best[:, :], ps_n[:, 0:HEADS], ALU.add).then_inc(added, 1)
                            dve.wait_ge(added, q + 1)
                    if again:
                        of_edge = AR[:, bass.ds(c, 1), 1, :].rearrange("p a h -> p (a h)")
                        nc.vector.tensor_tensor(of_edge, of_edge, best[:, :], ALU.max).then_inc(merged, 1)
                        dve.wait_ge(merged, c + 1)
            general(dve, body)
            nc.vector.tensor_tensor(AR[:, :, 0, :], AR[:, :, 0, :], AR[:, :, 1, :], ALU.subtract).then_inc(shifted, 1)

        @block.scalar
        def _(act):
            act.wait_ge(shifted, 1)
            nc.scalar.activation(AR[:, :, 0, :], AR[:, :, 0, :], ACT.Exp).then_inc(shifted, 1)
            act.wait_ge(shifted, 2)

        @block.tensor
        def _(pe):
            def body(b, again):
                first, count, before = pairs_loop(pe, mem, b)
                for j in range(CB):
                    c = b * CB + j
                    pe.wait_ge(spread_ready, 2 * c + (2 + again * 2 * NCH))
                    for r in range(ROWS):
                        ins = nc.tensor.matmul(ps[:, r * P:(r + 1) * P], spread[:, r, :], mem.ident[:, :], start=True, stop=True)
                    ins.then_inc(turned, 1)
                    if again:
                        with pe.Fori(0, count) as r:
                            q, t = before * CB + count * j + r, tile_of(first, r)
                            pe.wait_ge(inside_ready, q + 1)
                            nc.tensor.matmul(ps_n[:, 0:HEADS], inside[:, :], tile_at(T, t), start=True, stop=True).then_inc(found, 1)
            general(pe, body)


def phase_attention(nc, mem, AR, acc):
    with ExitStack() as ctx:
        sb = lambda n, s, d=fp32: ctx.enter_context(nc.sbuf_tensor(f"at_{n}", s, d))
        sem = lambda n: ctx.enter_context(nc.semaphore(f"at_{n}"))
        SLOTS = 3
        idx = sb("idx", [P, SLOTS, CB], i32)
        member = [sb(f"member{k}", [P, CB, P]) for k in range(SLOTS + 1)]
        msg = sb("msg", [P, SLOTS, CB, MSG])
        ps = ctx.enter_context(nc.psum_tensor("at_ps", [P, SLOTS + 1, 512], fp32))
        cleared, idx_ready, msg_done, weights_in = sem("cleared"), sem("idx_ready"), sem("msg_done"), sem("weights_in")
        first_ready, first_read = sem("first_ready"), sem("first_read")
        more_ready, more_read = sem("more_ready"), sem("more_read")
        summed, acc_done = sem("summed"), sem("acc_done")
        landed = [sem(f"landed{s}") for s in range(SLOTS)]
        block = ctx.enter_context(nc.Block())

        def bodies(eng, do):
            rounds = (NB - 2) // SLOTS
            with eng.Fori(0, rounds - 1) as i:
                for s in range(SLOTS):
                    do(SLOTS * i + s, s, i)
            for b in range((rounds - 1) * SLOTS, NB):
                do(b, b % SLOTS, b // SLOTS)

        @block.gpsimd
        def _(pool):
            pool.memset(acc[:, :, :], 0.0).then_inc(cleared, 1)

            def gather(b, s, i):
                pool.wait_ge(idx_ready, b + 1)
                pool.sem_inc(mem.tick, 1)
                for j in range(CB):
                    pool.indirect_dma_start(msg[:, s, j, 0:D], None, mem.h_table[:, :],
                                            bass.IndirectOffsetOnAxis(ap=idx[:, s, j:j + 1].bitcast(u32), axis=0))\
                        .then_inc(landed[s], 16)
            bodies(pool, gather)

        @block.vector
        def _(dve):
            dve.sem_inc(first_read, SLOTS)
            dve.sem_inc(more_read, 1)

            def mark(dst, b, t):
                for j in range(CB):
                    ins = nc.vector.tensor_scalar(dst[:, j, :], mem.iota_row[:, :], cols(mem.dst_e, b * CB + j, 1),
                                                  col(mem.neg_base, t), ALU.subtract, ALU.is_equal)
                return ins

            def mark_first(b, s):
                first, _, _ = pairs_loop(dve, mem, b)
                dve.wait_ge(first_read, b + 1)
                mark(member[s], b, first).then_inc(first_ready, 1)

            mark_first(0, 0)

            def body(b, s, i):
                if last_plus(1, b):
                    mark_first(b + 1, (s + 1) % SLOTS)
                dve.wait_ge(landed[s], 16 * CB * (i + 1))
                for h in range(2):
                    at = slice(b * CB + h * HC, b * CB + (h + 1) * HC) if isinstance(b, int) else bass.ds(b * CB + h * HC, HC)
                    values = msg[:, s, h * HC:(h + 1) * HC, 0:D].rearrange("p c (h d) -> p c h d", d=HD)
                    nc.vector.tensor_tensor(values, values, AR[:, at, 0, :].unsqueeze(3).to_broadcast([P, HC, HEADS, HD]),
                                            ALU.mult).then_inc(msg_done, 1)
                first, count, before, further = body_pairs(dve, mem, b)
                with dve.If(count > 1):
                    with dve.Fori(1, count) as r:
                        dve.wait_ge(more_read, further + r)
                        mark(member[SLOTS], b, tile_of(first, r)).then_inc(more_ready, 1)
            bodies(dve, body)

        @block.tensor
        def _(pe):
            pe.wait_ge(cleared, 1)

            def products(which, s, b):
                for j in range(CB):
                    if j % HC == 0:
                        pe.wait_ge(msg_done, 2 * b + (j // HC + 1))
                        if j == 0:
                            pe.wait_ge(weights_in, b + 1)
                    ins = nc.tensor.matmul(ps[:, which, 0:MSG], member[which][:, j, :], msg[:, s, j, :], start=(j == 0), stop=False)
                return ins

            def add_so_far(which, q, t):
                pe.wait_ge(acc_done, q + 1)
                nc.tensor.matmul(ps[:, which, 0:MSG], mem.ident[:, :], tile_at(acc, t), start=False, stop=True).then_inc(summed, 1)

            def body(b, s, i):
                first, count, before, further = body_pairs(pe, mem, b)
                pe.wait_ge(first_ready, b + 1)
                products(s, s, b).then_inc(first_read, 1)
                add_so_far(s, before, first)
                with pe.If(count > 1):
                    with pe.Fori(1, count) as r:
                        pe.wait_ge(more_ready, further + r)
                        pe.wait_ge(acc_done, before + r + 1)
                        products(SLOTS, s, b).then_inc(more_read, 1)
                        add_so_far(SLOTS, before + r, tile_of(first, r))
            bodies(pe, body)

        @block.scalar
        def _(act):
            act.sem_inc(acc_done, 1)

            def prepare(b, s):
                nc.scalar.copy(idx[:, s, :], cols(mem.src_idx, b * CB, CB)).then_inc(idx_ready, 1)
                at = slice(b * CB, (b + 1) * CB) if isinstance(b, int) else bass.ds(b * CB, CB)
                nc.scalar.activation(msg[:, s, :, D:MSG], AR[:, at, 0, :], ACT.Copy).then_inc(weights_in, 1)

            prepare(0, 0)
            prepare(1, 1)
            prepare(2, 2)
            act.wait_ge(cleared, 1)

            def copy_out(which, q, t):
                act.wait_ge(summed, q + 1)
                nc.scalar.activation(tile_at(acc, t), ps[:, which, 0:MSG], ACT.Copy).then_inc(acc_done, 1)

            def body(b, s, i):
                first, count, before = pairs_loop(act, mem, b)
                copy_out(s, before, first)
                with act.If(count > 1):
                    with act.Fori(1, count) as r:
                        copy_out(SLOTS, before + r, tile_of(first, r))
                if last_plus(SLOTS, b):
                    prepare(b + SLOTS, s)
            bodies(act, body)


def phase_attention_out(nc, mem, a, acc):
    UN = 7
    with ExitStack() as ctx:
        sb = lambda n, s: ctx.enter_context(nc.sbuf_tensor(f"ao_{n}", s, fp32))
        sem = lambda n: ctx.enter_context(nc.semaphore(f"ao_{n}"))
        den = sb("den", [P, NT, HEADS])
        bias = sb("bias", [P, D])
        msg = sb("msg", [P, 2, D])
        bias_in, step, scaled, biased, done = sem("bias_in"), sem("step"), sem("scaled"), sem("biased"), sem("done")
        block = ctx.enter_context(nc.Block())

        @block.sync
        def _(sp):
            sp.dma_start(bias[:, :], a["L0_gnn_bias"].partition_broadcast(P)).then_inc(bias_in, 16)

        @block.vector
        def _(dve):
            nc.vector.tensor_scalar(den[:, :, :], acc[:, :, D:MSG], 1e-16, None, ALU.add).then_inc(step, 1)
            dve.wait_ge(step, 1)
            nc.vector.reciprocal(den[:, :, :], den[:, :, :]).then_inc(step, 1)
            dve.wait_ge(step, 2)
            dve.wait_ge(bias_in, 16)
            for t in range(NT):
                s = t % 2
                nc.vector.tensor_tensor(msg[:, s, :].rearrange("p (h d) -> p h d", d=HD),
                                        tile_at(acc, t, D).rearrange("p (h d) -> p h d", d=HD),
                                        den[:, t, :].unsqueeze(2).to_broadcast([P, HEADS, HD]), ALU.mult).then_inc(scaled, 1)
                dve.wait_ge(scaled, t + 1)
                nc.vector.tensor_tensor(msg[:, s, :], msg[:, s, :], bias[:, :], ALU.add).then_inc(biased, 1)
                dve.wait_ge(biased, t + 1)
                nc.vector.scalar_tensor_tensor(tile_at(mem.X, t), msg[:, s, :], 0.0, tile_at(mem.X, t),
                                               op0=ALU.max, op1=ALU.add).then_inc(done, 1)
            dve.wait_ge(done, NT)


def phase_normalize(nc, mem, name, src, dst, bias_ap=None, table=None):
    UN = 7
    with ExitStack() as ctx:
        sb = lambda n, s: ctx.enter_context(nc.sbuf_tensor(f"{name}_{n}", s, fp32))
        sem = lambda n: ctx.enter_context(nc.semaphore(f"{name}_{n}"))
        done = sem("done")
        if table is not None:
            bias = sb("bias", [P, D])
            bias_in, stored = sem("bias_in"), sem("stored")
        block = ctx.enter_context(nc.Block())

        if table is not None:
            @block.sync
            def _(sp):
                sp.dma_start(bias[:, :], bias_ap.partition_broadcast(P)).then_inc(bias_in, 16)
                sp.wait_ge(done, 2 * NT)
                sp.dma_start(table[:, :].rearrange("(t p) f -> p t f", p=P), dst[:, :, 0:D]).then_inc(stored, 16)
                sp.wait_ge(stored, 16)

        @block.vector
        def _(dve):
            with dve.Fori(0, NT // UN) as i:
                for j in range(UN):
                    t = i * UN + j
                    nc.vector.tensor_scalar(tile_at(dst, t, D), tile_at(src, t), col(mem.mean, t), col(mem.rstd, t),
                                            ALU.subtract, ALU.mult).then_inc(done, 1)
            dve.wait_ge(done, NT)
            if table is not None:
                dve.wait_ge(bias_in, 16)
                with dve.Fori(0, NT // UN) as i:
                    for j in range(UN):
                        t = i * UN + j
                        nc.vector.tensor_tensor(tile_at(dst, t, D), tile_at(dst, t, D), bias[:, :], ALU.add).then_inc(done, 1)
                dve.wait_ge(done, 2 * NT)


class Moe:
    pass


def phase_moe(nc, mem, a, m, src, out=None):
    nm = m.name
    NE, L = m.experts, len(m.weights)
    HB = m.hidden // P
    with ExitStack() as ctx:
        sb = lambda n, s, d=fp32: ctx.enter_context(nc.sbuf_tensor(f"{nm}_{n}", s, d))
        pb = lambda n, s: ctx.enter_context(nc.psum_tensor(f"{nm}_{n}", s, fp32))
        sem = lambda n: ctx.enter_context(nc.semaphore(f"{nm}_{n}"))
        Ws, Bs = [], []
        for l in range(L):
            kb = KD if l == 0 else HB
            width = D if l == L - 1 else m.hidden
            Ws.append(sb(f"w{l}", [P, NE, kb, width]))
            Bs.append(sb(f"b{l}", [P, NE, HB]) if l < L - 1 else sb(f"b{l}", [NE, D]))
        rows_in = sb("brows", [NE * HB, (L - 1), P])
        xs = sb("xs", [P, GT, D])
        xTs = [sb(f"xT{s}", [P, KD, GN]) for s in range(2)]
        hT = [sb(f"hT{l}", [P, 2, HB, GN]) for l in range(L - 1)]
        wr = sb("wr", [P, m.router_blocks, NE])
        br = sb("br", [1, NE])
        logit = sb("logit", [P, GT, 8])
        top = sb("top", [P, GT, 8])
        idx = sb("idx", [P, GT, 8], u32)
        idxf = sb("idxf", [P, GT, 2])
        diff = sb("diff", [P, GT])
        ex = sb("ex", [P, GT])
        w12 = sb("w12", [P, GT, 2])
        hot = sb("hot", [P, GT, 2, NE])
        wfs = [sb(f"wf{s}", [P, GT, NE]) for s in range(2)]
        wT = sb("wT", [NE, GN])
        num = sb("num", [P, NE])
        if m.affine:
            gb = sb("gb", [P, 2, KD])
        if m.router_hidden:
            wr1, br1, rh = sb("wr1", [P, KD, P]), sb("br1", [P, 1]), sb("rh", [P, GN])
            peak, total = sb("peak", [P, GT]), sb("total", [P, GT])
        ps_t = pb("pst", [P, KD, GN])
        ps_h = pb("psh", [P, 2, GN])
        ps_y = pb("psy", [P, 2, GN])
        ps_r = pb("psr", [P, GN])
        ps_w = pb("psw", [P, GN])
        w_in, b_turned, ready = sem("w_in"), sem("b_turned"), sem("ready")
        xs_ready, tr_done, xt_ready = sem("xs_ready"), sem("tr_done"), sem("xt_ready")
        hid_done, act_done, y_done, y_taken = sem("hid_done"), sem("act_done"), sem("y_done"), sem("y_taken")
        r_done, rh_ready, r_step, exp_done = sem("r_done"), sem("rh_ready"), sem("r_step"), sem("exp_done")
        wt_done, wt_ready, b_done, stored = sem("wt_done"), sem("wt_ready"), sem("b_done"), sem("stored")
        r_bias = sem("bias_added")
        layers = L - 1
        HPG = NE * layers * HB
        block = ctx.enter_context(nc.Block())

        APPLY, TURN, ROUTE, CHOOSE = 1, 2, 3, 4

        def groups(eng, do):
            tail = NT - NG * GT
            with eng.Fori(0, NG // 2 - 1) as i:
                do(2 * i, 0, GT, GT)
                do(2 * i + 1, 1, GT, GT)
            do(NG - 2, 0, GT, GT)
            do(NG - 1, 1, GT, tail)
            do(NG, 0, tail, 0)

        n_loads = [0]

        @block.sync
        def _(sp):
            def load(dst, src_ap, scattered=False):
                sp.dma_start(dst, src_ap, allow_slow_non_contiguous=scattered).then_inc(w_in, 16)
                n_loads[0] += 1
            load(br[:, :], a[m.router_bias].unsqueeze(0))
            if m.router_hidden:
                load(wr1[:, :, :], a["L1_ffn_router_w1"].rearrange("(k p) h -> p k h", p=P))
                load(br1[:, :], a["L1_ffn_router_b1"].unsqueeze(1), True)
                load(wr[:, 0, :], a[m.router])
            else:
                load(wr[:, :, :], a[m.router].rearrange("(k p) e -> p k e", p=P))
            if m.affine:
                load(gb[:, 0, :], a[m.affine[0]].rearrange("(k p) -> p k", p=P), True)
                load(gb[:, 1, :], a[m.affine[1]].rearrange("(k p) -> p k", p=P), True)
            for l in range(L):
                for e in range(NE):
                    load(Ws[l][:, e, :, :], a[m.weights[l]][e, :, :].rearrange("(k p) n -> p k n", p=P))
                if l < L - 1:
                    load(rows_in[:, l, :], a[m.biases[l]].rearrange("e (b p) -> (e b) p", p=P))
                else:
                    load(Bs[l][:, :], a[m.biases[l]])
            if out is not None:
                def store(g, s, nt, _):
                    if isinstance(g, int) and g < NG:
                        sp.wait_ge(y_taken, (g + 1) * (NE * GT) + 2)
                        sp.dma_start(out[g * GN:(g + 1) * GN, :].rearrange("(t p) f -> p t f", p=P),
                                     mem.X[:, g * GT:(g + 1) * GT, :]).then_inc(stored, 16)
                    elif isinstance(g, int):
                        sp.wait_ge(y_taken, 2 + NG * NE * GT + NE * nt)
                        sp.dma_start(out[FULL_T * P:N, :], mem.X[0:TAIL, FULL_T, :]).then_inc(stored, 16)
                    else:
                        sp.wait_ge(y_taken, (g + 1) * (NE * GT) + 2)
                        sp.dma_start(out[bass.ds(g * GN, GN), :].rearrange("(t p) f -> p t f", p=P),
                                     mem.X[:, bass.ds(g * GT, GT), :]).then_inc(stored, 16)
                groups(sp, store)
                sp.wait_ge(stored, 16 * (NG + 1))

        @block.gpsimd
        def _(pool):
            pool.iota(num[:, :], pattern=[[1, NE]], base=0, channel_multiplier=0,
                      allow_small_or_imprecise_dtypes=True).then_inc(ready, 1)

        @block.vector
        def _(dve):
            dve.sem_inc(y_taken, 2)
            nc.vector.memset(logit[:, :, :], -BIG).then_inc(ready, 1)
            dve.wait_ge(ready, 3)
            STEPS = m.router_steps
            def apply(g, nt):
                if not isinstance(g, int) or g > 0:
                    dve.wait_ge(tr_done, g)
                for j in range(nt):
                    t = g * GT + j
                    nc.vector.tensor_scalar(xs[:, j, :], tile_at(src, t, D), col(mem.mean, t), col(mem.rstd, t),
                                            ALU.subtract, ALU.mult).then_inc(xs_ready, 1)

            def choose(g, s, nt):
                wf = wfs[s]
                n = [0]

                def chain(ins):
                    ins.then_inc(r_step, 1)
                    n[0] += 1
                    dve.wait_ge(r_step, g * STEPS + n[0])

                dve.wait_ge(r_done, g + 1)
                chain(nc.vector.tensor_copy(logit[:, 0:nt, 0:NE], ps_r[:, 0:nt * 8].rearrange("p (t e) -> p t e", e=8)[:, :, 0:NE]))
                if m.router_hidden:
                    chain(nc.vector.tensor_reduce(peak[:, 0:nt], logit[:, 0:nt, 0:NE], AX.X, ALU.max))
                    chain(nc.vector.tensor_tensor(logit[:, 0:nt, 0:NE], logit[:, 0:nt, 0:NE],
                                                  peak[:, 0:nt].unsqueeze(2).to_broadcast([P, nt, NE]), ALU.subtract))
                    dve.wait_ge(exp_done, 2 * g + 1)
                    chain(nc.vector.tensor_reduce(total[:, 0:nt], logit[:, 0:nt, 0:NE], AX.X, ALU.add))
                    chain(nc.vector.reciprocal(total[:, 0:nt], total[:, 0:nt]))
                    chain(nc.vector.tensor_tensor(logit[:, 0:nt, 0:NE], logit[:, 0:nt, 0:NE],
                                                  total[:, 0:nt].unsqueeze(2).to_broadcast([P, nt, NE]), ALU.mult))
                dve.sem_inc(mem.tick, 1)
                for j in range(nt):
                    ins = nc.vector.max(top[:, j, :], logit[:, j, :])
                chain(ins)
                dve.sem_inc(mem.tick, 1)
                for j in range(nt):
                    ins = nc.vector.max_index(idx[:, j, :], top[:, j, :], logit[:, j, :])
                chain(ins)
                chain(nc.vector.tensor_copy(idxf[:, 0:nt, :], idx[:, 0:nt, 0:2]))
                chain(nc.vector.tensor_tensor(diff[:, 0:nt], top[:, 0:nt, 1], top[:, 0:nt, 0], ALU.subtract))
                dve.wait_ge(exp_done, (2 * g + 2) if m.router_hidden else (g + 1))
                chain(nc.vector.tensor_scalar(w12[:, 0:nt, 0], ex[:, 0:nt], 1.0, None, ALU.add))
                chain(nc.vector.reciprocal(w12[:, 0:nt, 0], w12[:, 0:nt, 0]))
                chain(nc.vector.tensor_tensor(w12[:, 0:nt, 1], w12[:, 0:nt, 0], ex[:, 0:nt], ALU.mult))
                for j in range(nt):
                    for w in range(2):
                        ins = nc.vector.tensor_scalar(hot[:, j, w, :], num[:, :], idxf[:, j, w:w + 1], w12[:, j, w:w + 1],
                                                      ALU.is_equal, ALU.mult)
                chain(ins)
                chain(nc.vector.tensor_tensor(wf[:, 0:nt, :], hot[:, 0:nt, 0, :], hot[:, 0:nt, 1, :], ALU.add))
                assert n[0] == STEPS, n[0]

            apply(0, GT)
            choose(0, 0, GT)

            def group(g, s, nt, nt_next):
                wf = wfs[s]
                dve.wait_ge(wt_done, g + 1)
                nc.vector.tensor_copy(wT[:, 0:nt * P], ps_w[0:NE, 0:nt * P]).then_inc(wt_ready, 1)
                for h in range(-(-nt // 2)):
                    w = min(2, nt - 2 * h)
                    dve.wait_ge(b_done, 2 * g + h + 1)
                    t = g * GT + 2 * h
                    nc.vector.tensor_tensor(tiles_at(mem.X, t, w), tiles_at(mem.X, t, w), ps_y[:, h, 0:w * D], ALU.add)\
                        .then_inc(r_bias, 1)
                dve.wait_ge(r_bias, 2 * g + -(-nt // 2))
                for e in range(NE):
                    for j in range(nt):
                        t = g * GT + j
                        at = g * (NE * GT) + e * nt + j
                        dve.wait_ge(y_done, at + 1)
                        if e > 0:
                            dve.wait_ge(y_taken, at - nt + 3)
                        nc.vector.scalar_tensor_tensor(tile_at(mem.X, t), ps_y[:, at_slot(e * nt + j), 0:D], wf[:, j, e:e + 1],
                                                       tile_at(mem.X, t), op0=ALU.mult, op1=ALU.add).then_inc(y_taken, 1)
                    if nt_next and e == APPLY:
                        apply(g + 1, nt_next)
                    if nt_next and e == CHOOSE:
                        choose(g + 1, 1 - s, nt_next)
            groups(dve, group)
            dve.wait_ge(y_taken, 2 + NE * NT)

        @block.tensor
        def _(pe):
            pe.wait_ge(w_in, 16 * n_loads[0])
            for l in range(layers):
                nc.tensor.transpose(ps_r[:, l * NE * HB:(l + 1) * NE * HB], rows_in[:, l, :], mem.ident[0:NE * HB, 0:NE * HB])
            pe.wait_ge(ready, 2)
            nc.tensor.matmul(ps_w[:, 0:1], mem.zeros[:, :], mem.zeros[:, 0:1], start=True, stop=True).then_inc(b_turned, 1)
            pe.wait_ge(ready, 3)

            def turn(g, nt):
                pe.wait_ge(xs_ready, g * GT + nt)
                for k in range(KD):
                    for j in range(nt):
                        ins = nc.tensor.transpose(ps_t[:, k, j * P:(j + 1) * P], xs[:, j, k * P:(k + 1) * P], mem.ident[:, :])
                ins.then_inc(tr_done, 1)

            def route(g, s, nt):
                pe.wait_ge(xt_ready, g + 1)
                if m.router_hidden:
                    for k in range(KD):
                        ins = nc.tensor.matmul(ps_r[:, 0:nt * P], wr1[:, k, :], xTs[s][:, k, 0:nt * P], start=(k == 0), stop=(k == KD - 1))
                    ins.then_inc(rh_ready, 1)

            def logits(g, s, nt):
                if m.router_hidden:
                    pe.wait_ge(rh_ready, 2 * g + 2)
                for j in range(nt):
                    o = ps_r[:, j * 8:j * 8 + NE]
                    nc.tensor.matmul(o, mem.ones[0:1, :], br[:, :], start=True, stop=False)
                    for k in range(m.router_blocks):
                        lhs = rh[:, j * P:(j + 1) * P] if m.router_hidden else xTs[s][:, k, j * P:(j + 1) * P]
                        ins = nc.tensor.matmul(o, lhs, wr[:, k, :], start=False, stop=(k == m.router_blocks - 1))
                ins.then_inc(r_done, 1)

            turn(0, GT)
            route(0, 0, GT)
            logits(0, 0, GT)

            def group(g, s, nt, nt_next):
                w = nt * P
                xT, wf = xTs[s], wfs[s]

                def hidden(e, l):
                    src_t = xT if l == 0 else hT[l - 1][:, e % 2, :, :]
                    kb = KD if l == 0 else HB
                    base = g * HPG + (e * layers + l) * HB
                    if l > 0:
                        pe.wait_ge(act_done, base + 2)
                    for b in range(HB):
                        pe.wait_ge(act_done, base + b + 1)
                        for k in range(kb):
                            ins = nc.tensor.matmul(ps_h[:, (e * layers * HB + l * HB + b) % 2, 0:w], Ws[l][:, e, k, b * P:(b + 1) * P],
                                                   src_t[:, k, 0:w], start=(k == 0), stop=(k == kb - 1))
                        ins.then_inc(hid_done, 1)

                def last(e):
                    base = g * HPG + (e + 1) * layers * HB
                    pe.wait_ge(act_done, base + 2)
                    for j in range(nt):
                        at = g * (NE * GT) + e * nt + j
                        pe.wait_ge(y_taken, at + 1)
                        for k in range(HB):
                            ins = nc.tensor.matmul(ps_y[:, at_slot(e * nt + j), 0:D], hT[layers - 1][:, e % 2, k, j * P:(j + 1) * P],
                                                   Ws[L - 1][:, e, k, :], start=(k == 0), stop=(k == HB - 1))
                        ins.then_inc(y_done, 1)

                hidden(0, 0)
                pe.wait_ge(r_step, (g + 1) * m.router_steps)
                for j in range(nt):
                    ins = nc.tensor.transpose(ps_w[0:NE, j * P:(j + 1) * P], wf[:, j, :], mem.ident[:, :])
                ins.then_inc(wt_done, 1)
                pe.wait_ge(wt_ready, g + 1)
                pe.wait_ge(y_taken, g * (NE * GT) + 2)
                for h in range(-(-nt // 2)):
                    n = min(2, nt - 2 * h)
                    for j in range(n):
                        at = 2 * h + j
                        ins = nc.tensor.matmul(ps_y[:, h, j * D:(j + 1) * D], wT[:, at * P:(at + 1) * P], Bs[L - 1][:, :],
                                               start=True, stop=True)
                    ins.then_inc(b_done, 1)
                pe.wait_ge(r_bias, 2 * g + -(-nt // 2))
                for e in range(NE):
                    for l in range(layers):
                        if (e, l) != (0, 0) and not (l == 0):
                            hidden(e, l)
                    if e + 1 < NE:
                        hidden(e + 1, 0)
                    last(e)
                    if nt_next and e == TURN:
                        turn(g + 1, nt_next)
                    if nt_next and e == ROUTE:
                        route(g + 1, 1 - s, nt_next)
                    if nt_next and e == CHOOSE:
                        logits(g + 1, 1 - s, nt_next)
            groups(pe, group)

        @block.scalar
        def _(act):
            act.sem_inc(act_done, 2)
            act.wait_ge(b_turned, 1)
            for l in range(layers):
                nc.scalar.activation(Bs[l][:, :, :].rearrange("p e b -> p (e b)"), ps_r[:, l * NE * HB:(l + 1) * NE * HB],
                                     ACT.Copy).then_inc(ready, 1) if l == layers - 1 else \
                    nc.scalar.activation(Bs[l][:, :, :].rearrange("p e b -> p (e b)"), ps_r[:, l * NE * HB:(l + 1) * NE * HB], ACT.Copy)
            act.wait_ge(ready, 3)

            def turned(g, s, nt):
                xT, w = xTs[s], nt * P
                act.wait_ge(tr_done, g + 1)
                if m.affine:
                    for k in range(KD):
                        ins = nc.scalar.activation(xT[:, k, 0:w], ps_t[:, k, 0:w], ACT.Identity,
                                                   bias=gb[:, 1, k:k + 1], scale=gb[:, 0, k:k + 1])
                else:
                    ins = nc.scalar.activation(xT[:, :, 0:w], ps_t[:, :, 0:w], ACT.Copy)
                ins.then_inc(xt_ready, 1)

            def routed(g, nt):
                if m.router_hidden:
                    act.wait_ge(rh_ready, 2 * g + 1)
                    nc.scalar.activation(rh[:, 0:nt * P], ps_r[:, 0:nt * P], ACT.Relu, bias=br1[:, 0:1]).then_inc(rh_ready, 1)

            def choose(g, nt):
                if m.router_hidden:
                    act.wait_ge(r_step, g * m.router_steps + 3)
                    nc.scalar.activation(logit[:, 0:nt, 0:NE], logit[:, 0:nt, 0:NE], ACT.Exp).then_inc(exp_done, 1)
                act.wait_ge(r_step, g * m.router_steps + m.diff_step)
                nc.scalar.activation(ex[:, 0:nt], diff[:, 0:nt], ACT.Exp).then_inc(exp_done, 1)

            turned(0, 0, GT)
            routed(0, GT)
            choose(0, GT)

            def group(g, s, nt, nt_next):
                w = nt * P

                def hidden(e, l):
                    base = g * HPG + (e * layers + l) * HB
                    for b in range(HB):
                        act.wait_ge(hid_done, base + b + 1)
                        nc.scalar.activation(hT[l][:, e % 2, b, 0:w], ps_h[:, (e * layers * HB + l * HB + b) % 2, 0:w], m.act,
                                             bias=Bs[l][:, e, b:b + 1]).then_inc(act_done, 1)
                hidden(0, 0)
                for e in range(NE):
                    for l in range(1, layers):
                        hidden(e, l)
                    if e + 1 < NE:
                        hidden(e + 1, 0)
                    if nt_next and e == TURN:
                        turned(g + 1, 1 - s, nt_next)
                    if nt_next and e == ROUTE:
                        routed(g + 1, nt_next)
                    if nt_next and e == CHOOSE:
                        choose(g + 1, nt_next)
            groups(act, group)


def at_slot(n):
    return n % 2


def tiles_at(tensor, t, n):
    ap = tensor[:, t:t + n, :] if isinstance(t, int) else tensor[:, bass.ds(t, n), :]
    return ap.rearrange("p t f -> p (t f)")


def phase_edge_messages(nc, mem, a, acc):
    with ExitStack() as ctx:
        sb = lambda n, s, d=fp32: ctx.enter_context(nc.sbuf_tensor(f"em_{n}", s, d))
        pb = lambda n, s: ctx.enter_context(nc.psum_tensor(f"em_{n}", s, fp32))
        sem = lambda n: ctx.enter_context(nc.semaphore(f"em_{n}"))
        We = sb("We", [P, D])
        idx = sb("idx", [P, 2, CB], i32)
        xrow = sb("xrow", [P, 2, CB, D])
        attr = sb("attr", [P, 2, CB, ED])
        attr_t = sb("attr_t", [P, 2, EB])
        member = [sb(f"member{k}", [P, CB, P]) for k in range(3)]
        msg = sb("msg", [P, 2, CB, D])
        ps_t = pb("pst", [P, 2, HC * P])
        ps_e = [pb(f"pse{s}", [P, HC, D]) for s in range(2)]
        ps_a = pb("psa", [P, 2, 512])
        cleared, w_in, part_in = sem("cleared"), sem("w_in"), sem("part_in")
        idx_ready, tr_done, at_ready, e_done = sem("idx_ready"), sem("tr_done"), sem("at_ready"), sem("e_done")
        add_done, relu_done, first_ready = sem("add_done"), sem("relu_done"), sem("first_ready")
        more_ready, more_read = sem("more_ready"), sem("more_read")
        summed, acc_done = sem("summed"), sem("acc_done")
        landed = [sem(f"landed{s}") for s in range(2)]
        attr_in = [sem(f"attr_in{s}") for s in range(2)]
        block = ctx.enter_context(nc.Block())

        @block.sync
        def _(sp):
            sp.dma_start(We[:, :], a["L1_gnn_W_edge"]).then_inc(w_in, 16)

            def load(b, s, i):
                sp.wait_ge(tr_done, 2 * b + 2)
                if isinstance(b, int) and b == NB - 1:
                    full = LAST_E // P
                    at = b * EB
                    sp.dma_start(attr[0:LAST_E % P, s, full, :], a["edge_attr_128"][at + full * P:E, :]).then_inc(part_in, 16)
                    sp.wait_ge(part_in, 16)
                    sp.dma_start(attr[:, s, 0:full, :], a["edge_attr_128"][at:at + full * P, :]
                                 .rearrange("(c p) f -> p c f", p=P)).then_inc(attr_in[s], 16)
                else:
                    rows = a["edge_attr_128"][b * EB:(b + 1) * EB, :] if isinstance(b, int) else \
                        a["edge_attr_128"][bass.ds(b * EB, EB), :]
                    sp.dma_start(attr[:, s, :, :], rows.rearrange("(c p) f -> p c f", p=P)).then_inc(attr_in[s], 16)
            bodies(sp, load)

        @block.gpsimd
        def _(pool):
            pool.memset(acc[:, :, 0:D], 0.0).then_inc(cleared, 1)

            def gather(b, s, i):
                pool.wait_ge(idx_ready, b + 1)
                pool.sem_inc(mem.tick, 1)
                for j in range(CB):
                    pool.indirect_dma_start(xrow[:, s, j, :], None, mem.xn_table[:, :],
                                            bass.IndirectOffsetOnAxis(ap=idx[:, s, j:j + 1].bitcast(u32), axis=0))\
                        .then_inc(landed[s], 16)
            bodies(pool, gather)

        @block.vector
        def _(dve):
            dve.sem_inc(add_done, 4)

            dve.sem_inc(more_read, 1)

            def mark(dst, b, t):
                for j in range(CB):
                    ins = nc.vector.tensor_scalar(dst[:, j, :], mem.iota_row[:, :], cols(mem.dst_e, b * CB + j, 1),
                                                  col(mem.neg_base, t), ALU.subtract, ALU.is_equal)
                return ins

            def mark_first(b, s):
                first, _, _ = pairs_loop(dve, mem, b)
                dve.wait_ge(e_done, 2 * b + 5)
                mark(member[s], b, first).then_inc(first_ready, 1)

            def body(b, s, i):
                mark_first(b, s)
                dve.wait_ge(landed[s], 16 * CB * (i + 1))
                for h in range(2):
                    half = slice(h * HC, (h + 1) * HC)
                    dve.wait_ge(e_done, 2 * b + (h + 5))
                    nc.vector.tensor_tensor(msg[:, s, half, :], ps_e[h][:, :, :], xrow[:, s, half, :], ALU.add)\
                        .then_inc(add_done, 1)
                first, count, before, further = body_pairs(dve, mem, b)
                with dve.If(count > 1):
                    with dve.Fori(1, count) as r:
                        dve.wait_ge(more_read, further + r)
                        mark(member[2], b, tile_of(first, r)).then_inc(more_ready, 1)
            bodies(dve, body)

        @block.tensor
        def _(pe):
            pe.sem_inc(tr_done, 4)
            pe.sem_inc(e_done, 4)
            pe.wait_ge(w_in, 16)
            pe.wait_ge(cleared, 1)

            def turn(b, s, i):
                pe.wait_ge(attr_in[s], 16 * (i + 1))
                for h in range(2):
                    pe.wait_ge(at_ready, 2 * b + (h + 1))
                    for j in range(HC):
                        ins = nc.tensor.transpose(ps_t[:, h, j * P:(j + 1) * P], attr[:, s, h * HC + j, :], mem.ident[:, :])
                    ins.then_inc(tr_done, 1)

            def edge_linear(b, s):
                for h in range(2):
                    pe.wait_ge(at_ready, 2 * b + (h + 3))
                    pe.wait_ge(add_done, 2 * b + (h + 3))
                    for j in range(HC):
                        c = h * HC + j
                        ins = nc.tensor.matmul(ps_e[h][:, j, :], attr_t[:, s, c * P:(c + 1) * P], We[:, :], start=True, stop=True)
                    ins.then_inc(e_done, 1)

            def products(which, s, b):
                bank = 0 if which < 2 else 1
                for j in range(CB):
                    if j % HC == 0:
                        pe.wait_ge(relu_done, 2 * b + (j // HC + 1))
                    ins = nc.tensor.matmul(ps_a[:, bank, 0:D], member[s if which < 2 else 2][:, j, :], msg[:, s, j, :],
                                           start=(j == 0), stop=False)
                return ins

            def add_so_far(bank, t):
                nc.tensor.matmul(ps_a[:, bank, 0:D], mem.ident[:, :], tile_at(acc, t, D), start=False, stop=True).then_inc(summed, 1)

            turn(0, 0, 0)
            turn(1, 1, 0)
            edge_linear(0, 0)

            def body(b, s, i):
                if last_plus(2, b):
                    turn(b + 2, s, i + 1)
                if last_plus(1, b):
                    edge_linear(b + 1, 1 - s)
                first, count, before, further = body_pairs(pe, mem, b)
                pe.wait_ge(acc_done, before + 1)
                pe.wait_ge(first_ready, b + 1)
                products(0, s, b)
                add_so_far(0, first)
                with pe.If(count > 1):
                    with pe.Fori(1, count) as r:
                        pe.wait_ge(more_ready, further + r)
                        pe.wait_ge(acc_done, before + r)
                        products(2, s, b).then_inc(more_read, 1)
                        pe.wait_ge(acc_done, before + r + 1)
                        add_so_far(1, tile_of(first, r))
            bodies(pe, body)

        @block.scalar
        def _(act):
            act.sem_inc(acc_done, 1)
            act.sem_inc(at_ready, 2)

            def take_index(b, s):
                act.wait_ge(add_done, 2 * b + 2)
                nc.scalar.copy(idx[:, s, :], cols(mem.src_idx, b * CB, CB)).then_inc(idx_ready, 1)

            def take_attr(b, s):
                for h in range(2):
                    act.wait_ge(tr_done, 2 * b + (h + 5))
                    act.wait_ge(e_done, 2 * b + (h + 1))
                    nc.scalar.activation(attr_t[:, s, h * HC * P:(h + 1) * HC * P], ps_t[:, h, :], ACT.Copy)\
                        .then_inc(at_ready, 1)
            def copy_out(bank, q, t):
                act.wait_ge(summed, q + 1)
                nc.scalar.activation(tile_at(acc, t, D), ps_a[:, bank, 0:D], ACT.Copy).then_inc(acc_done, 1)

            take_index(0, 0)
            take_index(1, 1)
            take_attr(0, 0)
            take_attr(1, 1)
            act.wait_ge(cleared, 1)

            def body(b, s, i):
                for h in range(2):
                    half = slice(h * HC, (h + 1) * HC)
                    act.wait_ge(add_done, 2 * b + (h + 5))
                    nc.scalar.activation(msg[:, s, half, :], msg[:, s, half, :], ACT.Relu).then_inc(relu_done, 1)
                if last_plus(2, b):
                    take_index(b + 2, s)
                    take_attr(b + 2, s)
                first, count, before = pairs_loop(act, mem, b)
                copy_out(0, before, first)
                with act.If(count > 1):
                    with act.Fori(1, count) as r:
                        copy_out(1, before + r, tile_of(first, r))
            bodies(act, body)


def phase_node_mlp(nc, mem, a, acc):
    LN_ = (N - NG * GN)
    with ExitStack() as ctx:
        sb = lambda n, s, d=fp32: ctx.enter_context(nc.sbuf_tensor(f"ml_{n}", s, d))
        pb = lambda n, s: ctx.enter_context(nc.psum_tensor(f"ml_{n}", s, fp32))
        sem = lambda n: ctx.enter_context(nc.semaphore(f"ml_{n}"))
        W1, W2 = sb("W1", [P, KD, D]), sb("W2", [P, KD, D])
        vecs = sb("vecs", [P, 4, KD])
        eps1 = sb("eps1", [P, 1])
        xn = sb("xn", [P, 2, D])
        hs = sb("hs", [P, GT, D])
        hT = sb("hT", [P, KD, GN])
        h1 = sb("h1", [P, KD, GN])
        H = sb("H", [P, KD, NT * P])
        stats = sb("stats", [P, KD, NG + 1, 6])
        mv = sb("mv", [P, KD, 2])
        scale, shift, std = sb("scale", [P, KD]), sb("shift", [P, KD]), sb("std", [P, KD])
        yT = sb("yT", [P, 2, KD, GN])
        ps_t = pb("pst", [P, KD, GN])
        ps_h = pb("psh", [P, KD, GN])
        ps_y = pb("psy", [P, 2, 2, 512])
        w_in, xn_done, hs_ready, tr_done = sem("w_in"), sem("xn_done"), sem("hs_ready"), sem("tr_done")
        ht_ready, m_done, h1_ready, h2_ready = sem("ht_ready"), sem("m_done"), sem("h1_ready"), sem("h2_ready")
        seen, step, rooted, scaled = sem("seen"), sem("step"), sem("rooted"), sem("scaled")
        y_ready, y_turned, y_added = sem("y_ready"), sem("y_turned"), sem("y_added")
        block = ctx.enter_context(nc.Block())
        names = ("L1_gnn_b1", "L1_gnn_b2", "L1_gnn_gamma", "L1_gnn_beta")

        @block.sync
        def _(sp):
            sp.dma_start(W1[:, :, :], a["L1_gnn_W1"].rearrange("(k p) n -> p k n", p=P)).then_inc(w_in, 16)
            sp.dma_start(W2[:, :, :], a["L1_gnn_W2"].rearrange("(k p) n -> p k n", p=P)).then_inc(w_in, 16)
            sp.dma_start(eps1[:, :], a["L1_gnn_eps"].partition_broadcast(P)).then_inc(w_in, 16)
            for n, name in enumerate(names):
                sp.dma_start(vecs[:, n, :], a[name].rearrange("(k p) -> p k", p=P), allow_slow_non_contiguous=True).then_inc(w_in, 16)

        @block.vector
        def _(dve):
            dve.sem_inc(hs_ready, 1)
            dve.wait_ge(w_in, 16 * 7)
            nc.vector.tensor_scalar(eps1[:, :], eps1[:, :], 1.0, None, ALU.add).then_inc(step, 1)
            dve.wait_ge(step, 1)

            def group(g, nt):
                dve.wait_ge(tr_done, g + 1)
                for j in range(nt):
                    t = g * GT + j
                    s = j % 2
                    nc.vector.tensor_scalar(xn[:, s, :], tile_at(mem.X, t), col(mem.mean, t), col(mem.rstd, t),
                                            ALU.subtract, ALU.mult).then_inc(xn_done, 1)
                    dve.wait_ge(xn_done, t + 1)
                    nc.vector.scalar_tensor_tensor(hs[:, j, :], xn[:, s, :], eps1[:, 0:1], tile_at(acc, t, D),
                                                   op0=ALU.mult, op1=ALU.add).then_inc(hs_ready, 1)

            def groups_(do):
                with dve.Fori(0, NG) as g:
                    do(g, GT)
                do(NG, NT - NG * GT)
            groups_(group)
            dve.wait_ge(h2_ready, NG + 1)
            for g in range(NG + 1):
                w = GN if g < NG else LN_
                for k in range(KD):
                    nc.vector.bn_stats(stats[:, k, g, :], H[:, k, g * GN:g * GN + w]).then_inc(seen, 1)
            dve.wait_ge(seen, KD * (NG + 1))
            for k in range(KD):
                nc.vector.bn_aggr(mv[:, k, :], stats[:, k, :, :].rearrange("p g s -> p (g s)")).then_inc(step, 1)
            dve.wait_ge(step, 3)
            nc.vector.tensor_scalar(shift[:, :], mv[:, :, 1], EPS, None, ALU.add).then_inc(step, 1)
            dve.wait_ge(rooted, 1)
            nc.vector.reciprocal(scale[:, :], std[:, :]).then_inc(step, 1)
            dve.wait_ge(step, 5)
            nc.vector.tensor_tensor(scale[:, :], scale[:, :], vecs[:, 2, :], ALU.mult).then_inc(step, 1)
            dve.wait_ge(step, 6)
            nc.vector.tensor_tensor(shift[:, :], mv[:, :, 0], scale[:, :], ALU.mult).then_inc(step, 1)
            dve.wait_ge(step, 7)
            nc.vector.tensor_tensor(shift[:, :], vecs[:, 3, :], shift[:, :], ALU.subtract).then_inc(scaled, 1)
            for g in range(NG + 1):
                nt = GT if g < NG else NT - NG * GT
                dve.wait_ge(y_turned, g + 1)
                x4 = mem.X[:, g * GT:g * GT + nt, :].rearrange("p t f -> p (t f)")
                y4 = ps_y[:, g % 2, :, :].rearrange("p b f -> p (b f)")[:, 0:nt * D]
                nc.vector.tensor_tensor(x4, x4, y4, ALU.add).then_inc(y_added, 1)
            dve.wait_ge(y_added, NG + 1)

        @block.tensor
        def _(pe):
            pe.sem_inc(tr_done, 1)
            pe.wait_ge(w_in, 16 * 7)

            def group(g, nt):
                w = nt * P
                pe.wait_ge(hs_ready, g * GT + nt + 1)
                for k in range(KD):
                    for j in range(nt):
                        ins = nc.tensor.transpose(ps_t[:, k, j * P:(j + 1) * P], hs[:, j, k * P:(k + 1) * P], mem.ident[:, :])
                ins.then_inc(tr_done, 1)
                for n, (W, x, ready) in enumerate(((W1, hT, ht_ready), (W2, h1, h1_ready))):
                    pe.wait_ge(ready, g + 1)
                    for b in range(KD):
                        for k in range(KD):
                            ins = nc.tensor.matmul(ps_h[:, b, 0:w], W[:, k, b * P:(b + 1) * P], x[:, k, 0:w],
                                                   start=(k == 0), stop=(k == KD - 1))
                    ins.then_inc(m_done, 1)
            with pe.Fori(0, NG) as g:
                group(g, GT)
            pe_last = group(NG, NT - NG * GT)
            for g in range(NG + 1):
                nt = GT if g < NG else NT - NG * GT
                pe.wait_ge(y_ready, g + 1)
                if g >= 2:
                    pe.wait_ge(y_added, g - 1)
                for j in range(nt):
                    for k in range(KD):
                        ins = nc.tensor.transpose(ps_y[:, g % 2, j // 2, (j % 2) * D + k * P:(j % 2) * D + (k + 1) * P],
                                                  yT[:, g % 2, k, j * P:(j + 1) * P], mem.ident[:, :])
                ins.then_inc(y_turned, 1)

        @block.scalar
        def _(act):
            act.wait_ge(w_in, 16 * 7)

            def group(g, nt):
                w = nt * P
                act.wait_ge(tr_done, g + 2)
                nc.scalar.activation(hT[:, :, 0:w], ps_t[:, :, 0:w], ACT.Copy).then_inc(ht_ready, 1)
                act.wait_ge(m_done, 2 * g + 1)
                for k in range(KD):
                    ins = nc.scalar.activation(h1[:, k, 0:w], ps_h[:, k, 0:w], ACT.Relu, bias=vecs[:, 0, k:k + 1])
                ins.then_inc(h1_ready, 1)
                act.wait_ge(m_done, 2 * g + 2)
                for k in range(KD):
                    o = H[:, k, g * GN:g * GN + w] if isinstance(g, int) else H[:, k, bass.ds(g * GN, w)]
                    ins = nc.scalar.activation(o, ps_h[:, k, 0:w], ACT.Identity, bias=vecs[:, 1, k:k + 1])
                ins.then_inc(h2_ready, 1)
            with act.Fori(0, NG) as g:
                group(g, GT)
            group(NG, NT - NG * GT)
            act.wait_ge(step, 4)
            nc.scalar.activation(std[:, :], shift[:, :], ACT.Sqrt).then_inc(rooted, 1)
            act.wait_ge(scaled, 1)
            for g in range(NG + 1):
                w = GN if g < NG else (NT - NG * GT) * P
                if g >= 2:
                    act.wait_ge(y_turned, g - 1)
                for k in range(KD):
                    ins = nc.scalar.activation(yT[:, g % 2, k, 0:w], H[:, k, g * GN:g * GN + w], ACT.Relu,
                                               bias=shift[:, k:k + 1], scale=scale[:, k:k + 1])
                ins.then_inc(y_ready, 1)


def build(nc, a, out):
    mem = Mem()
    mem.NBP = CQ * BQ
    top = ExitStack()
    with top:
        sb = lambda n, s, d=fp32: top.enter_context(nc.sbuf_tensor(n, s, d))
        mem.tick = top.enter_context(nc.semaphore("tick"))
        mem.rooted = top.enter_context(nc.semaphore("rooted"))
        mem.roots = 0
        dr = lambda n, s, d=fp32: nc.dram_tensor(n, s, d, kind="Internal").ap()
        mem.dst_flat, mem.reset_flat = dr("dst_flat", [NCH * P]), dr("reset_flat", [NCH * P + 1])
        mem.range_flat = dr("range_flat", [2, mem.NBP], i32)
        mem.h_table, mem.as_table, mem.xn_table = dr("h_table", [NT * P, D]), dr("as_table", [NT * P, HEADS]), dr("xn_table", [NT * P, D])
        mem.ident = sb("ident", [P, P])
        mem.flip = sb("flip", [P, P])
        mem.iota_row = sb("iota_row", [P, P])
        mem.node_id = sb("node_id", [P, NT])
        mem.neg_base = sb("neg_base", [P, NT])
        mem.ones = sb("ones", [P, P])
        mem.zeros = sb("zeros", [P, P])
        mem.src_idx = sb("src_idx", [P, NCH], i32)
        mem.dst_e = sb("dst_e", [P, NCH])
        mem.general_steps = sb("general_steps", [1, 1], i32)
        mem.ranges = sb("ranges", [1, mem.NBP], i32)
        mem.mean, mem.rstd = sb("mean", [P, NT]), sb("rstd", [P, NT])
        mem.X = sb("X", [P, NT, D])
        acc = sb("acc", [P, NT, MSG])
        with ExitStack() as inner:
            AR = inner.enter_context(nc.sbuf_tensor("AR", [P, NCH, 2, HEADS], fp32))
            early = inner.enter_context(ExitStack())
            mem.reset_e = early.enter_context(nc.sbuf_tensor("reset_e", [P, NCH], fp32))
            mem.a_node = early.enter_context(nc.sbuf_tensor("a_node", [P, NT, 2 * HEADS], fp32))
            phase_load(nc, mem, a)
            phase_edges(nc, mem, a)
            layernorm_stats(nc, mem, "ln0", mem.X)
            phase_project(nc, mem, a)
            S = acc_as(acc, NCH * HEADS).rearrange("p (g e) -> p g e", e=P)
            mem.scratch = acc[:, :, :].rearrange("p t f -> p (t f)")[:, NCH * HEADS:2 * NCH * HEADS]
            phase_scores(nc, mem, AR)
            phase_run_max(nc, mem, AR, S)
            phase_weights(nc, mem, AR)
            early.close()
            phase_attention(nc, mem, AR, acc)
        phase_attention_out(nc, mem, a, acc)
        layernorm_stats(nc, mem, "ln1", mem.X)
        phase_normalize(nc, mem, "no1", mem.X, acc)
        layernorm_stats(nc, mem, "ln2", acc)
        m = Moe()
        m.name, m.experts, m.hidden, m.act = "m0", 8, 512, ACT.Gelu
        m.weights, m.biases = ("L0_ffn_W1", "L0_ffn_W2"), ("L0_ffn_b1", "L0_ffn_b2")
        m.affine, m.router, m.router_bias, m.router_hidden, m.router_blocks = \
            ("L0_ffn_gamma", "L0_ffn_beta"), "L0_ffn_Wr", "L0_ffn_br", False, KD
        m.router_steps, m.diff_step = 10, 5
        phase_moe(nc, mem, a, m, acc)
        layernorm_stats(nc, mem, "ln3", mem.X)
        phase_normalize(nc, mem, "no3", mem.X, acc, a["L1_gnn_b_edge"], mem.xn_table)
        phase_edge_messages(nc, mem, a, acc)
        phase_node_mlp(nc, mem, a, acc)
        layernorm_stats(nc, mem, "ln4", mem.X)
        m = Moe()
        m.name, m.experts, m.hidden, m.act = "m1", 6, 256, ACT.Relu
        m.weights = ("L1_ffn_expert_w1", "L1_ffn_expert_w2", "L1_ffn_expert_w3")
        m.biases = ("L1_ffn_expert_b1", "L1_ffn_expert_b2", "L1_ffn_expert_b3")
        m.affine, m.router, m.router_bias, m.router_hidden, m.router_blocks = \
            None, "L1_ffn_router_w2", "L1_ffn_router_b2", True, 1
        m.router_steps, m.diff_step = 15, 10
        phase_moe(nc, mem, a, m, mem.X, out)


_OUTS = [((N, D), "float32")]


def kernel(**inputs):
    import numpy as _np
    import concourse.bacc as _bacc
    from concourse import mybir as _mybir
    from concourse.bass_utils import run_bass_kernel_spmd as _run

    nc = _bacc.Bacc("TRN2", target_bir_lowering=False, num_devices=1)
    arrays, args = {}, {}
    for name, value in inputs.items():
        a = _np.ascontiguousarray(value)
        if a.ndim == 0:
            a = a.reshape(1)
        arrays[f"in_{name}_dram"] = a
        args[name] = nc.dram_tensor(f"in_{name}_dram", a.shape, _mybir.dt.from_np(a.dtype), kind="ExternalInput").ap()
    outs = [nc.dram_tensor(f"out_{i}_dram", shape, _mybir.dt.from_np(_np.dtype(dtype)), kind="ExternalOutput").ap()
            for i, (shape, dtype) in enumerate(_OUTS)]
    build(nc, args, outs[0])
    r = _run(nc, [arrays], core_ids=[0])
    return r.results[0]["out_0_dram"]
```

```python
import concourse.bass as bass
from concourse import mybir
from contextlib import ExitStack

fp32 = mybir.dt.float32
bf16 = mybir.dt.bfloat16
i32 = mybir.dt.int32
u32 = mybir.dt.uint32
ALU = mybir.AluOpType
ACT = mybir.ActivationFunctionType
AX = mybir.AxisListType

P = 128
N = 6250
D = 256
KD = D // P
E = 100000
HEADS = 8
HD = D // HEADS
NEG_SLOPE = 0.2
ED = 128
EPS = 1e-5
BIG = 1e30

NT = -(-N // P)
FULL_T = N // P
TAIL = N - FULL_T * P

CB = 8
EB = CB * P
NB = -(-E // EB)
NCH = NB * CB
LAST_E = E - (NB - 1) * EB
CQ = -(-NCH // P)
LAST_ROWS = NCH - (CQ - 1) * P
COUNT_AT, FURTHER_AT = 6, 12
BODIES_FIELD = 255
FIELD, FURTHER_FIELD = 63, (1 << 14) - 1
SB = 16
SG = NCH // SB
HC = CB // 2
BQ = P // CB

GT = 4
NG = NT // GT
GN = GT * P

PARTS = 3
GN_BITS = GN.bit_length() - 1
GROUPS = 2 * NT * P // GN + 8 + 2

MSG = D + HEADS


class Mem:
    pass


def new_semaphore(nc, mem, ctx, name):
    s = ctx.enter_context(nc.semaphore(name))
    mem.used.append(s)
    return s


def gather_semaphore(nc, mem, name):
    return mem.top.enter_context(nc.semaphore(name))


def clear_semaphores(nc, mem):
    with nc.Block() as block:
        @block.gpsimd
        def _(pool):
            for s in mem.used:
                pool.sem_clear(s)
    mem.used = []


def body_pairs(eng, mem, body):
    at = slice(body, body + 1) if isinstance(body, int) else bass.ds(body, 1)
    word = eng.value_load(mem.ranges[0:1, at])
    first = eng.snap((word & FIELD).with_bounds(min_val=0, max_val=NT - 1))
    count = eng.snap(((word >> COUNT_AT) & FIELD).with_bounds(min_val=1, max_val=NT))
    further = eng.snap(((word >> FURTHER_AT) & FURTHER_FIELD).with_bounds(min_val=0, max_val=NB * (NT - 1)))
    before = eng.snap(further + body)
    return first, count, before, further


def pairs_loop(eng, mem, body):
    return body_pairs(eng, mem, body)[0:3]


def phase_load(nc, mem, a):
    with ExitStack() as ctx:
        sem = lambda n: new_semaphore(nc, mem, ctx, n)
        zeroed, made, loaded = sem("ld_zeroed"), sem("ld_made"), sem("ld_loaded")
        block = ctx.enter_context(nc.Block())

        @block.gpsimd
        def _(pool):
            pool.memset(mem.ident[:, :], 1.0).then_inc(made, 1)
            pool.wait_ge(made, 1)
            pool.affine_select(out=mem.ident[:, :], in_=mem.ident[:, :], compare_op=ALU.is_equal, fill=0.0,
                               base=0, pattern=[[-1, P]], channel_multiplier=1).then_inc(made, 1)
            pool.memset(mem.flip[:, :], 1.0).then_inc(made, 1)
            pool.wait_ge(made, 3)
            pool.affine_select(out=mem.flip[:, :], in_=mem.flip[:, :], compare_op=ALU.is_equal, fill=0.0,
                               base=-(P - 1), pattern=[[1, P]], channel_multiplier=1).then_inc(made, 1)
            pool.iota(mem.iota_row[:, :], pattern=[[1, P]], base=0, channel_multiplier=0,
                      allow_small_or_imprecise_dtypes=True).then_inc(made, 1)
            pool.iota(mem.node_id[:, :], pattern=[[P, NT]], base=0, channel_multiplier=1,
                      allow_small_or_imprecise_dtypes=True).then_inc(made, 1)
            pool.iota(mem.neg_base[:, :], pattern=[[-P, NT]], base=0, channel_multiplier=0,
                      allow_small_or_imprecise_dtypes=True).then_inc(made, 1)
            pool.wait_ge(made, 7)

        @block.vector
        def _(dve):
            nc.vector.memset(mem.ones[:, :], 1.0).then_inc(zeroed, 1)
            nc.vector.memset(mem.zeros[:, :], 0.0).then_inc(zeroed, 1)
            nc.vector.memset(mem.X[:, FULL_T, :], 0.0).then_inc(zeroed, 1)
            dve.wait_ge(zeroed, 3)

        @block.sync
        def _(sp):
            sp.dma_start(mem.X[:, 0:FULL_T, :],
                         a["x"][0:FULL_T * P, :].rearrange("(t p) f -> p t f", p=P)).then_inc(loaded, 16)
            sp.wait_ge(zeroed, 3)
            sp.dma_start(mem.X[0:TAIL, FULL_T, :], a["x"][FULL_T * P:N, :]).then_inc(loaded, 16)
            sp.wait_ge(loaded, 32)


def phase_edges(nc, mem, a):
    with ExitStack() as ctx:
        sb = lambda n, s, d=fp32: ctx.enter_context(nc.sbuf_tensor(n, s, d))
        sem = lambda n: new_semaphore(nc, mem, ctx, n)
        raw_src = sb("raw_src", [P, CQ, P], i32)
        raw_dst = sb("raw_dst", [P, CQ, P], i32)
        srcf = sb("srcf", [P, CQ, P])
        raw_next = sb("raw_next", [P, CQ, P], i32)
        dstf = sb("dstf", [P, CQ, P])
        nextf = sb("nextf", [P, CQ, P])
        falls = sb("falls", [P, CQ, P])
        real_next = sb("real_next", [P, CQ, P])
        any_falls = sb("any_falls", [P, 1])
        unsorted = sb("unsorted", [1, 1])
        first_reset = sb("first_reset", [1, 1])
        real_min = sb("real_min", [P, CQ, P])
        reset = sb("reset", [P, CQ, P])
        row_min = sb("row_min", [P, CQ])
        row_max = sb("row_max", [P, CQ])
        mm = sb("mm", [CQ, 2, BQ])
        mm_i = sb("mm_i", [CQ, 2, BQ], i32)
        mm_t = sb("mm_t", [CQ, 2, BQ], i32)
        flat = sb("flat", [1, 2, mem.NBP], i32)
        flat_f = sb("flat_f", [1, 2, mem.NBP])
        counts = sb("counts", [1, mem.NBP])
        plus_one = sb("plus_one", [1, mem.NBP])
        so_far = sb("so_far", [1, mem.NBP])
        packs = sb("packs", [1, 3, mem.NBP], i32)
        ps = ctx.enter_context(nc.psum_tensor("e_ps", [P, 2, 512], fp32))
        ps_m = ctx.enter_context(nc.psum_tensor("e_psm", [P, 2, P], fp32))
        filled, loaded = sem("ed_filled"), sem("ed_loaded")
        step, tr, ev = sem("ed_step"), sem("ed_tr"), sem("ed_ev")
        stored, back, next_step, tr_falls = sem("ed_stored"), sem("ed_back"), sem("ed_next_step"), sem("ed_tr_falls")
        block = ctx.enter_context(nc.Block())

        @block.sync
        def _(sp):
            sp.wait_ge(filled, 3)
            whole = (CQ - 1) * P * P
            rows = (E - whole) // P
            for raw, e in ((raw_src, a["src"]), (raw_dst, a["dst"])):
                sp.dma_start(raw[:, 0:CQ - 1, :],
                             e[0:whole].rearrange("(q p e) -> p q e", p=P, e=P)).then_inc(loaded, 16)
                sp.dma_start(raw[0:rows, CQ - 1, :],
                             e[whole:whole + rows * P].rearrange("(p e) -> p e", e=P)).then_inc(loaded, 16)
                sp.dma_start(raw[rows:rows + 1, CQ - 1, 0:E % P],
                             e[whole + rows * P:E].unsqueeze(0)).then_inc(loaded, 16)
            sp.dma_start(raw_next[:, 0:CQ - 1, :],
                         a["dst"][1:whole + 1].rearrange("(q p e) -> p q e", p=P, e=P)).then_inc(loaded, 16)
            sp.dma_start(raw_next[0:rows, CQ - 1, :],
                         a["dst"][whole + 1:whole + 1 + rows * P].rearrange("(p e) -> p e", e=P)).then_inc(loaded, 16)
            sp.dma_start(raw_next[rows:rows + 1, CQ - 1, 0:E % P - 1],
                         a["dst"][whole + 1 + rows * P:E].unsqueeze(0)).then_inc(loaded, 16)
            sp.wait_ge(step, 6)
            sp.dma_start(mem.reset_flat[0:1].unsqueeze(0), first_reset[:, :]).then_inc(stored, 16)
            for sbt, dr in ((dstf, mem.dst_flat), (reset, mem.reset_flat[1:1 + NCH * P])):
                sp.dma_start(dr[0:whole].rearrange("(q p e) -> p q e", p=P, e=P),
                             sbt[:, 0:CQ - 1, :]).then_inc(stored, 16)
                sp.dma_start(dr[whole:NCH * P].rearrange("(p e) -> p e", e=P),
                             sbt[0:LAST_ROWS, CQ - 1, :]).then_inc(stored, 16)
            sp.wait_ge(step, 8)
            for w in range(2):
                sp.dma_start(mem.range_flat[w, :].rearrange("(q b) -> q b", b=BQ), mm_t[:, w, :]).then_inc(back, 16)
            sp.wait_ge(back, 32)
            sp.dma_start(flat[:, :, :], mem.range_flat[:, :].unsqueeze(0)).then_inc(back, 16)
            sp.wait_ge(stored, 80)

        @block.vector
        def _(dve):
            nc.vector.memset(raw_src[:, :, :], 0).then_inc(filled, 1)
            nc.vector.memset(raw_dst[:, :, :], -1).then_inc(filled, 1)
            nc.vector.memset(raw_next[:, :, :], -1).then_inc(filled, 1)
            nc.vector.memset(first_reset[:, :], -BIG).then_inc(filled, 1)
            dve.wait_ge(loaded, 144)
            nc.vector.tensor_copy(nextf[:, :, :], raw_next[:, :, :]).then_inc(next_step, 1)
            nc.vector.tensor_copy(srcf[:, :, :], raw_src[:, :, :]).then_inc(step, 1)
            nc.vector.tensor_copy(dstf[:, :, :], raw_dst[:, :, :]).then_inc(step, 1)
            dve.wait_ge(step, 2)
            nc.vector.tensor_scalar(real_min[:, :, :], dstf[:, :, :], 0.0, float(NT * P), ALU.is_lt, ALU.mult).then_inc(step, 1)
            nc.vector.tensor_reduce(row_max[:, :], dstf[:, :, :], AX.X, ALU.max).then_inc(step, 1)
            dve.wait_ge(step, 4)
            nc.vector.tensor_tensor(real_min[:, :, :], real_min[:, :, :], dstf[:, :, :], ALU.add).then_inc(step, 1)
            dve.wait_ge(step, 5)
            nc.vector.tensor_reduce(row_min[:, :], real_min[:, :, :], AX.X, ALU.min).then_inc(next_step, 1)
            dve.wait_ge(next_step, 1)
            nc.vector.tensor_tensor(falls[:, :, :], nextf[:, :, :], dstf[:, :, :], ALU.is_lt).then_inc(next_step, 1)
            nc.vector.tensor_scalar(real_next[:, :, :], nextf[:, :, :], 0.0, None, ALU.is_ge).then_inc(next_step, 1)
            nc.vector.tensor_tensor(reset[:, :, :], nextf[:, :, :], dstf[:, :, :], ALU.not_equal).then_inc(next_step, 1)
            dve.wait_ge(next_step, 5)
            nc.vector.tensor_tensor(falls[:, :, :], falls[:, :, :], real_next[:, :, :], ALU.mult).then_inc(next_step, 1)
            nc.vector.tensor_scalar(reset[:, :, :], reset[:, :, :], -BIG, None, ALU.mult).then_inc(step, 1)
            dve.wait_ge(next_step, 6)
            nc.vector.tensor_reduce(any_falls[:, :], falls[:, :, :].rearrange("p q e -> p (q e)"), AX.X, ALU.max).then_inc(next_step, 1)
            dve.wait_ge(tr_falls, 1)
            nc.vector.tensor_reduce(unsorted[:, :], ps_m[0:1, 0, :], AX.X, ALU.max).then_inc(next_step, 1)
            dve.wait_ge(next_step, 8)
            nc.vector.tensor_scalar(mem.general_steps[:, :], unsorted[:, :], float(NB), None, ALU.mult).then_inc(next_step, 1)
            dve.wait_ge(tr, 1)
            for w, op in ((0, ALU.min), (1, ALU.max)):
                ins = nc.vector.tensor_reduce(mm[:, w, :], ps_m[0:CQ, w, :].rearrange("q (b c) -> q b c", c=CB), AX.X, op)
            ins.then_inc(ev, 1)
            dve.wait_ge(ev, 1)
            nc.vector.tensor_copy(mm_i[:, :, :], mm[:, :, :]).then_inc(step, 1)
            dve.wait_ge(step, 7)
            nc.vector.tensor_scalar(mm_t[:, :, :], mm_i[:, :, :], 7, None, ALU.arith_shift_right).then_inc(step, 1)
            n_tr = 1
            for src, dst in ((srcf, mem.src_idx), (dstf, mem.dst_e), (reset, mem.reset_e)):
                for q in range(CQ):
                    w = P if q < CQ - 1 else LAST_ROWS
                    n_tr += 1
                    dve.wait_ge(tr, n_tr)
                    nc.vector.tensor_copy(dst[:, q * P:q * P + w], ps[:, n_tr % 2, 0:w]).then_inc(ev, 1)
            dve.wait_ge(back, 48)
            nc.vector.tensor_copy(flat_f[:, :, :], flat[:, :, :]).then_inc(step, 1)
            dve.wait_ge(step, 9)
            nc.vector.tensor_tensor(counts[:, :], flat_f[:, 1, :], flat_f[:, 0, :], ALU.subtract).then_inc(step, 1)
            dve.wait_ge(step, 10)
            nc.vector.tensor_scalar(plus_one[:, :], counts[:, :], 1.0, None, ALU.add).then_inc(step, 1)
            dve.wait_ge(step, 11)
            nc.vector.tensor_tensor_scan(so_far[:, :], counts[:, :], counts[:, :], 0.0, ALU.add, ALU.bypass).then_inc(step, 1)
            dve.wait_ge(step, 12)
            nc.vector.tensor_copy(packs[:, 1, :], plus_one[:, :]).then_inc(step, 1)
            nc.vector.tensor_tensor(packs[:, 2, :], so_far[:, :], counts[:, :], ALU.subtract).then_inc(step, 1)
            dve.wait_ge(step, 14)
            nc.vector.tensor_scalar(packs[:, 1, :], packs[:, 1, :], COUNT_AT, None, ALU.arith_shift_left).then_inc(step, 1)
            nc.vector.tensor_scalar(packs[:, 2, :], packs[:, 2, :], FURTHER_AT, None, ALU.arith_shift_left).then_inc(step, 1)
            dve.wait_ge(step, 16)
            nc.vector.tensor_tensor(packs[:, 0, :], packs[:, 1, :], packs[:, 2, :], ALU.bitwise_or).then_inc(step, 1)
            dve.wait_ge(step, 17)
            nc.vector.tensor_tensor(mem.ranges[:, :], packs[:, 0, :], flat[:, 0, :], ALU.bitwise_or).then_inc(step, 1)
            dve.wait_ge(step, 18)

        @block.tensor
        def _(pe):
            pe.wait_ge(next_step, 7)
            nc.tensor.transpose(ps_m[0:1, 0, :], any_falls[:, :], mem.ident[:, :]).then_inc(tr_falls, 1)
            pe.wait_ge(next_step, 8)
            nc.tensor.transpose(ps_m[0:CQ, 0, :], row_min[:, :], mem.ident[:, :])
            nc.tensor.transpose(ps_m[0:CQ, 1, :], row_max[:, :], mem.ident[:, :]).then_inc(tr, 1)
            pe.wait_ge(step, 6)
            n_tr = 1
            for src in (srcf, dstf, reset):
                for q in range(CQ):
                    n_tr += 1
                    if n_tr >= 4:
                        pe.wait_ge(ev, n_tr - 2)
                    nc.tensor.transpose(ps[:, n_tr % 2, 0:P], src[:, q, :], mem.ident[:, :]).then_inc(tr, 1)


def layernorm_stats(nc, mem, name, src, first=None):
    with ExitStack() as ctx:
        sb = lambda n, s: ctx.enter_context(nc.sbuf_tensor(f"{name}_{n}", s, fp32))
        sem = lambda n: new_semaphore(nc, mem, ctx, f"{name}_{n}")
        stats = sb("stats", [P, NT, 6])
        total, diff, m2, var = sb("total", [P, NT]), sb("diff", [P, NT]), sb("m2", [P, NT]), sb("var", [P, NT])
        std = sb("std", [P, NT])
        step = sem("step")
        mem.roots += 1
        block = ctx.enter_context(nc.Block())
        UN = 7

        @block.vector
        def _(dve):
            with dve.Fori(0, NT // UN) as i:
                for j in range(UN):
                    nc.vector.bn_stats(stats[:, bass.ds(i * UN + j, 1), :].rearrange("p a s -> p (a s)"),
                                       src[:, bass.ds(i * UN + j, 1), 0:D].rearrange("p a f -> p (a f)")).then_inc(step, 1)
            dve.wait_ge(step, NT)
            nc.vector.tensor_tensor(total[:, :], stats[:, :, 1], stats[:, :, 4], ALU.add).then_inc(step, 1)
            nc.vector.tensor_tensor(diff[:, :], stats[:, :, 1], stats[:, :, 4], ALU.subtract).then_inc(step, 1)
            nc.vector.tensor_tensor(m2[:, :], stats[:, :, 2], stats[:, :, 5], ALU.add).then_inc(step, 1)
            dve.wait_ge(step, NT + 3)
            nc.vector.tensor_scalar(mem.mean[:, :], total[:, :], 0.5, None, ALU.mult).then_inc(step, 1)
            nc.vector.scalar_tensor_tensor(diff[:, :], diff[:, :], 0.25, diff[:, :],
                                           op0=ALU.mult, op1=ALU.mult).then_inc(step, 1)
            dve.wait_ge(step, NT + 5)
            nc.vector.scalar_tensor_tensor(var[:, :], m2[:, :], 1.0 / D, diff[:, :],
                                           op0=ALU.mult, op1=ALU.add).then_inc(step, 1)
            dve.wait_ge(step, NT + 6)
            nc.vector.tensor_scalar(var[:, :], var[:, :], EPS, None, ALU.add).then_inc(step, 1)
            dve.wait_ge(mem.rooted, mem.roots)
            nc.vector.reciprocal(mem.rstd[:, :], std[:, :]).then_inc(step, 1)
            dve.wait_ge(step, NT + 8)

        @block.scalar
        def _(act):
            act.wait_ge(step, NT + 7)
            nc.scalar.activation(std[:, :], var[:, :], ACT.Sqrt).then_inc(mem.rooted, 1)


def phase_project(nc, mem, a):
    WN = D + 2 * HEADS
    with ExitStack() as ctx:
        sb = lambda n, s: ctx.enter_context(nc.sbuf_tensor(f"pj_{n}", s, fp32))
        sem = lambda n: new_semaphore(nc, mem, ctx, f"pj_{n}")
        W = sb("W", [P, KD, WN])
        att = sb("att", [P, 2, D])
        prod = sb("prod", [P, KD, 2, D])
        xs = sb("xs", [P, 2, GT, D])
        xT = sb("xT", [P, KD, GN])
        hs = sb("hs", [P, 2, GT, WN])
        ps_t = ctx.enter_context(nc.psum_tensor("pj_pst", [P, KD, GN], fp32))
        ps_h = ctx.enter_context(nc.psum_tensor("pj_psh", [P, 2, 512], fp32))
        w_in, prods, w_ready = sem("w_in"), sem("prods"), sem("w_ready")
        xs_ready, tr_done, xt_ready = sem("xs_ready"), sem("tr_done"), sem("xt_ready")
        h_done, h_taken, a_taken = sem("h_done"), sem("h_taken"), sem("a_taken")
        h_stored = [sem(f"h_stored{s}") for s in range(2)]
        a_stored, hs_free = sem("a_stored"), sem("hs_free")
        block = ctx.enter_context(nc.Block())

        def groups(eng, do):
            with eng.Fori(0, NG // 2) as i:
                do(2 * i, 0, i, GT)
                do(2 * i + 1, 1, i, GT)
            do(NG, 0, NG // 2, NT - NG * GT)

        @block.sync
        def _(sp):
            sp.dma_start(W[:, :, 0:D], a["L0_gnn_W"].rearrange("(k p) h d -> p k (h d)", p=P)).then_inc(w_in, 16)
            for w, n in enumerate(("L0_gnn_att_src", "L0_gnn_att_dst")):
                sp.dma_start(att[:, w, :], a[n].rearrange("h d -> (h d)").partition_broadcast(P)).then_inc(w_in, 16)

            def store(g, s, i, nt):
                sp.wait_ge(a_taken, g * GT + nt)
                rows = mem.h_table[bass.ds(g * GN, nt * P), :] if not isinstance(g, int) else \
                    mem.h_table[g * GN:g * GN + nt * P, :]
                sp.dma_start(rows.rearrange("(t p) f -> p t f", p=P), hs[:, s, 0:nt, 0:D]).then_inc(h_stored[s], 16)
                sp.wait_ge(h_stored[s], 16 * (i + 1))
                sp.sem_inc(hs_free, 1)
            groups(sp, store)
            sp.wait_ge(a_taken, NT)
            sp.dma_start(mem.as_table[:, :].rearrange("(t p) h -> p t h", p=P),
                         mem.a_node[:, :, 0:HEADS]).then_inc(a_stored, 16)
            sp.wait_ge(a_stored, 16)
            sp.wait_ge(h_stored[0], 16 * (NG // 2 + 1))
            sp.wait_ge(h_stored[1], 16 * (NG // 2))

        @block.vector
        def _(dve):
            dve.wait_ge(w_in, 48)
            for k in range(KD):
                for w in range(2):
                    nc.vector.tensor_tensor(prod[:, k, w, :], W[:, k, 0:D], att[:, w, :], ALU.mult).then_inc(prods, 1)
            dve.wait_ge(prods, 2 * KD)
            for k in range(KD):
                nc.vector.tensor_reduce(W[:, k, D:WN].rearrange("p (w h) -> p w h", w=2),
                                        prod[:, k, :, :].rearrange("p w (h d) -> p w h d", d=HD),
                                        AX.X, ALU.add).then_inc(w_ready, 1)

            def apply(g, s, i, nt):
                dve.wait_ge(tr_done, g + 1)
                for j in range(nt):
                    t = g * GT + j
                    nc.vector.tensor_scalar(xs[:, s, j, :], tile_at(mem.X, t), col(mem.mean, t), col(mem.rstd, t),
                                            ALU.subtract, ALU.mult).then_inc(xs_ready, 1)

            def take(g, s, i, nt):
                for j in range(nt):
                    t = g * GT + j
                    dve.wait_ge(h_taken, t + 3)
                    nc.vector.tensor_copy(tile_at(mem.a_node, t), hs[:, s, j, D:WN]).then_inc(a_taken, 1)
            groups(dve, lambda *g: (apply(*g), take(*g)))

        @block.tensor
        def _(pe):
            pe.sem_inc(tr_done, 2)
            pe.wait_ge(w_ready, KD)

            def group(g, s, i, nt):
                pe.wait_ge(xs_ready, g * GT + nt)
                for k in range(KD):
                    for j in range(nt):
                        ins = nc.tensor.transpose(ps_t[:, k, j * P:(j + 1) * P], xs[:, s, j, k * P:(k + 1) * P],
                                                  mem.ident[:, :])
                ins.then_inc(tr_done, 1)
                pe.wait_ge(xt_ready, g + 1)
                for j in range(nt):
                    t = g * GT + j
                    pe.wait_ge(h_taken, t + 1)
                    for k in range(KD):
                        ins = nc.tensor.matmul(ps_h[:, j % 2, 0:WN], xT[:, k, j * P:(j + 1) * P], W[:, k, :],
                                               start=(k == 0), stop=(k == KD - 1))
                    ins.then_inc(h_done, 1)
            groups(pe, group)

        @block.scalar
        def _(act):
            act.sem_inc(h_taken, 2)
            act.sem_inc(hs_free, 2)


            def group(g, s, i, nt):
                act.wait_ge(tr_done, g + 3)
                ins = nc.scalar.activation(xT[:, :, 0:nt * P], ps_t[:, :, 0:nt * P], ACT.Copy)
                ins.then_inc(xt_ready, 1)
                act.wait_ge(hs_free, g + 1)
                for j in range(nt):
                    t = g * GT + j
                    act.wait_ge(h_done, t + 1)
                    nc.scalar.activation(hs[:, s, j, :], ps_h[:, j % 2, 0:WN], ACT.Copy).then_inc(h_taken, 1)
            groups(act, group)


def tile_at(tensor, t, w=None):
    if isinstance(t, int):
        return tensor[:, t, :] if w is None else tensor[:, t, 0:w]
    ap = tensor[:, bass.ds(t, 1), :] if w is None else tensor[:, bass.ds(t, 1), 0:w]
    return ap.rearrange("p a f -> p (a f)")


def acc_as(acc, n):
    return acc[:, :, :].rearrange("p t f -> p (t f)")[:, 0:n]


def col(tensor, t):
    return tensor[:, t:t + 1] if isinstance(t, int) else tensor[:, bass.ds(t, 1)]


def phase_scores(nc, mem, AR):
    GC = 16
    PT = PARTS * HEADS
    with ExitStack() as ctx:
        sb = lambda n, s, d=fp32: ctx.enter_context(nc.sbuf_tensor(f"gs_{n}", s, d))
        sem = lambda n: new_semaphore(nc, mem, ctx, f"gs_{n}")
        idx = sb("idx", [P, 2, GC], i32)
        rows = sb("rows", [P, 2, GC, HEADS])
        parts = sb("parts", [P, NT, PT], bf16)
        rest = sb("rest", [P, 2, NT, HEADS])
        dst_row = sb("dst_row", [P, 2, EB])
        member_t = sb("member_t", [P, 2 * EB], bf16)
        zeros = sb("zeros", [P, CB * PT], bf16)
        ps = ctx.enter_context(nc.psum_tensor("gs_ps", [P, 2, 512], fp32))
        idx_ready, taken, dve_step, marked = sem("idx_ready"), sem("taken"), sem("dve_step"), sem("marked")
        spread, a_dst_taken = sem("spread"), sem("a_dst_taken")
        landed = [gather_semaphore(nc, mem, "gs_landed" + str(s)) for s in range(2)]
        dst_in = [sem(f"dst_in{s}") for s in range(2)]
        terms = [ps[:, s, 0:CB * PT].rearrange("p (c h) -> p c h", c=CB) for s in range(2)]
        block = ctx.enter_context(nc.Block())

        def steps(eng, do):
            with eng.Fori(0, SG // 2) as i:
                do(2 * i, 0, i)
                do(2 * i + 1, 1, i)
            do(SG - 1, 0, SG // 2)

        def pair_slot(q):
            return (q & 1) * EB

        @block.sync
        def _(sp):
            def load(b, s, i):
                sp.wait_ge(a_dst_taken, b + 1)
                row = mem.dst_flat[b * EB:(b + 1) * EB] if isinstance(b, int) else mem.dst_flat[bass.ds(b * EB, EB)]
                sp.dma_start(dst_row[:, s, :], row.partition_broadcast(P)).then_inc(dst_in[s], 16)
            bodies(sp, load)

        @block.gpsimd
        def _(pool):
            def gather(n, s, i):
                pool.wait_ge(idx_ready, n + 1)
                pool.sem_inc(mem.tick, 1)
                for j in range(GC):
                    pool.indirect_dma_start(rows[:, s, j, :], None, mem.as_table[:, :],
                                            bass.IndirectOffsetOnAxis(ap=idx[:, s, j:j + 1].bitcast(u32), axis=0))\
                        .then_inc(landed[s], 16)
            steps(pool, gather)

        @block.scalar
        def _(act):
            act.sem_inc(taken, 2)

            def take_index(n, s):
                act.wait_ge(taken, n + 1)
                nc.scalar.copy(idx[:, s, :], cols(mem.src_idx, n * GC, GC)).then_inc(idx_ready, 1)
            take_index(0, 0)
            take_index(1, 1)

            def step(n, s, i):
                act.wait_ge(landed[s], 16 * GC * (i + 1))
                nc.scalar.activation(AR[:, n * GC:(n + 1) * GC, 0, :] if isinstance(n, int) else AR[:, bass.ds(n * GC, GC), 0, :],
                                     rows[:, s, :, :], ACT.Copy).then_inc(taken, 1)
                if not isinstance(n, int) or n + 2 < SG:
                    take_index(n + 2, s)

            with act.Fori(0, SG // 2 - 1) as i:
                step(2 * i, 0, i)
                step(2 * i + 1, 1, i)
            for n in range(SG - 3, SG):
                step(n, n % 2, n // 2)

        @block.vector
        def _(dve):
            dve.sem_inc(a_dst_taken, 2)
            left = mem.a_node[:, :, HEADS:2 * HEADS]
            for k in range(PARTS):
                part = parts[:, :, k * HEADS:(k + 1) * HEADS]
                nc.vector.tensor_copy(part, left).then_inc(dve_step, 1)
                dve.wait_ge(dve_step, 2 * k + 1)
                if k < PARTS - 1:
                    nc.vector.tensor_tensor(rest[:, k, :, :], left, part, ALU.subtract).then_inc(dve_step, 1)
                    dve.wait_ge(dve_step, 2 * k + 2)
                    left = rest[:, k, :, :]
            nc.vector.memset(zeros[:, :], 0.0).then_inc(dve_step, 1)

            def mark(b, s, i):
                first, count, before = pairs_loop(dve, mem, b)
                with dve.Fori(0, count) as r:
                    q, t = before + r, tile_of(first, r)
                    dve.wait_ge(dst_in[s], 16 * (i + 1))
                    dve.wait_ge(spread, q + 1)
                    nc.vector.tensor_scalar(member_t[:, bass.ds(pair_slot(q), EB)], dst_row[:, s, :],
                                            col(mem.node_id, t), None, ALU.is_equal).then_inc(marked, 1)

            mark(0, 0, 0)

            def body(b, s, i):
                if last_plus(1, b):
                    mark(b + 1, 1 - s, i + s)
                _, count, before = pairs_loop(dve, mem, b)
                dve.wait_ge(spread, before + count + 2)
                nc.vector.tensor_reduce(AR[:, b * CB:(b + 1) * CB, 1, :] if isinstance(b, int) else AR[:, bass.ds(b * CB, CB), 1, :],
                                        terms[s].rearrange("p c (k h) -> p c h k", k=PARTS), AX.X, ALU.add)\
                    .then_inc(a_dst_taken, 1)
            bodies(dve, body)
            dve.wait_ge(a_dst_taken, NB + 2)
            dve.wait_ge(taken, SG + 2)
            nc.vector.tensor_tensor(AR[:, :, 0, :], AR[:, :, 0, :], AR[:, :, 1, :], ALU.add).then_inc(dve_step, 1)
            dve.wait_ge(dve_step, 2 * PARTS + 1)
            nc.vector.scalar_tensor_tensor(AR[:, :, 0, :], AR[:, :, 0, :], NEG_SLOPE, AR[:, :, 0, :],
                                           op0=ALU.mult, op1=ALU.max).then_inc(dve_step, 1)
            dve.wait_ge(dve_step, 2 * PARTS + 2)

        @block.tensor
        def _(pe):
            pe.sem_inc(spread, 2)
            pe.wait_ge(dve_step, 2 * PARTS)

            def body(b, s, i):
                pe.wait_ge(a_dst_taken, b + 1)
                nc.tensor.matmul(ps[:, s, 0:CB * PT], zeros[:, 0:P], zeros[:, :],
                                 start=True, stop=False, skip_group_check=True)
                first, count, before = pairs_loop(pe, mem, b)
                with pe.Fori(0, count) as r:
                    q, t = before + r, tile_of(first, r)
                    pe.wait_ge(marked, q + 1)
                    for j in range(CB):
                        ins = nc.tensor.matmul(terms[s][:, j, :], member_t[:, bass.ds(pair_slot(q) + j * P, P)],
                                               tile_at(parts, t), start=False, stop=True, skip_group_check=True)
                    ins.then_inc(spread, 1)
            bodies(pe, body)


def phase_run_max(nc, mem, AR, S):
    with ExitStack() as ctx:
        sb = lambda n, s: ctx.enter_context(nc.sbuf_tensor(f"pm_{n}", s, fp32))
        sem = lambda n: new_semaphore(nc, mem, ctx, f"pm_{n}")
        reset = sb("reset", [P, SG, P])
        slot = sb("slot", [P, 2, 2, SB, HEADS])
        ends = sb("ends", [P, 2])
        chain = sb("chain", [1, 2, HEADS, SB])
        carry_chain = sb("carry_chain", [1, HEADS, SB])
        carry_row = sb("carry_row", [1, P + HEADS])
        carry_part = sb("carry_part", [P, 1])
        carry = sb("carry", [P, 1])
        ps = ctx.enter_context(nc.psum_tensor("pm_ps", [P, 2, 512], fp32))
        ps_c = ctx.enter_context(nc.psum_tensor("pm_psc", [P, 512], fp32))
        loaded = sem("loaded")
        Av = AR[:, :, 0, :].rearrange("e (k g) h -> e g k h", g=SG)
        Rv = AR[:, :, 1, :].rearrange("e (k g) h -> e g k h", g=SG)
        Ev = mem.reset_e[:, :].rearrange("e (k g) -> e g k", g=SG)
        flat = S[:, :, :].rearrange("p g e -> p (g e)")
        flat_reset = reset[:, :, :].rearrange("p g e -> p (g e)")
        packed, turned, out, scanned = sem("packed"), sem("turned"), sem("out"), sem("scanned")
        chained, crossed = sem("chained"), sem("crossed")
        packed_back, turned_back, out_back = sem("packed_back"), sem("turned_back"), sem("out_back")
        SCANNED, CHAINED, CROSSED = 4, 8, 3
        flipped, flip_read = sem("flipped"), sem("flip_read")
        WC = 512 // HEADS
        WIDE = -(-NCH // WC)
        block = ctx.enter_context(nc.Block())

        def steps(eng, do):
            with eng.Fori(0, SG // 2) as i:
                do(2 * i, 0)
                do(2 * i + 1, 1)
            do(SG - 1, 0)

        def group(view, g):
            v = view[:, g:g + 1] if isinstance(g, int) else view[:, bass.ds(g, 1)]
            return v.rearrange("e a k h -> e (a k) h") if len(v.shape) == 4 else v.rearrange("e a k -> e (a k)")


        passes = ((0, True, mem.ident), (1, False, mem.flip))

        @block.sync
        def _(sp):
            resets = mem.reset_flat[0:NCH * P].rearrange("(k e) -> k e", k=SB)
            for k in range(SB):
                sp.dma_start(reset[k * HEADS:(k + 1) * HEADS, :, :].rearrange("h g e -> h (g e)"),
                             resets[k, :].partition_broadcast(HEADS)).then_inc(loaded, 16)

        def at(forward, g):
            return g if forward else ((SG - 1) - g if isinstance(g, int) else (g * -1 + (SG - 1)))

        @block.vector
        def _(dve):
            dve.sem_inc(turned, 2)
            dve.sem_inc(turned_back, 2)
            for n, forward, matrix in passes:
                if n == 1:
                    dve.wait_ge(out_back, SG + 2)

                def pack(g, s):
                    dve.wait_ge(turned, n * SG + g + 1)
                    ins = nc.vector.tensor_copy(slot[:, s, 0, :, :], group(Av if forward else Rv, g))
                    if not forward:
                        ins = nc.vector.tensor_copy(slot[:, s, 1, :, :],
                                                    group(Ev, g).unsqueeze(2).to_broadcast([P, SB, HEADS]))
                    ins.then_inc(packed, 1)
                steps(dve, pack)
                dve.wait_ge(out, (n + 1) * SG + 2)
                if forward:
                    dve.wait_ge(loaded, 16 * SB)
                nc.vector.tensor_tensor_scan(mem.scratch, flat_reset, flat, -BIG, ALU.add, ALU.max).then_inc(scanned, 1)
                nc.vector.tensor_reduce(ends[:, 1:2], flat_reset, AX.X, ALU.min).then_inc(scanned, 1)
                dve.wait_ge(scanned, n * SCANNED + 2)
                nc.vector.tensor_copy(ends[:, 0:1], mem.scratch[:, SG * P - 1:SG * P]).then_inc(scanned, 1)
                dve.wait_ge(crossed, n * CROSSED + 1)
                nc.vector.tensor_copy(chain[:, 0, :, :], ps_c[0:1, 0:P].rearrange("p (k h) -> p h k", h=HEADS)).then_inc(chained, 1)
                nc.vector.tensor_copy(chain[:, 1, :, :], ps_c[0:1, P:2 * P].rearrange("p (k h) -> p h k", h=HEADS)).then_inc(chained, 1)
                dve.wait_ge(chained, n * CHAINED + 2)
                nc.vector.memset(chain[:, 1, :, 0:1], -BIG).then_inc(chained, 1)
                nc.vector.memset(carry_row[:, 0:HEADS], -BIG).then_inc(chained, 1)
                dve.wait_ge(chained, n * CHAINED + 4)
                nc.vector.tensor_tensor_scan(carry_chain[:, :, :].rearrange("p h k -> p (h k)"),
                                             chain[:, 1, :, :].rearrange("p h k -> p (h k)"),
                                             chain[:, 0, :, :].rearrange("p h k -> p (h k)"), -BIG,
                                             ALU.add, ALU.max).then_inc(chained, 1)
                dve.wait_ge(chained, n * CHAINED + 5)
                nc.vector.tensor_copy(carry_row[:, HEADS:HEADS + P].rearrange("p (k h) -> p h k", h=HEADS),
                                      carry_chain[:, :, :]).then_inc(chained, 1)
                dve.wait_ge(crossed, n * CROSSED + 2)
                nc.vector.tensor_copy(carry_part[:, :], ps_c[:, 0:1]).then_inc(chained, 1)
                dve.wait_ge(crossed, n * CROSSED + 3)
                nc.vector.tensor_copy(carry[:, :], ps_c[:, 0:1]).then_inc(chained, 1)
                dve.wait_ge(chained, n * CHAINED + 8)
                nc.vector.tensor_tensor_scan(flat, flat_reset, flat, carry[:, 0:1], ALU.add, ALU.max).then_inc(scanned, 1)
                dve.wait_ge(scanned, n * SCANNED + 4)

                def pack_back(g, s):
                    dve.wait_ge(turned_back, n * SG + g + 1)
                    nc.vector.tensor_copy(slot[:, s, 0, :, :].rearrange("p k h -> p (k h)"),
                                          tile_at(S, at(forward, g))).then_inc(packed_back, 1)
                steps(dve, pack_back)
            for w in range(WIDE):
                dve.wait_ge(flipped, w + 1)
                c0, c1 = w * WC, min((w + 1) * WC, NCH)
                nc.vector.tensor_copy(AR[:, c0:c1, 1, :], ps[:, w % 2, 0:(c1 - c0) * HEADS].rearrange("p (c h) -> p c h", h=HEADS))\
                    .then_inc(flip_read, 1)
            dve.wait_ge(flip_read, WIDE)

        @block.tensor
        def _(pe):
            for n, forward, matrix in passes:
                width = 1 if forward else 2

                def turn(g, s):
                    pe.wait_ge(packed, n * SG + g + 1)
                    pe.wait_ge(out, n * SG + g + 1)
                    for w in range(width):
                        ins = nc.tensor.matmul(ps[:, s, w * P:(w + 1) * P], slot[:, s, w, :, :].rearrange("p k h -> p (k h)"),
                                               matrix[:, :], start=True, stop=True)
                    ins.then_inc(turned, 1)
                steps(pe, turn)
                pe.wait_ge(scanned, n * SCANNED + 3)
                nc.tensor.matmul(ps_c[0:1, 0:P], ends[:, 0:1], matrix[:, :], start=True, stop=True)
                nc.tensor.matmul(ps_c[0:1, P:2 * P], ends[:, 1:2], matrix[:, :], start=True, stop=True).then_inc(crossed, 1)
                pe.wait_ge(chained, n * CHAINED + 6)
                nc.tensor.matmul(ps_c[:, 0:1], carry_row[:, 0:P], mem.ones[0:1, 0:1], start=True, stop=True).then_inc(crossed, 1)
                pe.wait_ge(chained, n * CHAINED + 7)
                nc.tensor.matmul(ps_c[:, 0:1], matrix[:, :], carry_part[:, :], start=True, stop=True).then_inc(crossed, 1)

                def turn_back(g, s):
                    pe.wait_ge(packed_back, n * SG + g + 1)
                    pe.wait_ge(out_back, n * SG + g + 1)
                    nc.tensor.matmul(ps[:, s, 0:P], slot[:, s, 0, :, :].rearrange("p k h -> p (k h)"), mem.ident[:, :],
                                     start=True, stop=True).then_inc(turned_back, 1)
                steps(pe, turn_back)
            for w in range(WIDE):
                if w == 0:
                    pe.wait_ge(out_back, 2 * SG + 2)
                if w >= 2:
                    pe.wait_ge(flip_read, w - 1)
                c0, c1 = w * WC, min((w + 1) * WC, NCH)
                nc.tensor.matmul(ps[:, w % 2, 0:(c1 - c0) * HEADS], mem.flip[:, :], mem.scratch[:, c0 * HEADS:c1 * HEADS],
                                 start=True, stop=True).then_inc(flipped, 1)

        @block.scalar
        def _(act):
            act.sem_inc(out, 2)
            act.sem_inc(out_back, 2)
            for n, forward, matrix in passes:

                def copy_out(g, s):
                    act.wait_ge(turned, n * SG + g + 3)
                    ins = nc.scalar.activation(tile_at(S, at(forward, g)), ps[:, s, 0:P], ACT.Copy)
                    if not forward:
                        ins = nc.scalar.activation(tile_at(reset, at(forward, g)), ps[:, s, P:2 * P], ACT.Copy)
                    ins.then_inc(out, 1)
                steps(act, copy_out)

                def copy_back(g, s):
                    act.wait_ge(turned_back, n * SG + g + 3)
                    view = Rv if forward else mem.scratch[:, :].rearrange("e (k g h) -> e g k h", g=SG, h=HEADS)
                    nc.scalar.activation(group(view, g), ps[:, s, 0:P].rearrange("p (k h) -> p k h", h=HEADS),
                                         ACT.Copy).then_inc(out_back, 1)
                steps(act, copy_back)


def tile_of(first, r):
    return (first + r).with_bounds(min_val=0, max_val=NT - 1)


def bodies(eng, do):
    with eng.Fori(0, NB // 2 - 1) as i:
        do(2 * i, 0, i)
        do(2 * i + 1, 1, i)
    do(NB - 2, 0, NB // 2 - 1)
    do(NB - 1, 1, NB // 2 - 1)


def cols(tensor, at, n):
    return tensor[:, at:at + n] if isinstance(at, int) else tensor[:, bass.ds(at, n)]


def chunks(tensor, at, n):
    return tensor[:, at:at + n, :] if isinstance(at, int) else tensor[:, bass.ds(at, n), :]


def last_plus(n, b):
    return not isinstance(b, int) or b + n < NB


def phase_weights(nc, mem, AR):
    with ExitStack() as ctx:
        sb = lambda n, s, d=fp32: ctx.enter_context(nc.sbuf_tensor(f"nm_{n}", s, d))
        sem = lambda n: new_semaphore(nc, mem, ctx, f"nm_{n}")
        ROWS = HEADS + 1
        T = sb("T", [P, NT, HEADS])
        spread = sb("spread", [P, ROWS, P])
        rows = sb("rows", [P, ROWS, P])
        inside = sb("inside", [P, P])
        outside = sb("outside", [P, P])
        cand = sb("cand", [P, HEADS, P])
        best = sb("best", [P, HEADS])
        ps = ctx.enter_context(nc.psum_tensor("nm_ps", [P, 3 * 512], fp32))
        ps_n = ctx.enter_context(nc.psum_tensor("nm_psn", [P, 512], fp32))
        spread_ready, turned, step, start = sem("spread_ready"), sem("turned"), sem("step"), sem("start")
        inside_ready, found, added = sem("inside_ready"), sem("found"), sem("added")
        merged, shifted = sem("merged"), sem("shifted")
        block = ctx.enter_context(nc.Block())
        STEPS = 5

        def general(eng, do):
            steps = eng.value_load(mem.general_steps[0:1, 0:1])
            steps = eng.snap((steps & BODIES_FIELD).with_bounds(min_val=0, max_val=NB))
            with eng.If(steps > 0):
                for again in range(2):
                    with eng.Fori(0, steps) as b:
                        do(b, again)

        @block.vector
        def _(dve):
            nc.vector.memset(T[:, :, :], -BIG).then_inc(start, 1)
            dve.wait_ge(start, 1)

            def body(b, again):
                first, count, before = pairs_loop(dve, mem, b)
                for j in range(CB):
                    c = b * CB + j
                    n = c + again * NCH
                    nc.vector.tensor_copy(spread[:, 0:HEADS, :], AR[:, bass.ds(c, 1), 0, :].rearrange("p a h -> p (a h)")
                                          .unsqueeze(2).to_broadcast([P, HEADS, P])).then_inc(spread_ready, 1)
                    nc.vector.tensor_copy(spread[:, HEADS, :], cols(mem.dst_e, c, 1).to_broadcast([P, P]))\
                        .then_inc(spread_ready, 1)
                    dve.wait_ge(turned, n + 1)
                    nc.vector.tensor_copy(rows[:, :, :].rearrange("p r e -> p (r e)"), ps[:, 0:ROWS * P])\
                        .then_inc(start, 1)
                    if again:
                        nc.vector.memset(best[:, :], 0.0).then_inc(start, 1)
                    with dve.Fori(0, count) as r:
                        q, t = before * CB + count * j + r, tile_of(first, r)
                        if not again:
                            dve.wait_ge(start, c + 2)
                            nc.vector.tensor_scalar(inside[:, :], rows[:, HEADS, :], col(mem.node_id, t), None,
                                                    ALU.is_equal).then_inc(step, 1)
                            dve.wait_ge(step, q * STEPS + 1)
                            nc.vector.tensor_scalar(outside[:, :], inside[:, :], BIG, -BIG, ALU.mult, ALU.add).then_inc(step, 1)
                            dve.wait_ge(step, q * STEPS + 2)
                            nc.vector.tensor_tensor(cand[:, :, :], rows[:, 0:HEADS, :],
                                                    outside[:, :].unsqueeze(1).to_broadcast([P, HEADS, P]), ALU.add).then_inc(step, 1)
                            dve.wait_ge(step, q * STEPS + 3)
                            nc.vector.tensor_reduce(best[:, :], cand[:, :, :], AX.X, ALU.max).then_inc(step, 1)
                            dve.wait_ge(step, q * STEPS + 4)
                            nc.vector.tensor_tensor(tile_at(T, t), tile_at(T, t), best[:, :], ALU.max).then_inc(step, 1)
                            dve.wait_ge(step, q * STEPS + 5)
                        else:
                            dve.wait_ge(start, 2 * c + (NCH + 3))
                            nc.vector.tensor_scalar(inside[:, :], rows[:, HEADS, :], col(mem.node_id, t), None,
                                                    ALU.is_equal).then_inc(inside_ready, 1)
                            dve.wait_ge(found, q + 1)
                            nc.vector.tensor_tensor(best[:, :], best[:, :], ps_n[:, 0:HEADS], ALU.add).then_inc(added, 1)
                            dve.wait_ge(added, q + 1)
                    if again:
                        of_edge = AR[:, bass.ds(c, 1), 1, :].rearrange("p a h -> p (a h)")
                        nc.vector.tensor_tensor(of_edge, of_edge, best[:, :], ALU.max).then_inc(merged, 1)
                        dve.wait_ge(merged, c + 1)
            general(dve, body)
            nc.vector.tensor_tensor(AR[:, :, 0, :], AR[:, :, 0, :], AR[:, :, 1, :], ALU.subtract).then_inc(shifted, 1)

        @block.scalar
        def _(act):
            act.wait_ge(shifted, 1)
            nc.scalar.activation(AR[:, :, 0, :], AR[:, :, 0, :], ACT.Exp).then_inc(shifted, 1)
            act.wait_ge(shifted, 2)

        @block.tensor
        def _(pe):
            def body(b, again):
                first, count, before = pairs_loop(pe, mem, b)
                for j in range(CB):
                    c = b * CB + j
                    pe.wait_ge(spread_ready, 2 * c + (2 + again * 2 * NCH))
                    for r in range(ROWS):
                        ins = nc.tensor.matmul(ps[:, r * P:(r + 1) * P], spread[:, r, :], mem.ident[:, :], start=True, stop=True)
                    ins.then_inc(turned, 1)
                    if again:
                        with pe.Fori(0, count) as r:
                            q, t = before * CB + count * j + r, tile_of(first, r)
                            pe.wait_ge(inside_ready, q + 1)
                            nc.tensor.matmul(ps_n[:, 0:HEADS], inside[:, :], tile_at(T, t), start=True, stop=True).then_inc(found, 1)
            general(pe, body)


def phase_attention(nc, mem, AR, acc):
    with ExitStack() as ctx:
        sb = lambda n, s, d=fp32: ctx.enter_context(nc.sbuf_tensor(f"at_{n}", s, d))
        sem = lambda n: new_semaphore(nc, mem, ctx, f"at_{n}")
        SLOTS = 3
        idx = sb("idx", [P, SLOTS, CB], i32)
        member = [sb(f"member{k}", [P, CB, P]) for k in range(SLOTS + 1)]
        msg = sb("msg", [P, SLOTS, CB, MSG])
        ps = ctx.enter_context(nc.psum_tensor("at_ps", [P, SLOTS + 1, 512], fp32))
        cleared, idx_ready, msg_done, weights_in = sem("cleared"), sem("idx_ready"), sem("msg_done"), sem("weights_in")
        first_ready, first_read = sem("first_ready"), sem("first_read")
        more_ready, more_read = sem("more_ready"), sem("more_read")
        summed, acc_done = sem("summed"), sem("acc_done")
        landed = [gather_semaphore(nc, mem, "at_landed" + str(s)) for s in range(SLOTS)]
        block = ctx.enter_context(nc.Block())

        def bodies(eng, do):
            rounds = (NB - 2) // SLOTS
            with eng.Fori(0, rounds - 1) as i:
                for s in range(SLOTS):
                    do(SLOTS * i + s, s, i)
            for b in range((rounds - 1) * SLOTS, NB):
                do(b, b % SLOTS, b // SLOTS)

        @block.gpsimd
        def _(pool):
            pool.memset(acc[:, :, :], 0.0).then_inc(cleared, 1)

            def gather(b, s, i):
                pool.wait_ge(idx_ready, b + 1)
                pool.sem_inc(mem.tick, 1)
                for j in range(CB):
                    pool.indirect_dma_start(msg[:, s, j, 0:D], None, mem.h_table[:, :],
                                            bass.IndirectOffsetOnAxis(ap=idx[:, s, j:j + 1].bitcast(u32), axis=0))\
                        .then_inc(landed[s], 16)
            bodies(pool, gather)

        @block.vector
        def _(dve):
            dve.sem_inc(first_read, SLOTS)
            dve.sem_inc(more_read, 1)

            def mark(dst, b, t):
                for j in range(CB):
                    ins = nc.vector.tensor_scalar(dst[:, j, :], mem.iota_row[:, :], cols(mem.dst_e, b * CB + j, 1),
                                                  col(mem.neg_base, t), ALU.subtract, ALU.is_equal)
                return ins

            def mark_first(b, s):
                first, _, _ = pairs_loop(dve, mem, b)
                dve.wait_ge(first_read, b + 1)
                mark(member[s], b, first).then_inc(first_ready, 1)

            mark_first(0, 0)

            def body(b, s, i):
                if last_plus(1, b):
                    mark_first(b + 1, (s + 1) % SLOTS)
                dve.wait_ge(landed[s], 16 * CB * (i + 1))
                for h in range(2):
                    at = slice(b * CB + h * HC, b * CB + (h + 1) * HC) if isinstance(b, int) else bass.ds(b * CB + h * HC, HC)
                    values = msg[:, s, h * HC:(h + 1) * HC, 0:D].rearrange("p c (h d) -> p c h d", d=HD)
                    nc.vector.tensor_tensor(values, values, AR[:, at, 0, :].unsqueeze(3).to_broadcast([P, HC, HEADS, HD]),
                                            ALU.mult).then_inc(msg_done, 1)
                first, count, before, further = body_pairs(dve, mem, b)
                with dve.If(count > 1):
                    with dve.Fori(1, count) as r:
                        dve.wait_ge(more_read, further + r)
                        mark(member[SLOTS], b, tile_of(first, r)).then_inc(more_ready, 1)
            bodies(dve, body)

        @block.tensor
        def _(pe):
            pe.wait_ge(cleared, 1)

            def products(which, s, b):
                for j in range(CB):
                    if j % HC == 0:
                        pe.wait_ge(msg_done, 2 * b + (j // HC + 1))
                        if j == 0:
                            pe.wait_ge(weights_in, b + 1)
                    ins = nc.tensor.matmul(ps[:, which, 0:MSG], member[which][:, j, :], msg[:, s, j, :], start=(j == 0), stop=False)
                return ins

            def add_so_far(which, q, t):
                pe.wait_ge(acc_done, q + 1)
                nc.tensor.matmul(ps[:, which, 0:MSG], mem.ident[:, :], tile_at(acc, t), start=False, stop=True).then_inc(summed, 1)

            def body(b, s, i):
                first, count, before, further = body_pairs(pe, mem, b)
                pe.wait_ge(first_ready, b + 1)
                products(s, s, b).then_inc(first_read, 1)
                add_so_far(s, before, first)
                with pe.If(count > 1):
                    with pe.Fori(1, count) as r:
                        pe.wait_ge(more_ready, further + r)
                        pe.wait_ge(acc_done, before + r + 1)
                        products(SLOTS, s, b).then_inc(more_read, 1)
                        add_so_far(SLOTS, before + r, tile_of(first, r))
            bodies(pe, body)

        @block.scalar
        def _(act):
            act.sem_inc(acc_done, 1)

            def prepare(b, s):
                nc.scalar.copy(idx[:, s, :], cols(mem.src_idx, b * CB, CB)).then_inc(idx_ready, 1)
                at = slice(b * CB, (b + 1) * CB) if isinstance(b, int) else bass.ds(b * CB, CB)
                nc.scalar.activation(msg[:, s, :, D:MSG], AR[:, at, 0, :], ACT.Copy).then_inc(weights_in, 1)

            prepare(0, 0)
            prepare(1, 1)
            prepare(2, 2)
            act.wait_ge(cleared, 1)

            def copy_out(which, q, t):
                act.wait_ge(summed, q + 1)
                nc.scalar.activation(tile_at(acc, t), ps[:, which, 0:MSG], ACT.Copy).then_inc(acc_done, 1)

            def body(b, s, i):
                first, count, before = pairs_loop(act, mem, b)
                copy_out(s, before, first)
                with act.If(count > 1):
                    with act.Fori(1, count) as r:
                        copy_out(SLOTS, before + r, tile_of(first, r))
                if last_plus(SLOTS, b):
                    prepare(b + SLOTS, s)
            bodies(act, body)


def phase_attention_out(nc, mem, a, acc):
    TC = 7
    with ExitStack() as ctx:
        sb = lambda n, s: ctx.enter_context(nc.sbuf_tensor(f"ao_{n}", s, fp32))
        sem = lambda n: new_semaphore(nc, mem, ctx, f"ao_{n}")
        den = sb("den", [P, NT, HEADS])
        bias = sb("bias", [P, D])
        msg = sb("msg", [P, 2, TC, D])
        bias_in, step, scaled, biased, done = sem("bias_in"), sem("step"), sem("scaled"), sem("biased"), sem("done")
        block = ctx.enter_context(nc.Block())

        @block.sync
        def _(sp):
            sp.dma_start(bias[:, :], a["L0_gnn_bias"].partition_broadcast(P)).then_inc(bias_in, 16)

        @block.vector
        def _(dve):
            nc.vector.tensor_scalar(den[:, :, :], acc[:, :, D:MSG], 1e-16, None, ALU.add).then_inc(step, 1)
            dve.wait_ge(step, 1)
            nc.vector.reciprocal(den[:, :, :], den[:, :, :]).then_inc(step, 1)
            dve.wait_ge(step, 2)
            dve.wait_ge(bias_in, 16)

            def scale(n):
                t = n * TC
                nc.vector.tensor_tensor(msg[:, n % 2, :, :].rearrange("p t (h d) -> p t h d", d=HD),
                                        acc[:, t:t + TC, 0:D].rearrange("p t (h d) -> p t h d", d=HD),
                                        den[:, t:t + TC, :].unsqueeze(3).to_broadcast([P, TC, HEADS, HD]),
                                        ALU.mult).then_inc(scaled, 1)

            scale(0)
            for n in range(NT // TC):
                t = n * TC
                part = msg[:, n % 2, :, :]
                dve.wait_ge(scaled, n + 1)
                nc.vector.tensor_tensor(part, part, bias[:, :].unsqueeze(1).to_broadcast([P, TC, D]), ALU.add).then_inc(biased, 1)
                if n + 1 < NT // TC:
                    if n > 0:
                        dve.wait_ge(done, n)
                    scale(n + 1)
                dve.wait_ge(biased, n + 1)
                nc.vector.scalar_tensor_tensor(mem.X[:, t:t + TC, :], part, 0.0, mem.X[:, t:t + TC, :],
                                               op0=ALU.max, op1=ALU.add).then_inc(done, 1)
            dve.wait_ge(done, NT // TC)


def phase_normalize(nc, mem, name, src, dst, bias_ap=None, table=None):
    UN = 7
    with ExitStack() as ctx:
        sb = lambda n, s: ctx.enter_context(nc.sbuf_tensor(f"{name}_{n}", s, fp32))
        sem = lambda n: new_semaphore(nc, mem, ctx, f"{name}_{n}")
        done = sem("done")
        if table is not None:
            bias = sb("bias", [P, D])
            bias_in, stored = sem("bias_in"), sem("stored")
        block = ctx.enter_context(nc.Block())

        if table is not None:
            @block.sync
            def _(sp):
                sp.dma_start(bias[:, :], bias_ap.partition_broadcast(P)).then_inc(bias_in, 16)
                for t in range(0, NT, UN):
                    sp.wait_ge(done, NT + t + UN)
                    sp.dma_start(table[t * P:(t + UN) * P, :].rearrange("(t p) f -> p t f", p=P),
                                 dst[:, t:t + UN, 0:D]).then_inc(stored, 16)
                sp.wait_ge(stored, 16 * (NT // UN))

        @block.vector
        def _(dve):
            with dve.Fori(0, NT // UN) as i:
                for j in range(UN):
                    t = i * UN + j
                    nc.vector.tensor_scalar(tile_at(dst, t, D), tile_at(src, t), col(mem.mean, t), col(mem.rstd, t),
                                            ALU.subtract, ALU.mult).then_inc(done, 1)
            dve.wait_ge(done, NT)
            if table is not None:
                dve.wait_ge(bias_in, 16)
                with dve.Fori(0, NT // UN) as i:
                    for j in range(UN):
                        t = i * UN + j
                        nc.vector.tensor_tensor(tile_at(dst, t, D), tile_at(dst, t, D), bias[:, :], ALU.add).then_inc(done, 1)
                dve.wait_ge(done, 2 * NT)


class Moe:
    pass


def phase_route(nc, mem, a, m, src):
    NE = m.experts
    with ExitStack() as ctx:
        sb = lambda n, s, d=fp32: ctx.enter_context(nc.sbuf_tensor(f"{m.name}r_{n}", s, d))
        pb = lambda n, s: ctx.enter_context(nc.psum_tensor(f"{m.name}r_{n}", s, fp32))
        sem = lambda n: new_semaphore(nc, mem, ctx, f"{m.name}r_{n}")
        xs = sb("xs", [P, 2, GT, D])
        xT = sb("xT", [P, KD, GN])
        wr = sb("wr", [P, m.router_blocks, NE])
        br = sb("br", [1, NE])
        if m.router_hidden:
            wr1, br1, rh = sb("wr1", [P, KD, P]), sb("br1", [P, 1]), sb("rh", [P, GN])
        full = lambda n, d=fp32: sb(n, [P, NT, NE], d)
        L, L2, same, cand, number, sel, pos_all = (full(n) for n in ("L", "L2", "same", "cand", "number", "sel", "pos_all"))
        hot = [full(f"hot{w}") for w in range(2)]
        top = [sb(f"top{w}", [P, NT]) for w in range(2)]
        low, ex, total = sb("low", [P, NT]), sb("ex", [P, NT]), sb("total", [P, NT])
        before = sb("before", [P, P])
        tiles, so_far = sb("tiles", [P, NE, NT]), sb("so_far", [P, NE, NT])
        counts, counts_i = sb("counts", [P, NE]), sb("counts_i", [P, NE], i32)
        ends, pos_f = sb("ends", [P, NE]), sb("pos_f", [P, NT, 2])
        ps_t = pb("pst", [P, KD, GN])
        ps_rh = pb("psrh", [P, GN])
        ps_l = pb("psl", [P, 512])
        ps_c = pb("psc", [P, 2, 512])
        w_in, made, xs_ready, tr_done, xt_ready = sem("w_in"), sem("made"), sem("xs_ready"), sem("tr_done"), sem("xt_ready")
        rh_done, rh_ready, r_done, xs_free = sem("rh_done"), sem("rh_ready"), sem("r_done"), sem("xs_free")
        step, exp_done, counted = sem("step"), sem("exp_done"), sem("counted")
        stored = [sem(f"stored{s}") for s in range(2)]
        block = ctx.enter_context(nc.Block())

        def groups(eng, do):
            with eng.Fori(0, NG // 2) as i:
                do(2 * i, 0, i, GT)
                do(2 * i + 1, 1, i, GT)
            do(NG, 0, NG // 2, NT - NG * GT)

        @block.sync
        def _(sp):
            sp.dma_start(br[:, :], a[m.router_bias].unsqueeze(0)).then_inc(w_in, 16)
            if m.router_hidden:
                sp.dma_start(wr1[:, :, :], a["L1_ffn_router_w1"].rearrange("(k p) h -> p k h", p=P)).then_inc(w_in, 16)
                sp.dma_start(br1[:, :], a["L1_ffn_router_b1"].unsqueeze(1), allow_slow_non_contiguous=True).then_inc(w_in, 16)
                sp.dma_start(wr[:, 0, :], a[m.router]).then_inc(w_in, 16)
            else:
                sp.dma_start(wr[:, :, :], a[m.router].rearrange("(k p) e -> p k e", p=P)).then_inc(w_in, 16)
            if m.affine:
                for k in range(2):
                    sp.dma_start(m.gb[:, k, :], a[m.affine[k]].rearrange("(k p) -> p k", p=P),
                                 allow_slow_non_contiguous=True).then_inc(w_in, 16)

            def store(g, s, i, nt):
                sp.wait_ge(xs_ready, g * GT + nt)
                rows = mem.xn_table[bass.ds(g * GN, nt * P), :] if not isinstance(g, int) else \
                    mem.xn_table[g * GN:g * GN + nt * P, :]
                sp.dma_start(rows.rearrange("(t p) f -> p t f", p=P), xs[:, s, 0:nt, :]).then_inc(stored[s], 16)
                sp.wait_ge(stored[s], 16 * (i + 1))
                sp.sem_inc(xs_free, 1)
            groups(sp, store)

        @block.gpsimd
        def _(pool):
            pool.iota(number[:, :, :], pattern=[[0, NT], [1, NE]], base=-NE, channel_multiplier=0,
                      allow_small_or_imprecise_dtypes=True).then_inc(made, 1)
            pool.memset(before[:, :], 1.0).then_inc(made, 1)
            pool.wait_ge(made, 2)
            pool.affine_select(out=before[:, :], in_=before[:, :], compare_op=ALU.is_ge, fill=0.0,
                               base=-1, pattern=[[1, P]], channel_multiplier=-1).then_inc(made, 1)

        @block.vector
        def _(dve):
            def apply(g, s, i, nt):
                dve.wait_ge(tr_done, g + 1)
                dve.wait_ge(xs_free, g + 1)
                for j in range(nt):
                    t = g * GT + j
                    nc.vector.tensor_scalar(xs[:, s, j, :], tile_at(src, t, D), col(mem.mean, t), col(mem.rstd, t),
                                            ALU.subtract, ALU.mult).then_inc(xs_ready, 1)
            groups(dve, apply)
            n = [0]

            def chain(ins):
                ins.then_inc(step, 1)
                n[0] += 1
                dve.wait_ge(step, n[0])

            wide = lambda v: v[:, :].unsqueeze(2).to_broadcast([P, NT, NE])
            v = nc.vector
            dve.wait_ge(made, 3)
            dve.wait_ge(r_done, NT)
            chain(v.tensor_copy(L[:, :, :].rearrange("p t e -> p (t e)"), ps_l[:, 0:NT * NE]))
            if m.router_hidden:
                chain(v.tensor_reduce(low[:, :], L[:, :, :], AX.X, ALU.max))
                chain(v.tensor_tensor(L[:, :, :], L[:, :, :], wide(low), ALU.subtract))
                dve.sem_inc(exp_done, 1)
                dve.wait_ge(exp_done, 2)
                chain(v.tensor_reduce(total[:, :], L[:, :, :], AX.X, ALU.add))
                chain(v.reciprocal(total[:, :], total[:, :]))
                chain(v.tensor_tensor(L[:, :, :], L[:, :, :], wide(total), ALU.mult))
            for w, of in enumerate((L, L2)):
                chain(v.tensor_reduce(top[w][:, :], of[:, :, :], AX.X, ALU.max))
                chain(v.tensor_tensor(same[:, :, :], of[:, :, :], wide(top[w]), ALU.is_equal))
                chain(v.tensor_tensor(cand[:, :, :], same[:, :, :], number[:, :, :], ALU.mult))
                chain(v.tensor_reduce(low[:, :], cand[:, :, :], AX.X, ALU.min))
                chain(v.tensor_tensor(hot[w][:, :, :], number[:, :, :], wide(low), ALU.is_equal))
                if w == 0:
                    chain(v.scalar_tensor_tensor(L2[:, :, :], hot[0][:, :, :], -BIG, L[:, :, :], op0=ALU.mult, op1=ALU.add))
            chain(v.tensor_tensor(sel[:, :, :], hot[0][:, :, :], hot[1][:, :, :], ALU.add))
            dve.sem_inc(counted, 1)
            chain(v.tensor_tensor(low[:, :], top[1][:, :], top[0][:, :], ALU.subtract))
            dve.sem_inc(exp_done, 1)
            dve.wait_ge(exp_done, 4 if m.router_hidden else 2)
            chain(v.tensor_scalar(total[:, :], ex[:, :], 1.0, None, ALU.add))
            chain(v.reciprocal(m.w12[:, :, 0], total[:, :]))
            chain(v.tensor_tensor(m.w12[:, :, 1], m.w12[:, :, 0], ex[:, :], ALU.mult))
            dve.wait_ge(counted, 2)
            chain(v.tensor_copy(tiles[:, :, :], ps_c[:, 1, 0:NT * NE].rearrange("p (t e) -> p e t", e=NE)))
            for e in range(NE):
                chain(v.tensor_tensor_scan(so_far[:, e, :], tiles[:, e, :], tiles[:, e, :], 0.0, ALU.add, ALU.bypass))
            chain(v.tensor_scalar(counts[:, :], so_far[:, :, NT - 1], float(GN - 1), None, ALU.add))
            chain(v.tensor_copy(counts_i[:, :], counts[:, :]))
            chain(v.tensor_scalar(counts_i[:, :], counts_i[:, :], GN_BITS, None, ALU.arith_shift_right))
            chain(v.tensor_copy(counts[:, :], counts_i[:, :]))
            chain(v.tensor_scalar(counts[:, :], counts[:, :], 1.0, None, ALU.max))
            chain(v.tensor_tensor_scan(ends[:, :], counts[:, :], counts[:, :], 0.0, ALU.add, ALU.bypass))
            chain(v.tensor_copy(m.plan[:, 0, :], counts[0:1, :]))
            chain(v.tensor_copy(m.plan[:, 2, :], ends[0:1, :]))
            chain(v.tensor_tensor(ends[:, :], ends[:, :], counts[:, :], ALU.subtract))
            chain(v.tensor_copy(m.plan[:, 1, :], ends[0:1, :]))
            chain(v.tensor_scalar(ends[:, :], ends[:, :], float(GN), None, ALU.mult))
            chain(v.tensor_tensor(so_far[:, :, :], so_far[:, :, :], tiles[:, :, :], ALU.subtract))
            chain(v.tensor_tensor(so_far[:, :, :], so_far[:, :, :], ends[:, :].unsqueeze(2).to_broadcast([P, NE, NT]), ALU.add))
            chain(v.tensor_tensor(pos_all[:, :, :], ps_c[:, 0, 0:NT * NE].rearrange("p (t e) -> p t e", e=NE),
                                  so_far[:, :, :].rearrange("p e t -> p t e"), ALU.add))
            for w in range(2):
                chain(v.tensor_tensor(cand[:, :, :], pos_all[:, :, :], hot[w][:, :, :], ALU.mult))
                chain(v.tensor_reduce(pos_f[:, :, w], cand[:, :, :], AX.X, ALU.add))
                chain(v.tensor_copy(m.ids[:, :, w], mem.node_id[:, :]))
            chain(v.tensor_copy(m.pos[:, :, :], pos_f[:, :, :]))

        @block.tensor
        def _(pe):
            pe.sem_inc(tr_done, 2)
            pe.wait_ge(w_in, 16 * m.router_loads)

            def group(g, s, i, nt):
                pe.wait_ge(xs_ready, g * GT + nt)
                pe.wait_ge(xt_ready, g + 1)
                for k in range(KD):
                    for j in range(nt):
                        ins = nc.tensor.transpose(ps_t[:, k, j * P:(j + 1) * P], xs[:, s, j, k * P:(k + 1) * P], mem.ident[:, :])
                ins.then_inc(tr_done, 1)
                pe.wait_ge(xt_ready, g + 2)
                if m.router_hidden:
                    for k in range(KD):
                        ins = nc.tensor.matmul(ps_rh[:, 0:nt * P], wr1[:, k, :], xT[:, k, 0:nt * P], start=(k == 0), stop=(k == KD - 1))
                    ins.then_inc(rh_done, 1)
                    pe.wait_ge(rh_ready, g + 1)
                for j in range(nt):
                    t = g * GT + j
                    o = ps_l[:, t * NE:(t + 1) * NE] if isinstance(g, int) else ps_l[:, bass.ds(t * NE, NE)]
                    nc.tensor.matmul(o, mem.ones[0:1, :], br[:, :], start=True, stop=False)
                    for k in range(m.router_blocks):
                        lhs = rh[:, j * P:(j + 1) * P] if m.router_hidden else xT[:, k, j * P:(j + 1) * P]
                        ins = nc.tensor.matmul(o, lhs, wr[:, k, :], start=False, stop=(k == m.router_blocks - 1))
                    ins.then_inc(r_done, 1)
            groups(pe, group)
            pe.wait_ge(made, 3)
            pe.wait_ge(counted, 1)
            flat = sel[:, :, :].rearrange("p t e -> p (t e)")
            nc.tensor.matmul(ps_c[:, 0, 0:NT * NE], before[:, :], flat, start=True, stop=True)
            nc.tensor.matmul(ps_c[:, 1, 0:NT * NE], mem.ones[:, :], flat, start=True, stop=True).then_inc(counted, 1)

        @block.scalar
        def _(act):
            act.sem_inc(xs_free, 2)
            act.sem_inc(xt_ready, 1)
            act.wait_ge(w_in, 16 * m.router_loads)

            def group(g, s, i, nt):
                act.wait_ge(tr_done, g + 3)
                feature_major(nc, m, xT, ps_t, nt * P).then_inc(xt_ready, 1)
                if m.router_hidden:
                    act.wait_ge(rh_done, g + 1)
                    nc.scalar.activation(rh[:, 0:nt * P], ps_rh[:, 0:nt * P], ACT.Relu, bias=br1[:, 0:1]).then_inc(rh_ready, 1)
            groups(act, group)
            if m.router_hidden:
                act.wait_ge(exp_done, 1)
                nc.scalar.activation(L[:, :, :], L[:, :, :], ACT.Exp).then_inc(exp_done, 1)
            act.wait_ge(exp_done, 3 if m.router_hidden else 1)
            nc.scalar.activation(ex[:, :], low[:, :], ACT.Exp).then_inc(exp_done, 1)


def feature_major(nc, m, xT, ps_t, w):
    if not m.affine:
        return nc.scalar.activation(xT[:, :, 0:w], ps_t[:, :, 0:w], ACT.Copy)
    for k in range(KD):
        ins = nc.scalar.activation(xT[:, k, 0:w], ps_t[:, k, 0:w], ACT.Identity,
                                   bias=m.gb[:, 1, k:k + 1], scale=m.gb[:, 0, k:k + 1])
    return ins


def phase_list(nc, mem, m):
    LC = 7
    with ExitStack() as ctx:
        sb = lambda n, s, d=fp32: ctx.enter_context(nc.sbuf_tensor(f"{m.name}l_{n}", s, d))
        sem = lambda n: new_semaphore(nc, mem, ctx, f"{m.name}l_{n}")
        none = sb("none", [P, GROUPS * GT], i32)
        where, what = sb("where", [P, 2, LC], i32), sb("what", [P, 2, LC], i32)
        emptied, ready = sem("emptied"), sem("ready")
        cleared = gather_semaphore(nc, mem, m.name + "l_cleared")
        landed = [gather_semaphore(nc, mem, m.name + "l_landed" + str(s)) for s in range(2)]
        pos = m.pos[:, :, :].rearrange("p t w -> p (t w)")
        ids = m.ids[:, :, :].rearrange("p t w -> p (t w)")
        block = ctx.enter_context(nc.Block())

        @block.gpsimd
        def _(pool):
            pool.memset(none[:, :], 0).then_inc(emptied, 1)
            pool.wait_ge(emptied, 1)
            pool.dma_start(mem.order[:, :].rearrange("(p r) o -> p (r o)", p=P), none[:, :]).then_inc(cleared, 16)
            pool.wait_ge(cleared, 16)
            with pool.Fori(0, 2 * NT // (2 * LC)) as i:
                for s in range(2):
                    pool.wait_ge(ready, 2 * i + (s + 1))
                    pool.sem_inc(mem.tick, 1)
                    for j in range(LC):
                        pool.indirect_dma_start(mem.order[:, :], bass.IndirectOffsetOnAxis(ap=where[:, s, j:j + 1].bitcast(u32), axis=0),
                                                what[:, s, j:j + 1], None).then_inc(landed[s], 16)
            for s in range(2):
                pool.wait_ge(landed[s], 16 * NT)

        @block.vector
        def _(dve):
            def stage(at, s):
                nc.vector.tensor_copy(where[:, s, :], cols(pos, at, LC))
                nc.vector.tensor_copy(what[:, s, :], cols(ids, at, LC)).then_inc(ready, 1)

            for s in range(2):
                stage(s * LC, s)
            with dve.Fori(0, 2 * NT // (2 * LC) - 1) as i:
                for s in range(2):
                    dve.wait_ge(landed[s], i * (16 * LC) + 16 * LC)
                    stage(2 * LC * i + (2 + s) * LC, s)


def phase_experts(nc, mem, a, m):
    NE, LAYERS = m.experts, len(m.weights)
    HB = m.hidden // P
    hiddens = LAYERS - 1
    HPG = hiddens * HB
    with ExitStack() as ctx:
        sb = lambda n, s, d=fp32: ctx.enter_context(nc.sbuf_tensor(f"{m.name}e_{n}", s, d))
        pb = lambda n, s: ctx.enter_context(nc.psum_tensor(f"{m.name}e_{n}", s, fp32))
        sem = lambda n: new_semaphore(nc, mem, ctx, f"{m.name}e_{n}")
        W = [sb(f"w{l}", [P, NE, KD if l == 0 else HB, D if l == hiddens else m.hidden]) for l in range(LAYERS)]
        B = [sb(f"b{l}", [P, NE, HB]) for l in range(hiddens)]
        b_last = sb("b_last", [P, NE, D])
        rows_in = sb("brows", [NE * HB, hiddens, P])
        order = sb("order", [P, GROUPS, GT], i32)
        idx = sb("idx", [P, GT], i32)
        xs = sb("xs", [P, GT, D])
        xT = sb("xT", [P, KD, GN])
        hT = [sb(f"hT{l}", [P, HB, GN]) for l in range(hiddens)]
        y = m.room[:, 0:2 * GT * D].rearrange("p (t f) -> p t f", f=D)
        ps_t = pb("pst", [P, KD, GN])
        ps_h = pb("psh", [P, 2, GN])
        ps_y = pb("psy", [P, 2, 512])
        w_in, b_turned, b_ready, order_in = sem("w_in"), sem("b_turned"), sem("b_ready"), sem("order_in")
        idx_ready, tr_done, xt_ready = sem("idx_ready"), sem("tr_done"), sem("xt_ready")
        landed = gather_semaphore(nc, mem, m.name + "e_landed")
        hid_done, act_done, y_done, y_ready = sem("hid_done"), sem("act_done"), sem("y_done"), sem("y_ready")
        stored, y_free, filled = sem("stored"), sem("y_free"), sem("filled")
        loads = NE * LAYERS + hiddens + 1
        block = ctx.enter_context(nc.Block())

        def number_of(eng, row, e, low):
            word = eng.value_load(m.plan[0:1, row, e:e + 1])
            return eng.snap((word & FIELD).with_bounds(min_val=low, max_val=GROUPS - 2))

        def groups(eng, do):
            for e in range(NE):
                count, first = number_of(eng, 0, e, 1), number_of(eng, 1, e, 0)
                with eng.Fori(0, count) as r:
                    do(e, eng.snap((first + r).with_bounds(min_val=0, max_val=GROUPS - 3)))

        @block.sync
        def _(sp):
            sp.dma_start(order[:, :, :], mem.order[:, :].rearrange("(g p t) o -> p g (t o)", p=P, t=GT)).then_inc(order_in, 16)
            for l in range(hiddens):
                sp.dma_start(rows_in[:, l, :], a[m.biases[l]].rearrange("e (b p) -> (e b) p", p=P)).then_inc(w_in, 16)
            sp.dma_start(b_last[:, :, :].rearrange("p e f -> p (e f)"),
                         a[m.biases[hiddens]].rearrange("e f -> (e f)").partition_broadcast(P)).then_inc(w_in, 16)
            for e in range(NE):
                for l in range(LAYERS):
                    sp.dma_start(W[l][:, e, :, :], a[m.weights[l]][e, :, :].rearrange("(k p) n -> p k n", p=P)).then_inc(w_in, 16)

            total = number_of(sp, 2, NE - 1, 1)
            with sp.Fori(0, GROUPS - total) as r:
                g = (total + r).with_bounds(min_val=0, max_val=GROUPS - 1)
                sp.dma_start(mem.y_table[bass.ds(g * GN, GN), :].rearrange("(p t) f -> p t f", t=GT),
                             mem.X[:, 0:GT, :]).then_inc(filled, 16)
                sp.wait_ge(filled, r * 16 + 16)
                sp.sem_inc(mem.tick, 1)

            def store(e, g):
                sp.wait_ge(y_ready, g * GT + (GT + 2))
                sp.dma_start(mem.y_table[bass.ds(g * GN, GN), :].rearrange("(p t) f -> p t f", t=GT),
                             y[:, bass.ds((g & 1) * GT, GT), :]).then_inc(stored, 16)
                sp.wait_ge(stored, 16 * g + 16)
                sp.sem_inc(y_free, 1)
            groups(sp, store)

        @block.gpsimd
        def _(pool):
            total = number_of(pool, 2, NE - 1, 1)
            with pool.Fori(0, total + 2) as g:
                pool.wait_ge(idx_ready, g + 1)
                pool.sem_inc(mem.tick, 1)
                for j in range(GT):
                    pool.indirect_dma_start(xs[:, j, :], None, mem.xn_table[:, :],
                                            bass.IndirectOffsetOnAxis(ap=idx[:, j:j + 1].bitcast(u32), axis=0))\
                        .then_inc(landed, 16)
            pool.wait_ge(landed, (total + 2) * (16 * GT))

        @block.vector
        def _(dve):
            dve.sem_inc(y_ready, 2)
            dve.sem_inc(y_free, 2)
            dve.wait_ge(w_in, 16 * loads)

            def take(e, g):
                for j in range(GT):
                    dve.wait_ge(y_free, g + 1)
                    dve.wait_ge(y_done, g * GT + (j + 1))
                    nc.vector.tensor_tensor(y[:, bass.ds((g & 1) * GT + j, 1), :].rearrange("p a f -> p (a f)"),
                                            ps_y[:, j % 2, 0:D], b_last[:, e, :], ALU.add).then_inc(y_ready, 1)
            groups(dve, take)

        @block.tensor
        def _(pe):
            pe.wait_ge(w_in, 16 * loads)
            for l in range(hiddens):
                ins = nc.tensor.transpose(ps_t[:, 0, l * NE * HB:(l + 1) * NE * HB], rows_in[:, l, :], mem.ident[0:NE * HB, 0:NE * HB])
            ins.then_inc(b_turned, 1)
            pe.wait_ge(b_ready, hiddens)

            def turn(g):
                pe.wait_ge(landed, g * (16 * GT) + 16 * GT)
                for k in range(KD):
                    for j in range(GT):
                        ins = nc.tensor.transpose(ps_t[:, k, j * P:(j + 1) * P], xs[:, j, k * P:(k + 1) * P], mem.ident[:, :])
                ins.then_inc(tr_done, 1)
            turn(0)

            def group(e, g):
                for l in range(hiddens):
                    src_t, kb = (xT, KD) if l == 0 else (hT[l - 1], HB)
                    if l == 0:
                        pe.wait_ge(xt_ready, g + 1)
                    else:
                        pe.wait_ge(act_done, g * HPG + (l * HB + 2))
                    for b in range(HB):
                        pe.wait_ge(act_done, g * HPG + (l * HB + b + 1))
                        for k in range(kb):
                            ins = nc.tensor.matmul(ps_h[:, (l * HB + b) % 2, :], W[l][:, e, k, b * P:(b + 1) * P],
                                                   src_t[:, k, :], start=(k == 0), stop=(k == kb - 1))
                        ins.then_inc(hid_done, 1)
                    if l == 0:
                        turn(g + 1)
                pe.wait_ge(act_done, g * HPG + (HPG + 2))
                for j in range(GT):
                    pe.wait_ge(y_ready, g * GT + (j + 1))
                    for k in range(HB):
                        ins = nc.tensor.matmul(ps_y[:, j % 2, 0:D], hT[hiddens - 1][:, k, j * P:(j + 1) * P],
                                               W[hiddens][:, e, k, :], start=(k == 0), stop=(k == HB - 1))
                    ins.then_inc(y_done, 1)
            groups(pe, group)

        @block.scalar
        def _(act):
            act.sem_inc(act_done, 2)
            act.wait_ge(b_turned, 1)
            for l in range(hiddens):
                nc.scalar.activation(B[l][:, :, :].rearrange("p e b -> p (e b)"), ps_t[:, 0, l * NE * HB:(l + 1) * NE * HB],
                                     ACT.Copy).then_inc(b_ready, 1)
            act.wait_ge(b_ready, hiddens)
            act.wait_ge(order_in, 16)
            nc.scalar.copy(idx[:, :], order[:, 0, :]).then_inc(idx_ready, 1)

            def turned(g):
                act.wait_ge(tr_done, g + 1)
                feature_major(nc, m, xT, ps_t, GN).then_inc(xt_ready, 1)
                nc.scalar.copy(idx[:, :], order[:, g + 1, :] if isinstance(g, int) else
                               order[:, bass.ds(g + 1, 1), :].rearrange("p a t -> p (a t)")).then_inc(idx_ready, 1)
            turned(0)

            def group(e, g):
                for l in range(hiddens):
                    for b in range(HB):
                        act.wait_ge(hid_done, g * HPG + (l * HB + b + 1))
                        nc.scalar.activation(hT[l][:, b, :], ps_h[:, (l * HB + b) % 2, :], m.act,
                                             bias=B[l][:, e, b:b + 1]).then_inc(act_done, 1)
                    if l == 0:
                        turned(g + 1)
            groups(act, group)


def phase_combine(nc, mem, m, out=None):
    TC = 7
    STEPS = NT // TC
    with ExitStack() as ctx:
        sb = lambda n, s, d=fp32: ctx.enter_context(nc.sbuf_tensor(f"{m.name}c_{n}", s, d))
        sem = lambda n: new_semaphore(nc, mem, ctx, f"{m.name}c_{n}")
        idx = sb("idx", [P, 2, 2 * TC], i32)
        rows = sb("rows", [P, 2, 2 * TC, D])
        idx_ready, added, taken, stored = sem("idx_ready"), sem("added"), sem("taken"), sem("stored")
        landed = [gather_semaphore(nc, mem, m.name + "c_landed" + str(s)) for s in range(2)]
        pos = m.pos[:, :, :].rearrange("p t w -> p (t w)")
        w12 = m.w12[:, :, :].rearrange("p t w -> p (t w)")
        block = ctx.enter_context(nc.Block())

        def steps(eng, do):
            with eng.Fori(0, STEPS // 2) as i:
                do(2 * i, 0, i)
                do(2 * i + 1, 1, i)
            do(STEPS - 1, 0, STEPS // 2)

        @block.gpsimd
        def _(pool):
            def gather(n, s, i):
                pool.wait_ge(idx_ready, n + 1)
                pool.sem_inc(mem.tick, 1)
                for j in range(2 * TC):
                    pool.indirect_dma_start(rows[:, s, j, :], None, mem.y_table[:, :],
                                            bass.IndirectOffsetOnAxis(ap=idx[:, s, j:j + 1].bitcast(u32), axis=0))\
                        .then_inc(landed[s], 16)
            steps(pool, gather)

        @block.scalar
        def _(act):
            act.sem_inc(taken, 2)

            def stage(n, s, i):
                act.wait_ge(taken, n + 1)
                nc.scalar.copy(idx[:, s, :], cols(pos, n * (2 * TC), 2 * TC)).then_inc(idx_ready, 1)
            steps(act, stage)

        @block.vector
        def _(dve):
            def step(n, s, i):
                dve.wait_ge(landed[s], 16 * 2 * TC * (i + 1))
                for w in range(2):
                    for j in range(TC):
                        t = n * TC + j
                        ins = nc.vector.scalar_tensor_tensor(tile_at(mem.X, t), rows[:, s, 2 * j + w, :], cols(w12, t * 2 + w, 1),
                                                             tile_at(mem.X, t), op0=ALU.mult, op1=ALU.add)
                    if w == 0:
                        ins.then_inc(added, 1)
                        dve.wait_ge(added, n + 1)
                ins.then_inc(taken, 1)
            steps(dve, step)
            dve.wait_ge(taken, STEPS + 2)

        @block.sync
        def _(sp):
            if out is not None:
                def store(n, s, i):
                    sp.wait_ge(taken, n + 3)
                    full = TC if not isinstance(n, int) else TC - 1
                    rows_at = out[n * TC * P:(n * TC + full) * P, :] if isinstance(n, int) else out[bass.ds(n * (TC * P), TC * P), :]
                    x_at = mem.X[:, n * TC:n * TC + full, :] if isinstance(n, int) else mem.X[:, bass.ds(n * TC, TC), :]
                    sp.dma_start(rows_at.rearrange("(t p) f -> p t f", p=P), x_at).then_inc(stored, 16)
                steps(sp, store)
                sp.dma_start(out[FULL_T * P:N, :], mem.X[0:TAIL, FULL_T, :]).then_inc(stored, 16)
                sp.wait_ge(stored, 16 * (STEPS + 1))


def sparse_moe(nc, mem, a, m, src, out=None):
    with ExitStack() as ctx:
        sb = lambda n, s, d=fp32: ctx.enter_context(nc.sbuf_tensor(f"{m.name}_{n}", s, d))
        m.w12, m.pos, m.ids = sb("w12", [P, NT, 2]), sb("pos", [P, NT, 2], i32), sb("ids", [P, NT, 2], i32)
        m.plan = sb("plan", [1, 3, m.experts], i32)
        if m.affine:
            m.gb = sb("gb", [P, 2, KD])
        m.router_loads = 4
        phase_route(nc, mem, a, m, src)
        phase_list(nc, mem, m)
        phase_experts(nc, mem, a, m)
        phase_combine(nc, mem, m, out)


def phase_edge_messages(nc, mem, a, acc):
    with ExitStack() as ctx:
        sb = lambda n, s, d=fp32: ctx.enter_context(nc.sbuf_tensor(f"em_{n}", s, d))
        pb = lambda n, s: ctx.enter_context(nc.psum_tensor(f"em_{n}", s, fp32))
        sem = lambda n: new_semaphore(nc, mem, ctx, f"em_{n}")
        We = sb("We", [P, D])
        idx = sb("idx", [P, 2, CB], i32)
        xrow = sb("xrow", [P, 2, CB, D])
        attr = sb("attr", [P, 2, CB, ED])
        attr_t = sb("attr_t", [P, 2, EB])
        member = [sb(f"member{k}", [P, CB, P]) for k in range(3)]
        msg = sb("msg", [P, 2, CB, D])
        ps_t = pb("pst", [P, 2, HC * P])
        ps_e = [pb(f"pse{s}", [P, HC, D]) for s in range(2)]
        ps_a = pb("psa", [P, 2, 512])
        cleared, w_in, part_in = sem("cleared"), sem("w_in"), sem("part_in")
        idx_ready, tr_done, at_ready, e_done = sem("idx_ready"), sem("tr_done"), sem("at_ready"), sem("e_done")
        add_done, relu_done, first_ready = sem("add_done"), sem("relu_done"), sem("first_ready")
        more_ready, more_read = sem("more_ready"), sem("more_read")
        summed, acc_done = sem("summed"), sem("acc_done")
        landed = [gather_semaphore(nc, mem, "em_landed" + str(s)) for s in range(2)]
        attr_in = [sem(f"attr_in{s}") for s in range(2)]
        block = ctx.enter_context(nc.Block())

        @block.sync
        def _(sp):
            sp.dma_start(We[:, :], a["L1_gnn_W_edge"]).then_inc(w_in, 16)

            def load(b, s, i):
                sp.wait_ge(tr_done, 2 * b + 2)
                if isinstance(b, int) and b == NB - 1:
                    full = LAST_E // P
                    at = b * EB
                    sp.dma_start(attr[0:LAST_E % P, s, full, :], a["edge_attr_128"][at + full * P:E, :]).then_inc(part_in, 16)
                    sp.wait_ge(part_in, 16)
                    sp.dma_start(attr[:, s, 0:full, :], a["edge_attr_128"][at:at + full * P, :]
                                 .rearrange("(c p) f -> p c f", p=P)).then_inc(attr_in[s], 16)
                else:
                    rows = a["edge_attr_128"][b * EB:(b + 1) * EB, :] if isinstance(b, int) else \
                        a["edge_attr_128"][bass.ds(b * EB, EB), :]
                    sp.dma_start(attr[:, s, :, :], rows.rearrange("(c p) f -> p c f", p=P)).then_inc(attr_in[s], 16)
            bodies(sp, load)

        @block.gpsimd
        def _(pool):
            pool.memset(acc[:, :, 0:D], 0.0).then_inc(cleared, 1)

            def gather(b, s, i):
                pool.wait_ge(idx_ready, b + 1)
                pool.sem_inc(mem.tick, 1)
                for j in range(CB):
                    pool.indirect_dma_start(xrow[:, s, j, :], None, mem.xn_table[:, :],
                                            bass.IndirectOffsetOnAxis(ap=idx[:, s, j:j + 1].bitcast(u32), axis=0))\
                        .then_inc(landed[s], 16)
            bodies(pool, gather)

        @block.vector
        def _(dve):
            dve.sem_inc(add_done, 4)

            dve.sem_inc(more_read, 1)

            def mark(dst, b, t):
                for j in range(CB):
                    ins = nc.vector.tensor_scalar(dst[:, j, :], mem.iota_row[:, :], cols(mem.dst_e, b * CB + j, 1),
                                                  col(mem.neg_base, t), ALU.subtract, ALU.is_equal)
                return ins

            def mark_first(b, s):
                first, _, _ = pairs_loop(dve, mem, b)
                dve.wait_ge(e_done, 2 * b + 5)
                mark(member[s], b, first).then_inc(first_ready, 1)

            def body(b, s, i):
                mark_first(b, s)
                dve.wait_ge(landed[s], 16 * CB * (i + 1))
                for h in range(2):
                    half = slice(h * HC, (h + 1) * HC)
                    dve.wait_ge(e_done, 2 * b + (h + 5))
                    nc.vector.tensor_tensor(msg[:, s, half, :], ps_e[h][:, :, :], xrow[:, s, half, :], ALU.add)\
                        .then_inc(add_done, 1)
                first, count, before, further = body_pairs(dve, mem, b)
                with dve.If(count > 1):
                    with dve.Fori(1, count) as r:
                        dve.wait_ge(more_read, further + r)
                        mark(member[2], b, tile_of(first, r)).then_inc(more_ready, 1)
            bodies(dve, body)

        @block.tensor
        def _(pe):
            pe.sem_inc(tr_done, 4)
            pe.sem_inc(e_done, 4)
            pe.wait_ge(w_in, 16)
            pe.wait_ge(cleared, 1)

            def turn(b, s, i):
                pe.wait_ge(attr_in[s], 16 * (i + 1))
                for h in range(2):
                    pe.wait_ge(at_ready, 2 * b + (h + 1))
                    for j in range(HC):
                        ins = nc.tensor.transpose(ps_t[:, h, j * P:(j + 1) * P], attr[:, s, h * HC + j, :], mem.ident[:, :])
                    ins.then_inc(tr_done, 1)

            def edge_linear(b, s):
                for h in range(2):
                    pe.wait_ge(at_ready, 2 * b + (h + 3))
                    pe.wait_ge(add_done, 2 * b + (h + 3))
                    for j in range(HC):
                        c = h * HC + j
                        ins = nc.tensor.matmul(ps_e[h][:, j, :], attr_t[:, s, c * P:(c + 1) * P], We[:, :], start=True, stop=True)
                    ins.then_inc(e_done, 1)

            def products(which, s, b):
                bank = 0 if which < 2 else 1
                for j in range(CB):
                    if j % HC == 0:
                        pe.wait_ge(relu_done, 2 * b + (j // HC + 1))
                    ins = nc.tensor.matmul(ps_a[:, bank, 0:D], member[s if which < 2 else 2][:, j, :], msg[:, s, j, :],
                                           start=(j == 0), stop=False)
                return ins

            def add_so_far(bank, t):
                nc.tensor.matmul(ps_a[:, bank, 0:D], mem.ident[:, :], tile_at(acc, t, D), start=False, stop=True).then_inc(summed, 1)

            turn(0, 0, 0)
            turn(1, 1, 0)
            edge_linear(0, 0)

            def body(b, s, i):
                if last_plus(2, b):
                    turn(b + 2, s, i + 1)
                if last_plus(1, b):
                    edge_linear(b + 1, 1 - s)
                first, count, before, further = body_pairs(pe, mem, b)
                pe.wait_ge(acc_done, before + 1)
                pe.wait_ge(first_ready, b + 1)
                products(0, s, b)
                add_so_far(0, first)
                with pe.If(count > 1):
                    with pe.Fori(1, count) as r:
                        pe.wait_ge(more_ready, further + r)
                        pe.wait_ge(acc_done, before + r)
                        products(2, s, b).then_inc(more_read, 1)
                        pe.wait_ge(acc_done, before + r + 1)
                        add_so_far(1, tile_of(first, r))
            bodies(pe, body)

        @block.scalar
        def _(act):
            act.sem_inc(acc_done, 1)
            act.sem_inc(at_ready, 2)

            def take_index(b, s):
                act.wait_ge(add_done, 2 * b + 2)
                nc.scalar.copy(idx[:, s, :], cols(mem.src_idx, b * CB, CB)).then_inc(idx_ready, 1)

            def take_attr(b, s):
                for h in range(2):
                    act.wait_ge(tr_done, 2 * b + (h + 5))
                    act.wait_ge(e_done, 2 * b + (h + 1))
                    nc.scalar.activation(attr_t[:, s, h * HC * P:(h + 1) * HC * P], ps_t[:, h, :], ACT.Copy)\
                        .then_inc(at_ready, 1)
            def copy_out(bank, q, t):
                act.wait_ge(summed, q + 1)
                nc.scalar.activation(tile_at(acc, t, D), ps_a[:, bank, 0:D], ACT.Copy).then_inc(acc_done, 1)

            take_index(0, 0)
            take_index(1, 1)
            take_attr(0, 0)
            take_attr(1, 1)
            act.wait_ge(cleared, 1)

            def body(b, s, i):
                for h in range(2):
                    half = slice(h * HC, (h + 1) * HC)
                    act.wait_ge(add_done, 2 * b + (h + 5))
                    nc.scalar.activation(msg[:, s, half, :], msg[:, s, half, :], ACT.Relu).then_inc(relu_done, 1)
                if last_plus(2, b):
                    take_index(b + 2, s)
                    take_attr(b + 2, s)
                first, count, before = pairs_loop(act, mem, b)
                copy_out(0, before, first)
                with act.If(count > 1):
                    with act.Fori(1, count) as r:
                        copy_out(1, before + r, tile_of(first, r))
            bodies(act, body)


def phase_node_mlp(nc, mem, a, acc):
    LN_ = (N - NG * GN)
    with ExitStack() as ctx:
        sb = lambda n, s, d=fp32: ctx.enter_context(nc.sbuf_tensor(f"ml_{n}", s, d))
        pb = lambda n, s: ctx.enter_context(nc.psum_tensor(f"ml_{n}", s, fp32))
        sem = lambda n: new_semaphore(nc, mem, ctx, f"ml_{n}")
        W1, W2 = sb("W1", [P, KD, D]), sb("W2", [P, KD, D])
        vecs = sb("vecs", [P, 4, KD])
        eps1 = sb("eps1", [P, 1])
        xn = sb("xn", [P, 2, D])
        hs = sb("hs", [P, GT, D])
        hT = sb("hT", [P, KD, GN])
        h1 = sb("h1", [P, KD, GN])
        H = sb("H", [P, KD, NT * P])
        stats = sb("stats", [P, KD, NG + 1, 6])
        mv = sb("mv", [P, KD, 2])
        scale, shift, std = sb("scale", [P, KD]), sb("shift", [P, KD]), sb("std", [P, KD])
        yT = sb("yT", [P, 2, KD, GN])
        ps_t = pb("pst", [P, KD, GN])
        ps_h = pb("psh", [P, KD, GN])
        ps_y = pb("psy", [P, 2, 2, 512])
        w_in, xn_done, hs_ready, tr_done = sem("w_in"), sem("xn_done"), sem("hs_ready"), sem("tr_done")
        ht_ready, m_done, h1_ready, h2_ready = sem("ht_ready"), sem("m_done"), sem("h1_ready"), sem("h2_ready")
        seen, step, rooted, scaled = sem("seen"), sem("step"), sem("rooted"), sem("scaled")
        y_ready, y_turned, y_added = sem("y_ready"), sem("y_turned"), sem("y_added")
        block = ctx.enter_context(nc.Block())
        names = ("L1_gnn_b1", "L1_gnn_b2", "L1_gnn_gamma", "L1_gnn_beta")

        @block.sync
        def _(sp):
            sp.dma_start(W1[:, :, :], a["L1_gnn_W1"].rearrange("(k p) n -> p k n", p=P)).then_inc(w_in, 16)
            sp.dma_start(W2[:, :, :], a["L1_gnn_W2"].rearrange("(k p) n -> p k n", p=P)).then_inc(w_in, 16)
            sp.dma_start(eps1[:, :], a["L1_gnn_eps"].partition_broadcast(P)).then_inc(w_in, 16)
            for n, name in enumerate(names):
                sp.dma_start(vecs[:, n, :], a[name].rearrange("(k p) -> p k", p=P), allow_slow_non_contiguous=True).then_inc(w_in, 16)

        @block.vector
        def _(dve):
            dve.sem_inc(hs_ready, 1)
            dve.wait_ge(w_in, 16 * 7)
            nc.vector.tensor_scalar(eps1[:, :], eps1[:, :], 1.0, None, ALU.add).then_inc(step, 1)
            dve.wait_ge(step, 1)

            def group(g, nt):
                dve.wait_ge(tr_done, g + 1)
                for j in range(nt):
                    t = g * GT + j
                    s = j % 2
                    nc.vector.tensor_scalar(xn[:, s, :], tile_at(mem.X, t), col(mem.mean, t), col(mem.rstd, t),
                                            ALU.subtract, ALU.mult).then_inc(xn_done, 1)
                    dve.wait_ge(xn_done, t + 1)
                    nc.vector.scalar_tensor_tensor(hs[:, j, :], xn[:, s, :], eps1[:, 0:1], tile_at(acc, t, D),
                                                   op0=ALU.mult, op1=ALU.add).then_inc(hs_ready, 1)

            def groups_(do):
                with dve.Fori(0, NG) as g:
                    do(g, GT)
                do(NG, NT - NG * GT)
            groups_(group)
            dve.wait_ge(h2_ready, NG + 1)
            for g in range(NG + 1):
                w = GN if g < NG else LN_
                for k in range(KD):
                    nc.vector.bn_stats(stats[:, k, g, :], H[:, k, g * GN:g * GN + w]).then_inc(seen, 1)
            dve.wait_ge(seen, KD * (NG + 1))
            for k in range(KD):
                nc.vector.bn_aggr(mv[:, k, :], stats[:, k, :, :].rearrange("p g s -> p (g s)")).then_inc(step, 1)
            dve.wait_ge(step, 3)
            nc.vector.tensor_scalar(shift[:, :], mv[:, :, 1], EPS, None, ALU.add).then_inc(step, 1)
            dve.wait_ge(rooted, 1)
            nc.vector.reciprocal(scale[:, :], std[:, :]).then_inc(step, 1)
            dve.wait_ge(step, 5)
            nc.vector.tensor_tensor(scale[:, :], scale[:, :], vecs[:, 2, :], ALU.mult).then_inc(step, 1)
            dve.wait_ge(step, 6)
            nc.vector.tensor_tensor(shift[:, :], mv[:, :, 0], scale[:, :], ALU.mult).then_inc(step, 1)
            dve.wait_ge(step, 7)
            nc.vector.tensor_tensor(shift[:, :], vecs[:, 3, :], shift[:, :], ALU.subtract).then_inc(scaled, 1)
            for g in range(NG + 1):
                nt = GT if g < NG else NT - NG * GT
                dve.wait_ge(y_turned, g + 1)
                x4 = mem.X[:, g * GT:g * GT + nt, :].rearrange("p t f -> p (t f)")
                y4 = ps_y[:, g % 2, :, :].rearrange("p b f -> p (b f)")[:, 0:nt * D]
                nc.vector.tensor_tensor(x4, x4, y4, ALU.add).then_inc(y_added, 1)
            dve.wait_ge(y_added, NG + 1)

        @block.tensor
        def _(pe):
            pe.sem_inc(tr_done, 1)
            pe.wait_ge(w_in, 16 * 7)

            def group(g, nt):
                w = nt * P
                pe.wait_ge(hs_ready, g * GT + nt + 1)
                for k in range(KD):
                    for j in range(nt):
                        ins = nc.tensor.transpose(ps_t[:, k, j * P:(j + 1) * P], hs[:, j, k * P:(k + 1) * P], mem.ident[:, :])
                ins.then_inc(tr_done, 1)
                for n, (W, x, ready) in enumerate(((W1, hT, ht_ready), (W2, h1, h1_ready))):
                    pe.wait_ge(ready, g + 1)
                    for b in range(KD):
                        for k in range(KD):
                            ins = nc.tensor.matmul(ps_h[:, b, 0:w], W[:, k, b * P:(b + 1) * P], x[:, k, 0:w],
                                                   start=(k == 0), stop=(k == KD - 1))
                    ins.then_inc(m_done, 1)
            with pe.Fori(0, NG) as g:
                group(g, GT)
            pe_last = group(NG, NT - NG * GT)
            for g in range(NG + 1):
                nt = GT if g < NG else NT - NG * GT
                pe.wait_ge(y_ready, g + 1)
                if g >= 2:
                    pe.wait_ge(y_added, g - 1)
                for j in range(nt):
                    for k in range(KD):
                        ins = nc.tensor.transpose(ps_y[:, g % 2, j // 2, (j % 2) * D + k * P:(j % 2) * D + (k + 1) * P],
                                                  yT[:, g % 2, k, j * P:(j + 1) * P], mem.ident[:, :])
                ins.then_inc(y_turned, 1)

        @block.scalar
        def _(act):
            act.wait_ge(w_in, 16 * 7)

            def group(g, nt):
                w = nt * P
                act.wait_ge(tr_done, g + 2)
                nc.scalar.activation(hT[:, :, 0:w], ps_t[:, :, 0:w], ACT.Copy).then_inc(ht_ready, 1)
                act.wait_ge(m_done, 2 * g + 1)
                for k in range(KD):
                    ins = nc.scalar.activation(h1[:, k, 0:w], ps_h[:, k, 0:w], ACT.Relu, bias=vecs[:, 0, k:k + 1])
                ins.then_inc(h1_ready, 1)
                act.wait_ge(m_done, 2 * g + 2)
                for k in range(KD):
                    o = H[:, k, g * GN:g * GN + w] if isinstance(g, int) else H[:, k, bass.ds(g * GN, w)]
                    ins = nc.scalar.activation(o, ps_h[:, k, 0:w], ACT.Identity, bias=vecs[:, 1, k:k + 1])
                ins.then_inc(h2_ready, 1)
            with act.Fori(0, NG) as g:
                group(g, GT)
            group(NG, NT - NG * GT)
            act.wait_ge(step, 4)
            nc.scalar.activation(std[:, :], shift[:, :], ACT.Sqrt).then_inc(rooted, 1)
            act.wait_ge(scaled, 1)
            for g in range(NG + 1):
                w = GN if g < NG else (NT - NG * GT) * P
                if g >= 2:
                    act.wait_ge(y_turned, g - 1)
                for k in range(KD):
                    ins = nc.scalar.activation(yT[:, g % 2, k, 0:w], H[:, k, g * GN:g * GN + w], ACT.Relu,
                                               bias=shift[:, k:k + 1], scale=scale[:, k:k + 1])
                ins.then_inc(y_ready, 1)


def build(nc, a, out):
    mem = Mem()
    mem.NBP = CQ * BQ
    top = ExitStack()
    with top:
        sb = lambda n, s, d=fp32: top.enter_context(nc.sbuf_tensor(n, s, d))
        mem.order, mem.y_table = nc.dram_tensor("order", [GROUPS * GN, 1], i32, kind="Internal").ap(), \
            nc.dram_tensor("y_table", [GROUPS * GN, D], fp32, kind="Internal").ap()
        mem.tick = top.enter_context(nc.semaphore("tick"))
        mem.rooted = top.enter_context(nc.semaphore("rooted"))
        mem.roots = 0
        mem.used, mem.top = [], top
        dr = lambda n, s, d=fp32: nc.dram_tensor(n, s, d, kind="Internal").ap()
        mem.dst_flat, mem.reset_flat = dr("dst_flat", [NCH * P]), dr("reset_flat", [NCH * P + 1])
        mem.range_flat = dr("range_flat", [2, mem.NBP], i32)
        mem.h_table, mem.as_table, mem.xn_table = dr("h_table", [NT * P, D]), dr("as_table", [NT * P, HEADS]), dr("xn_table", [NT * P, D])
        mem.ident = sb("ident", [P, P])
        mem.flip = sb("flip", [P, P])
        mem.iota_row = sb("iota_row", [P, P])
        mem.node_id = sb("node_id", [P, NT])
        mem.neg_base = sb("neg_base", [P, NT])
        mem.ones = sb("ones", [P, P])
        mem.zeros = sb("zeros", [P, P])
        mem.src_idx = sb("src_idx", [P, NCH], i32)
        mem.dst_e = sb("dst_e", [P, NCH])
        mem.general_steps = sb("general_steps", [1, 1], i32)
        mem.ranges = sb("ranges", [1, mem.NBP], i32)
        mem.mean, mem.rstd = sb("mean", [P, NT]), sb("rstd", [P, NT])
        mem.X = sb("X", [P, NT, D])
        acc = sb("acc", [P, NT, MSG])
        with ExitStack() as inner:
            AR = inner.enter_context(nc.sbuf_tensor("AR", [P, NCH, 2, HEADS], fp32))
            early = inner.enter_context(ExitStack())
            mem.reset_e = early.enter_context(nc.sbuf_tensor("reset_e", [P, NCH], fp32))
            mem.a_node = early.enter_context(nc.sbuf_tensor("a_node", [P, NT, 2 * HEADS], fp32))
            phase_load(nc, mem, a)
            phase_edges(nc, mem, a)
            layernorm_stats(nc, mem, "ln0", mem.X)
            phase_project(nc, mem, a)
            S = acc_as(acc, NCH * HEADS).rearrange("p (g e) -> p g e", e=P)
            mem.scratch = acc[:, :, :].rearrange("p t f -> p (t f)")[:, NCH * HEADS:2 * NCH * HEADS]
            phase_scores(nc, mem, AR)
            phase_run_max(nc, mem, AR, S)
            phase_weights(nc, mem, AR)
            early.close()
            phase_attention(nc, mem, AR, acc)
        clear_semaphores(nc, mem)
        phase_attention_out(nc, mem, a, acc)
        layernorm_stats(nc, mem, "ln1", mem.X)
        phase_normalize(nc, mem, "no1", mem.X, acc)
        layernorm_stats(nc, mem, "ln2", acc)
        m = Moe()
        m.name, m.experts, m.hidden, m.act = "m0", 8, 512, ACT.Gelu
        m.weights, m.biases = ("L0_ffn_W1", "L0_ffn_W2"), ("L0_ffn_b1", "L0_ffn_b2")
        m.affine, m.router, m.router_bias, m.router_hidden, m.router_blocks = \
            ("L0_ffn_gamma", "L0_ffn_beta"), "L0_ffn_Wr", "L0_ffn_br", False, KD
        m.room = acc[:, :, :].rearrange("p t f -> p (t f)")
        sparse_moe(nc, mem, a, m, acc)
        clear_semaphores(nc, mem)
        layernorm_stats(nc, mem, "ln3", mem.X)
        phase_normalize(nc, mem, "no3", mem.X, acc, a["L1_gnn_b_edge"], mem.xn_table)
        phase_edge_messages(nc, mem, a, acc)
        phase_node_mlp(nc, mem, a, acc)
        layernorm_stats(nc, mem, "ln4", mem.X)
        m = Moe()
        m.name, m.experts, m.hidden, m.act = "m1", 6, 256, ACT.Relu
        m.weights = ("L1_ffn_expert_w1", "L1_ffn_expert_w2", "L1_ffn_expert_w3")
        m.biases = ("L1_ffn_expert_b1", "L1_ffn_expert_b2", "L1_ffn_expert_b3")
        m.affine, m.router, m.router_bias, m.router_hidden, m.router_blocks = \
            None, "L1_ffn_router_w2", "L1_ffn_router_b2", True, 1
        m.room = acc[:, :, :].rearrange("p t f -> p (t f)")
        clear_semaphores(nc, mem)
        sparse_moe(nc, mem, a, m, mem.X, out)


_OUTS = [((N, D), "float32")]


def kernel(**inputs):
    import numpy as _np
    import concourse.bacc as _bacc
    from concourse import mybir as _mybir
    from concourse.bass_utils import run_bass_kernel_spmd as _run

    nc = _bacc.Bacc("TRN2", target_bir_lowering=False, num_devices=1)
    arrays, args = {}, {}
    for name, value in inputs.items():
        a = _np.ascontiguousarray(value)
        if a.ndim == 0:
            a = a.reshape(1)
        arrays[f"in_{name}_dram"] = a
        args[name] = nc.dram_tensor(f"in_{name}_dram", a.shape, _mybir.dt.from_np(a.dtype), kind="ExternalInput").ap()
    outs = [nc.dram_tensor(f"out_{i}_dram", shape, _mybir.dt.from_np(_np.dtype(dtype)), kind="ExternalOutput").ap()
            for i, (shape, dtype) in enumerate(_OUTS)]
    build(nc, args, outs[0])
    r = _run(nc, [arrays], core_ids=[0])
    return r.results[0]["out_0_dram"]
```
